# Optimizing a Trainium2 kernel written in Bass

```python
import numpy as np
import jax
import jax.numpy as jnp

def _softmax(x, axis=-1):
    return jax.nn.softmax(x, axis=axis)

def _gelu(x):
    return jax.nn.gelu(x, approximate=True)

def _silu(x):
    return jax.nn.silu(x)

def _sigmoid(x):
    return jax.nn.sigmoid(x)

def _layernorm(x, axis=-1, eps=1e-05):
    m = jnp.mean(x, axis=axis, keepdims=True)
    v = jnp.var(x, axis=axis, keepdims=True)
    return (x - m) / jnp.sqrt(v + eps)

def _scatter_add(tgt, idx, src, axis=0):
    return tgt.at[idx].add(src)

def _segment_sum(src, seg, n):
    return jax.ops.segment_sum(src, seg, n)
kernel_name = 'mk_xattn_ffn_d2_seqx_r4_b1f57e'

def setup_inputs(seed: int=0):
    np.random.seed(seed)
    _w = jnp.asarray

    def _rec_inputs():
        import jax
        import jax.numpy as jnp
        _rk = jax.random.key(seed)
        x = -0.0002928 + 1 * jax.random.normal(jax.random.fold_in(_rk, 1), (16, 128, 256), jnp.float32)
        _lenS = 128 - jax.random.randint(jax.random.fold_in(_rk, 7), (16,), 0, max(1, 128 // 4) + 1, jnp.int32)
        _lenS2 = 128 - jax.random.randint(jax.random.fold_in(_rk, 8), (16,), 0, max(1, 128 // 4) + 1, jnp.int32)
        _ctx_1024P = jax.random.normal(jax.random.fold_in(_rk, 11), (16, 16, 256), jnp.float32)
        _ctx_1024c = jax.random.dirichlet(jax.random.fold_in(_rk, 511), 0.3 * jnp.ones((16,), jnp.float32), (16, 128))
        _ctx_1024t = jnp.einsum('bsk,bkd->bsd', _ctx_1024c, _ctx_1024P)
        _ctx_1024t = _ctx_1024t * jax.lax.rsqrt(jnp.mean(jnp.square(_ctx_1024t)) + 1e-12) * 0.953939
        ctx_1024 = -1.39393e-06 + 0.999914 * (_ctx_1024t + 0.3 * jax.random.normal(jax.random.fold_in(_rk, 611), (16, 128, 256), jnp.float32))
        return (x, ctx_1024)
    x, ctx_1024 = _rec_inputs()

    def _L0_xattn_setup():
        import jax, jax.numpy as jnp
        import numpy as np
        HEADS = 16
        key = jax.random.key(seed)
        ks = jax.random.split(key, 5)
        B, N, D = (2, 512, 256)
        q = jax.random.normal(ks[0], (B, N, D), dtype=jnp.float32)
        kv = jax.random.normal(ks[1], (B, N, D), dtype=jnp.float32)
        s = 1.0 / np.sqrt(D)
        Wq = jax.random.normal(ks[2], (D, D), dtype=jnp.float32) * s
        Wkv = jax.random.normal(ks[3], (D, 2 * D), dtype=jnp.float32) * s
        Wout = jax.random.normal(ks[4], (D, D), dtype=jnp.float32) * s
        return {'q': q, 'kv': kv, 'Wq': Wq, 'Wkv': Wkv, 'Wout': Wout}
    _L0_xattn_all = _L0_xattn_setup()
    _L0_xattn_in = {k: v for k, v in _L0_xattn_all.items() if k in ('Wq', 'Wkv', 'Wout')}
    del _L0_xattn_all

    def _L0_ffn_setup():
        import jax, jax.numpy as jnp
        import numpy as np
        QMAX = 127.0

        def _ste_round(v):
            return v + jax.lax.stop_gradient(jnp.round(v) - v)

        def _act_fake_quant(x, clip_factor):
            scale = jax.nn.sigmoid(clip_factor) * jnp.max(jnp.abs(x)) / QMAX
            return jnp.clip(_ste_round(x / scale), -QMAX - 1.0, QMAX) * scale

        def _weight_fake_quant(w):
            scale = jnp.max(jnp.abs(w), axis=1, keepdims=True) / QMAX
            return jnp.clip(_ste_round(w / scale), -QMAX - 1.0, QMAX) * scale
        key = jax.random.key(seed)
        k1, k2, k3, k4 = jax.random.split(key, 4)
        B, S, H, I = (8, 2048, 256, 704)
        return {'x': jax.random.normal(k1, (B, S, H), dtype=jnp.float32), 'clip_x': jnp.full((1,), 4.0, dtype=jnp.float32), 'clip_down': jnp.full((1,), 4.0, dtype=jnp.float32), 'w_gate': jax.random.normal(k2, (I, H), dtype=jnp.float32) * 0.02, 'w_up': jax.random.normal(k3, (I, H), dtype=jnp.float32) * 0.02, 'w_down': jax.random.normal(k4, (H, I), dtype=jnp.float32) * 0.02}
    _L0_ffn_all = _L0_ffn_setup()
    _L0_ffn_in = {k: v for k, v in _L0_ffn_all.items() if k in ('clip_x', 'clip_down', 'w_gate', 'w_up', 'w_down')}
    del _L0_ffn_all

    def _L1_xattn_setup():
        import jax, jax.numpy as jnp
        import numpy as np
        B, S, E, NH = (2, 512, 256, 4)
        HD = E // NH

        def _mlstm_head(q, k, v, ig, fg, eps=1e-06):
            s, dh = q.shape
            log_f = jax.nn.log_sigmoid(fg)
            cs = jnp.concatenate([jnp.zeros((1, 1), log_f.dtype), jnp.cumsum(log_f, axis=0)], axis=0)
            neg = jnp.asarray(-0.7 * jnp.finfo(cs.dtype).max, cs.dtype)
            log_d = jnp.where(jnp.tri(s, dtype=bool), (cs - cs.T)[1:, 1:] + ig.T, neg)
            m = jnp.max(log_d, axis=-1, keepdims=True)
            d = jnp.exp(log_d - m)
            c = q @ (k.T / jnp.sqrt(dh)) * d
            n = jnp.maximum(jnp.sum(c, axis=-1, keepdims=True), jnp.exp(-m))
            return c / (n + eps) @ v
        key = jax.random.key(seed)
        ks = jax.random.split(key, 8)
        return {'q': jax.random.normal(ks[0], (B, S, E), jnp.float32), 'k': jax.random.normal(ks[1], (B, S, E), jnp.float32), 'v': jax.random.normal(ks[2], (B, S, E), jnp.float32), 'igate_kernel': jax.random.normal(ks[3], (3 * E, NH), jnp.float32) * 0.02, 'igate_bias': jax.random.normal(ks[4], (NH,), jnp.float32) * 0.1, 'fgate_kernel': jax.random.normal(ks[5], (3 * E, NH), jnp.float32) * 0.02, 'fgate_bias': jnp.linspace(3.0, 6.0, NH, dtype=jnp.float32), 'rms_scale': jax.random.normal(ks[6], (HD,), jnp.float32) * 0.02}
    _L1_xattn_all = _L1_xattn_setup()
    _L1_xattn_in = {k: v for k, v in _L1_xattn_all.items() if k in ('igate_kernel', 'igate_bias', 'fgate_kernel', 'fgate_bias', 'rms_scale')}
    del _L1_xattn_all

    def _L1_ffn_setup():
        import jax, jax.numpy as jnp
        import numpy as np
        TOP_K = 2
        key = jax.random.key(seed)
        ks = jax.random.split(key, 5)
        B, T, D, F, E = (4, 512, 256, 1024, 8)
        s = 0.02
        return {'x': jax.random.normal(ks[0], (B, T, D), jnp.float32), 'gate_w': jax.random.normal(ks[1], (D, E), jnp.float32) * s, 'w1': jax.random.normal(ks[2], (E, D, F), jnp.float32) * s, 'w3': jax.random.normal(ks[3], (E, D, F), jnp.float32) * s, 'w2': jax.random.normal(ks[4], (E, F, D), jnp.float32) * s}
    _L1_ffn_all = _L1_ffn_setup()
    _L1_ffn_in = {k: v for k, v in _L1_ffn_all.items() if k in ('gate_w', 'w1', 'w3', 'w2')}
    del _L1_ffn_all
    return {'x': x, 'ctx_1024': ctx_1024, 'L0_xattn_Wq': _L0_xattn_in['Wq'], 'L0_xattn_Wkv': _L0_xattn_in['Wkv'], 'L0_xattn_Wout': _L0_xattn_in['Wout'], 'L0_ffn_clip_x': _L0_ffn_in['clip_x'], 'L0_ffn_clip_down': _L0_ffn_in['clip_down'], 'L0_ffn_w_gate': _L0_ffn_in['w_gate'], 'L0_ffn_w_up': _L0_ffn_in['w_up'], 'L0_ffn_w_down': _L0_ffn_in['w_down'], 'L1_xattn_igate_kernel': _L1_xattn_in['igate_kernel'], 'L1_xattn_igate_bias': _L1_xattn_in['igate_bias'], 'L1_xattn_fgate_kernel': _L1_xattn_in['fgate_kernel'], 'L1_xattn_fgate_bias': _L1_xattn_in['fgate_bias'], 'L1_xattn_rms_scale': _L1_xattn_in['rms_scale'], 'L1_ffn_gate_w': _L1_ffn_in['gate_w'], 'L1_ffn_w1': _L1_ffn_in['w1'], 'L1_ffn_w3': _L1_ffn_in['w3'], 'L1_ffn_w2': _L1_ffn_in['w2']}

def reference(x, ctx_1024, L0_xattn_Wq, L0_xattn_Wkv, L0_xattn_Wout, L0_ffn_clip_x, L0_ffn_clip_down, L0_ffn_w_gate, L0_ffn_w_up, L0_ffn_w_down, L1_xattn_igate_kernel, L1_xattn_igate_bias, L1_xattn_fgate_kernel, L1_xattn_fgate_bias, L1_xattn_rms_scale, L1_ffn_gate_w, L1_ffn_w1, L1_ffn_w3, L1_ffn_w2):
    import jax
    import jax.numpy as jnp

    def _L0_xattn_ref(q, kv, Wq, Wkv, Wout):
        import jax, jax.numpy as jnp
        import numpy as np
        HEADS = 16
        B, N, D = q.shape
        H = HEADS
        Dh = D // H
        scale = Dh ** (-0.5)
        qp = q @ Wq
        kvp = kv @ Wkv
        kp, vp = (kvp[..., :D], kvp[..., D:])

        def split_heads(t):
            return t.reshape(B, N, H, Dh).transpose(0, 2, 1, 3)
        qh, kh, vh = (split_heads(qp), split_heads(kp), split_heads(vp))
        dots = jnp.einsum('bhid,bhjd->bhij', qh, kh) * scale
        attn = jax.nn.softmax(dots.astype(jnp.float32), axis=-1).astype(dots.dtype)
        out = jnp.einsum('bhij,bhjd->bhid', attn, vh)
        out = out.transpose(0, 2, 1, 3).reshape(B, N, D)
        return out @ Wout

    def _L0_ffn_ref(x, clip_x, clip_down, w_gate, w_up, w_down):
        import jax, jax.numpy as jnp
        import numpy as np
        QMAX = 127.0

        def _ste_round(v):
            return v + jax.lax.stop_gradient(jnp.round(v) - v)

        def _act_fake_quant(x, clip_factor):
            scale = jax.nn.sigmoid(clip_factor) * jnp.max(jnp.abs(x)) / QMAX
            return jnp.clip(_ste_round(x / scale), -QMAX - 1.0, QMAX) * scale

        def _weight_fake_quant(w):
            scale = jnp.max(jnp.abs(w), axis=1, keepdims=True) / QMAX
            return jnp.clip(_ste_round(w / scale), -QMAX - 1.0, QMAX) * scale
        xq = _act_fake_quant(x, clip_x[0])
        gate = jnp.einsum('bsh,ih->bsi', xq, _weight_fake_quant(w_gate))
        up = jnp.einsum('bsh,ih->bsi', xq, _weight_fake_quant(w_up))
        h = _act_fake_quant(jax.nn.silu(gate) * up, clip_down[0])
        return jnp.einsum('bsi,hi->bsh', h, _weight_fake_quant(w_down))

    def _L1_xattn_ref(q, k, v, igate_kernel, igate_bias, fgate_kernel, fgate_bias, rms_scale):
        import jax, jax.numpy as jnp
        import numpy as np
        B, S, E, NH = (2, 512, 256, 4)
        HD = E // NH

        def _mlstm_head(q, k, v, ig, fg, eps=1e-06):
            s, dh = q.shape
            log_f = jax.nn.log_sigmoid(fg)
            cs = jnp.concatenate([jnp.zeros((1, 1), log_f.dtype), jnp.cumsum(log_f, axis=0)], axis=0)
            neg = jnp.asarray(-0.7 * jnp.finfo(cs.dtype).max, cs.dtype)
            log_d = jnp.where(jnp.tri(s, dtype=bool), (cs - cs.T)[1:, 1:] + ig.T, neg)
            m = jnp.max(log_d, axis=-1, keepdims=True)
            d = jnp.exp(log_d - m)
            c = q @ (k.T / jnp.sqrt(dh)) * d
            n = jnp.maximum(jnp.sum(c, axis=-1, keepdims=True), jnp.exp(-m))
            return c / (n + eps) @ v
        b, s, e = q.shape
        nh = igate_kernel.shape[1]
        hd = e // nh
        gate_in = jnp.concatenate((q, k, v), axis=-1)
        ig = (gate_in @ igate_kernel + igate_bias).swapaxes(-1, -2)[..., None]
        fg = (gate_in @ fgate_kernel + fgate_bias).swapaxes(-1, -2)[..., None]
        qh = q.reshape(b, s, nh, hd).swapaxes(1, 2)
        kh = k.reshape(b, s, nh, hd).swapaxes(1, 2)
        vh = v.reshape(b, s, nh, hd).swapaxes(1, 2)
        h = jax.vmap(jax.vmap(_mlstm_head))(qh, kh, vh, ig, fg)
        var = jnp.mean(jnp.square(h.astype(jnp.float32)), axis=-1, keepdims=True)
        h = (h * jax.lax.rsqrt(var + 1e-06)).astype(h.dtype) * (1.0 + rms_scale)
        return h.swapaxes(1, 2).reshape(b, s, e)

    def _L1_ffn_ref(x, gate_w, w1, w3, w2):
        import jax, jax.numpy as jnp
        import numpy as np
        TOP_K = 2
        logits = jnp.einsum('btd,de->bte', x, gate_w)
        probs = jax.nn.softmax(logits, axis=-1)
        expert_weights, expert_indices = jax.lax.top_k(probs, TOP_K)
        expert_weights = expert_weights / expert_weights.sum(-1, keepdims=True)
        E = w1.shape[0]
        out = jnp.zeros_like(x)
        for i in range(E):
            wi = jnp.where(expert_indices == i, expert_weights, 0.0).sum(-1)
            h = jax.nn.silu(jnp.einsum('btd,df->btf', x, w1[i])) * jnp.einsum('btd,df->btf', x, w3[i])
            out = out + jnp.einsum('btf,fd->btd', h, w2[i]) * wi[..., None]
        return out
    x = x + _L0_xattn_ref(_layernorm(x, axis=-1), ctx_1024, L0_xattn_Wq, L0_xattn_Wkv, L0_xattn_Wout)
    x = x + _L0_ffn_ref(_layernorm(x, axis=-1), L0_ffn_clip_x, L0_ffn_clip_down, L0_ffn_w_gate, L0_ffn_w_up, L0_ffn_w_down)
    x = x + _L1_xattn_ref(_layernorm(x, axis=-1), ctx_1024, ctx_1024, L1_xattn_igate_kernel, L1_xattn_igate_bias, L1_xattn_fgate_kernel, L1_xattn_fgate_bias, L1_xattn_rms_scale)
    x = x + _L1_ffn_ref(_layernorm(x, axis=-1), L1_ffn_gate_w, L1_ffn_w1, L1_ffn_w3, L1_ffn_w2)
    return x

_drawn_inputs = setup_inputs


def setup_inputs(seed=0):
    import zlib

    import numpy as np

    out = dict(_drawn_inputs(seed))
    spreads = {}
    factors = {'L1_xattn_igate_bias': 64.0,
     'L1_xattn_rms_scale': 4.379,
     'L1_ffn_gate_w': 4.77,
     'L1_ffn_w1': 4.169,
     'L1_ffn_w3': 4.111,
     'L1_ffn_w2': 4.115}
    for name, (base, spread) in spreads.items():
        noise = np.random.default_rng([zlib.crc32(name.encode()), seed]).standard_normal(out[name].shape)
        drawn = base * np.exp(spread * noise) if base else spread * noise
        out[name] = jnp.asarray(drawn.astype(out[name].dtype))
    for name, factor in factors.items():
        out[name] = (out[name] * factor).astype(out[name].dtype)
    return out
```

```python
from contextlib import ExitStack

import concourse.bass as bass
from concourse import mybir

INPUTS = ['x', 'ctx_1024', 'L0_xattn_Wq', 'L0_xattn_Wkv', 'L0_xattn_Wout', 'L0_ffn_clip_x', 'L0_ffn_clip_down', 'L0_ffn_w_gate', 'L0_ffn_w_up', 'L0_ffn_w_down', 'L1_xattn_igate_kernel', 'L1_xattn_igate_bias', 'L1_xattn_fgate_kernel', 'L1_xattn_fgate_bias', 'L1_xattn_rms_scale', 'L1_ffn_gate_w', 'L1_ffn_w1', 'L1_ffn_w3', 'L1_ffn_w2']


def build(nc, x, ctx_in, wq, wkv, wout, clip_x, clip_down, w_gate, w_up, w_down, ig_k, ig_b, fg_k, fg_b, rms_scale,
          gate_w, w1, w3, w2, out):
    F32 = mybir.dt.float32
    BF16 = mybir.dt.bfloat16
    I32 = mybir.dt.int32
    U32 = mybir.dt.uint32
    ALU = mybir.AluOpType
    ACT = mybir.ActivationFunctionType
    AX = mybir.AxisListType

    B, S, D = x.shape
    P = 128
    KT = D // P
    H0 = 16
    DH0 = D // H0
    HT = P // DH0
    VW = 32
    LN_EPS = 1e-5
    I0 = w_gate.shape[0]
    IT = -(-I0 // P)
    IR = I0 - (IT - 1) * P
    QMAX = 127.0
    E, _, F1 = w1.shape
    FH = F1 // 2
    TOP = 2
    NT = B * S * TOP // P + E - 1
    ROW = D + 4
    SLOTS = 3
    SLOT = 2 * KT * F1 + (F1 // P) * D
    H1 = ig_k.shape[1]
    DH1 = D // H1
    VC = (H1 - 1) * (DH1 + 1) + 96 + 1
    NEG = -0.7 * 3.4028234663852886e38
    MAGIC = 1.5 * 2.0 ** 23
    G = 4
    GB = B // G
    TB = GB * P

    stack = ExitStack()
    with stack:
        def sb(name, shape, dt=F32):
            return stack.enter_context(nc.sbuf_tensor(name, shape, dt))

        def ps(name, shape, dt=F32):
            return stack.enter_context(nc.psum_tensor(name, shape, dt))

        def sem(name):
            return stack.enter_context(nc.semaphore(name))

        def lay(region, *specs):
            at, views = 0, []
            for dt, *shape in specs:
                n = 1
                for s in shape:
                    n *= s
                words = n if dt == F32 else n // 2
                view = region[:, at:at + words]
                if dt != F32:
                    view = view.bitcast(dt)
                names = "abcde"[:len(shape)]
                if len(shape) > 1:
                    view = view.rearrange(f"p ({' '.join(names)}) -> p {' '.join(names)}", **dict(zip(names[1:], shape[1:])))
                views.append(view)
                at += words
            assert at <= region.shape[1], (at, region.shape)
            return views

        x_sb = sb("x_sb", [P, B, D])
        ident = sb("ident", [P, P])
        ident_b = sb("ident_b", [P, P], BF16)
        head_mask = sb("head_mask", [P, HT])
        stats = sb("stats", [P, 2, 6])
        mv = sb("mv", [P, B, 2])
        mv1 = sb("mv1", [P, 2])
        pause = sb("pause", [P, 1])
        pause_p = sb("pause_p", [P, 1])
        one_col = sb("one_col", [P, 1])
        rstd = sb("rstd", [P, B])
        minus_half = sb("minus_half", [P, 64])
        clip = sb("clip", [P, 2])
        w_amax = sb("w_amax", [P, 2 * IT + KT])
        w_scale = sb("w_scale", [P, 2 * IT + KT])
        w_inv = sb("w_inv", [P, 2 * IT + KT])
        gu_scale = sb("gu_scale", [P, 2 * IT])
        wd_diag = sb("wd_diag", [P, KT, P])
        ones_sb = sb("ones_sb", [P, P])
        down_scale = sb("down_scale", [P, D])
        amax1 = sb("amax1", [P, G])
        amax_h = sb("amax_h", [P, G * IT])
        amax_col = sb("amax_col", [P, 2])
        amax_all = sb("amax_all", [P, 2])
        act_scale = sb("act_scale", [P, 2])
        act_inv = sb("act_inv", [P, 2])
        slots = sb("slots", [P, 2, B], U32)
        tile_info = sb("tile_info", [P, 3, NT], I32)
        tok_idx = sb("tok_idx", [P, 2], U32)
        int_tmp = sb("int_tmp", [P, 64], I32)
        empty_row = sb("empty_row", [P, ROW])
        before = sb("before", [P, P], BF16)
        ones_b = sb("ones_b", [P, P], BF16)
        chosen_b = sb("chosen_b", [P, B, E], BF16)
        gate_sb = sb("gate_sb", [P, KT, E])
        xn4 = sb("xn4", [P, 2, GB, D])
        sil = sb("sil", [P, 2, TB])
        down_out = sb("down_out", [P, 2, D])

        region1 = sb("region1", [P, 24500])
        region2 = sb("region2", [P, 18432])

        (wq_sb, wkv_sb, wout_sb, xn, ctx_sb, xcT, qkT, kbd, v_ones, probs, probsT, row_max, outT, rec0, o_sb,
         oT, wgu, wgu_q, wguT, wd, wd_q, wdT, wtmp) = lay(
            region1,
            (F32, KT, D), (F32, KT, 2 * D), (F32, KT, D),
            (F32, 2, D),
            (F32, 2, D),
            (F32, 2, 2 * KT, P),
            (F32, 2, 2 * KT, P),
            (F32, 2, KT, HT, P),
            (F32, 2, H0, VW),
            (F32, KT, HT, P), (F32, KT, HT, P),
            (F32, KT, HT), (F32, 4, P), (F32, H0, 1), (F32, D), (F32, KT, P),
            (F32, 2 * IT, D), (BF16, 2 * IT, D), (BF16, KT, 2 * IT, P),
            (F32, KT, I0), (BF16, KT, I0), (BF16, IT, D), (F32, 8))
        hT, x1nT, xq = lay(region2, (F32, IT, B * P), (F32, KT, B * P), (BF16, KT, B * P))
        _, hq = lay(region2, (F32, IT, B * P), (BF16, IT, B * P))

        (ST, neg_max, xn_c, ctx_c, ctxT_c, q_only, v_c, decay, decayed, h_c, h_sq, gates8, lf, gsum, gmax, ga, gtmp,
         aT, floorT, gk, gk_ctx, rms1, gbias, o_rec, ms, ms_rs) = lay(
            region1,
            (F32, B * H1, P), (F32, B * H1, P), (F32, 2, D), (F32, 2, D), (F32, 2, KT, P),
            (F32, 2, H1, P),
            (F32, 2, VC), (F32, 2, H1, P), (F32, 2, H1, P), (F32, 2, H1, DH1), (F32, H1, DH1),
            (F32, 3, P), (F32, P), (F32, P), (F32, P), (F32, P), (F32, 2, P),
            (F32, B * H1), (F32, B * H1), (F32, 3 * KT, 2 * H1), (F32, KT, 2 * H1), (F32, DH1), (F32, 2),
            (F32, H1), (F32, 2, H1), (F32, 2, H1))
        gates_all = lay(region2, (F32, B * P))[0]
        gates_dram = nc.dram_tensor("gates_dram", (2 * H1, B, P), F32, kind="Internal").ap()
        neg_max_dram = nc.dram_tensor("neg_max_dram", (B * H1, P), F32, kind="Internal").ap()

        (xrow, xT_d, logits, top, oh1, oh2, rt, rt2, rbase, incl, incl2, v1, v2, m12, e2, w12, etiles, eend, eend2, eoff,
         iota_e, iota_t, tcmp, te, tchg, tcum, tslot, slots_f, xg, xgT, sil_d, h_d, hT_d, y_d, w_col) = lay(
            region1,
            (F32, B, ROW), (F32, 2, KT, P), (F32, B, E), (F32, B, E), (F32, B, E), (F32, B, E), (F32, B, E),
            (F32, B, E), (F32, B, E), (F32, B, E), (F32, B, E), (F32, B), (F32, B), (F32, 2, B), (F32, B), (F32, 2, B),
            (F32, E), (F32, E), (F32, E), (F32, E), (F32, E), (F32, NT), (F32, NT, E), (F32, NT), (F32, NT), (F32, NT), (F32, NT),
            (F32, 2, B), (F32, 2, ROW), (F32, 2, KT, P), (F32, 2, FH), (F32, 2, F1), (F32, 2, F1 // P, P),
            (F32, 2, D), (F32, 2))
        routed_dram = nc.dram_tensor("routed_dram", (NT * P, ROW), F32, kind="Internal").ap()
        sum_dram = nc.dram_tensor("sum_dram", (B * P + P, D), F32, kind="Internal").ap()

        psum = ps("psum", [P, 8, 512])

        def bank(n, *shape, count=1, dt=F32):
            view = psum[:, n, :] if count == 1 else psum[:, n:n + count, :].rearrange("p n c -> p (n c)")
            if dt != F32:
                view = view.bitcast(dt)
            names = "abcde"[:len(shape)]
            return view.rearrange(f"p ({' '.join(names)}) -> p {' '.join(names)}", **dict(zip(names[1:], shape[1:])))

        bank0 = bank(0, 4, P)
        bank1 = bank(1, 4, P)
        bank2 = psum[:, 2, :]
        S_ps = [bank(3, HT, P, count=2), bank(5, HT, P, count=2)]
        bank7 = bank(7, 4, P)

        w_loaded = sem("w_loaded")
        x_loaded = [sem(f"x_loaded{i}") for i in range(4)]
        ctx_loaded = [sem(f"ctx_loaded{i}") for i in range(2)]
        out_stored = sem("out_stored")
        consts_ready = sem("consts_ready")
        v_preset = sem("v_preset")
        ln_chain = sem("ln_chain")
        rstd1_ready = sem("rstd1_ready")
        xn_ready = sem("xn_ready")
        t1_done = sem("t1_done")
        t1_evac = sem("t1_evac")
        qk_done = sem("qk_done")
        qk_evac = sem("qk_evac")
        v_done = sem("v_done")
        v_evac = sem("v_evac")
        kbd_ready = sem("kbd_ready")
        s_done = sem("s_done")
        max_ready = sem("max_ready")
        shifted_ready = sem("shifted_ready")
        probs_ready = sem("probs_ready")
        pt_done = sem("pt_done")
        pt_evac = sem("pt_evac")
        pv_done = sem("pv_done")
        outT_ready = sem("outT_ready")
        to_done = sem("to_done")
        rec0_ready = sem("rec0_ready")
        o_ready = sem("o_ready")
        ot_done = sem("ot_done")
        oT_ready = sem("oT_ready")
        wo_done = sem("wo_done")
        x1_ready = sem("x1_ready")

        b_chain = sem("b_chain")
        ln2_chain = sem("ln2_chain")
        rstd2_ready = sem("rstd2_ready")
        fw_loaded = sem("fw_loaded")
        fw_preset = sem("fw_preset")
        clip_loaded = sem("clip_loaded")
        clip_exp = sem("clip_exp")
        wq_ready = sem("wq_ready")
        wT_done = sem("wT_done")
        wT_evac = sem("wT_evac")
        xn4_ready = sem("xn4_ready")
        x1t_done = sem("x1t_done")
        x1nT_ready = sem("x1nT_ready")
        amax_ready = sem("amax_ready")
        amax_all_ready = sem("amax_all_ready")
        xq_ready = sem("xq_ready")
        gate_done = sem("gate_done")
        up_done = sem("up_done")
        sil_ready = sem("sil_ready")
        gu_ready = sem("gu_ready")
        hT_ready = sem("hT_ready")
        amax_h_step = sem("amax_h_step")
        h_clipped = sem("h_clipped")
        hq_ready = sem("hq_ready")
        down_done = sem("down_done")
        down_read = sem("down_read")
        x2_ready = sem("x2_ready")
        ln3_chain = sem("ln3_chain")

        gk_loaded = sem("gk_loaded")
        gk_ready = sem("gk_ready")
        q_preset = sem("q_preset")
        rstd3_ready = sem("rstd3_ready")
        c_chain = sem("c_chain")
        cctx_loaded = [sem(f"cctx_loaded{i}") for i in range(2)]
        xn_c_ready = sem("xn_c_ready")
        ct_done = sem("ct_done")
        ct_evac = sem("ct_evac")
        gates_done = sem("gates_done")
        gates_read = sem("gates_read")
        st_done = sem("st_done")
        st_read = sem("st_read")
        gates_stored = sem("gates_stored")
        gates_loaded = sem("gates_loaded")
        soft_abs = sem("soft_abs")
        soft_log = sem("soft_log")
        neg_max_ready = sem("neg_max_ready")
        neg_max_stored = sem("neg_max_stored")
        neg_max_loaded = [sem(f"neg_max_loaded{i}") for i in range(4)]
        floor_ready = sem("floor_ready")
        a_ready = sem("a_ready")
        aT_done = sem("aT_done")
        aT_ready = sem("aT_ready")
        masked_ready = sem("masked_ready")
        decay_ready = sem("decay_ready")
        decayed_ready = sem("decayed_ready")
        v_c_loaded = [sem(f"v_c_loaded{i}") for i in range(2)]
        pvc_done = sem("pvc_done")
        o_rec_ready = sem("o_rec_ready")
        h_c_ready = sem("h_c_ready")
        h_sq_ready = sem("h_sq_ready")
        ms_ready = sem("ms_ready")
        ms_eps_ready = sem("ms_eps_ready")
        rs_ready = sem("rs_ready")
        scaled_ready = sem("scaled_ready")
        x3_ready = sem("x3_ready")
        ln4_chain = sem("ln4_chain")

        rows_preset = sem("rows_preset")
        rows_emptied = sem("rows_emptied")
        gate_loaded = sem("gate_loaded")
        route_consts = sem("route_consts")
        rstd4_ready = sem("rstd4_ready")
        xrow_ready = sem("xrow_ready")
        dt_done = sem("dt_done")
        dt_evac = sem("dt_evac")
        logits_done = sem("logits_done")
        d_chain = sem("d_chain")
        gap_ready = sem("gap_ready")
        e2_ready = sem("e2_ready")
        chosen_ready = sem("chosen_ready")
        ranks_done = sem("ranks_done")
        route_ready = sem("route_ready")
        info_ready = sem("info_ready")
        routed_stored = sem("routed_stored")
        sum_preset = sem("sum_preset")
        xg_loaded = [sem(f"xg_loaded{i}") for i in range(2)]
        expert_loaded = [sem(f"expert_loaded{i}") for i in range(2)]
        tx_done = sem("tx_done")
        xgT_ready = sem("xgT_ready")
        gu_done = sem("gu_done")
        sil_d_ready = sem("sil_d_ready")
        h_d_ready = sem("h_d_ready")
        th_done = sem("th_done")
        hT_d_ready = sem("hT_d_ready")
        dn_done = sem("dn_done")
        w_part = sem("w_part")
        meta_ready = sem("meta_ready")
        y_ready = sem("y_ready")
        sum_added = sem("sum_added")
        paused = sem("paused")

        block = stack.enter_context(nc.Block())

        def steps(engine, step):
            step(0, 0)
            with engine.Fori(0, (B - 2) // 2) as i:
                step(2 * i + 1, 1, inner=True)
                step(2 * i + 2, 0, inner=True)
            step(B - 1, 1)

        @block.sync
        def _(sp):
            x_v = x.rearrange("b p d -> p b d")
            sp.dma_start(x_sb[:, 0:4, :], x_v[:, 0:4, :]).then_inc(x_loaded[0], 16)
            sp.dma_start(wq_sb[:], wq.rearrange("(t p) n -> p t n", p=P)).then_inc(w_loaded, 16)
            sp.dma_start(ctx_sb[:, 0, :], ctx_in[0, :, :]).then_inc(ctx_loaded[0], 16)
            sp.dma_start(wkv_sb[:], wkv.rearrange("(t p) n -> p t n", p=P)).then_inc(w_loaded, 16)
            sp.dma_start(ctx_sb[:, 1, :], ctx_in[1, :, :]).then_inc(ctx_loaded[1], 16)
            for i in range(1, 4):
                sp.dma_start(x_sb[:, 4 * i:4 * i + 4, :], x_v[:, 4 * i:4 * i + 4, :]).then_inc(x_loaded[i], 16)
            sp.dma_start(wout_sb[:], wout.rearrange("(t p) n -> p t n", p=P)).then_inc(w_loaded, 16)
            whole = (IT - 1) * P
            for n, w in enumerate((w_gate, w_up)):
                sp.dma_start(wgu[:, n * IT:n * IT + IT - 1, :], w[0:whole, :].rearrange("(t p) d -> p t d", p=P)).then_inc(fw_loaded, 16)
                sp.dma_start(wgu[0:IR, n * IT + IT - 1, :], w[whole:I0, :]).then_inc(fw_loaded, 16)
            sp.dma_start(wd, w_down.rearrange("(t p) i -> p t i", p=P)).then_inc(fw_loaded, 16)
            sp.dma_start(clip[:, 0:1], clip_x.unsqueeze(0).to_broadcast([P, 1])).then_inc(clip_loaded, 16)
            sp.dma_start(clip[:, 1:2], clip_down.unsqueeze(0).to_broadcast([P, 1])).then_inc(clip_loaded, 16)
            sp.wait_ge(rows_preset, 2)
            sp.dma_start(routed_dram.rearrange("(t p) c -> p t c", p=P), empty_row[:].unsqueeze(1).to_broadcast([P, NT, ROW])).then_inc(rows_emptied, 16)
            sp.dma_start(sum_dram[B * P:B * P + P, :], empty_row[:, 0:D]).then_inc(sum_preset, 16)
            sp.dma_start(gate_sb[:], gate_w.rearrange("(t p) e -> p t e", p=P)).then_inc(gate_loaded, 16)
            with sp.Fori(0, B // 2 - 1) as i:
                for p in range(2):
                    sp.wait_ge(t1_done, 2 * i + p + 1)
                    sp.dma_start(ctx_sb[:, p, :], ctx_in[2 * i + (p + 2), :, :]).then_inc(ctx_loaded[p], 16)
            sp.wait_ge(x2_ready, B)
            for n, w in enumerate((ig_k, fg_k)):
                sp.dma_start(gk[:, :, n * H1:(n + 1) * H1], w.rearrange("(t p) h -> p t h", p=P)).then_inc(gk_loaded, 16)
            sp.dma_start(rms1, rms_scale.unsqueeze(0).to_broadcast([P, DH1])).then_inc(gk_loaded, 16)
            for n, w in enumerate((ig_b, fg_b)):
                for b in range(B):
                    sp.dma_start(gbias[b * H1:(b + 1) * H1, n:n + 1], w.unsqueeze(1)).then_inc(gk_loaded, 16)
            for b in range(2):
                sp.dma_start(ctx_c[:, b, :], ctx_in[b, :, :]).then_inc(cctx_loaded[b], 16)
            with sp.Fori(0, B // 2 - 1) as i:
                for p in range(2):
                    sp.wait_ge(ct_done, 2 * i + p + 1)
                    sp.dma_start(ctx_c[:, p, :], ctx_in[2 * i + (p + 2), :, :]).then_inc(cctx_loaded[p], 16)
            sp.wait_ge(gates_read, B)
            sp.dma_start(gates_dram.rearrange("h b n -> h (b n)"), gates_all[0:2 * H1, :]).then_inc(gates_stored, 16)
            sp.wait_ge(gates_stored, 16)
            for n in range(2):
                for b in range(B):
                    sp.dma_start(gates8[b * H1:(b + 1) * H1, n, :], gates_dram[n * H1:(n + 1) * H1, b, :]).then_inc(gates_loaded, 16)
            v_v = v_c[:, :, 0:H1 * (DH1 + 1)].rearrange("p b (h d) -> p b h d", d=DH1 + 1)

            def load_v(p, b):
                sp.dma_start(v_v[:, p, :, 0:DH1], ctx_in[b, :, :].rearrange("p (h d) -> p h d", d=DH1)).then_inc(v_c_loaded[p], 16)

            load_v(0, 0)
            load_v(1, 1)
            sp.wait_ge(neg_max_ready, 1)
            sp.dma_start(neg_max_dram, ga[0:B * H1, :]).then_inc(neg_max_stored, 16)
            sp.wait_ge(neg_max_stored, 16)
            for g in range(G):
                rows = slice(g * GB * H1, (g + 1) * GB * H1)
                sp.dma_start(neg_max[:, rows, :], neg_max_dram[rows, :].unsqueeze(0).to_broadcast([P, GB * H1, P])).then_inc(neg_max_loaded[g], 16)
            with sp.Fori(0, B // 2 - 1) as i:
                for p in range(2):
                    sp.wait_ge(pvc_done, 2 * i + p + 1)
                    load_v(p, 2 * i + (p + 2))
            sp.wait_ge(x3_ready, B)
            sp.dma_start(sum_dram[0:B * P, :].rearrange("(b p) d -> p b d", p=P), x_sb[:]).then_inc(sum_preset, 16)
            sp.wait_ge(info_ready, 1)

            def load_tile(t, p, inner=False):
                expert = sp.value_load(tile_info[0:1, 0, bass.ds(t, 1)], min_val=0, max_val=E - 1)
                place = sp.value_load(tile_info[0:1, 1, bass.ds(t, 1)], min_val=0, max_val=(SLOTS - 1) * SLOT)
                new = sp.value_load(tile_info[0:1, 2, bass.ds(t, 1)], min_val=0, max_val=1)
                if inner or t >= 2:
                    sp.wait_ge(meta_ready, t - 1)
                    sp.dma_start(xg[:, p, :], routed_dram[bass.ts(t, P), :]).then_inc(xg_loaded[p], 16)
                    sp.wait_ge(gu_done, 2 * t - 2)
                else:
                    sp.dma_start(xg[:, p, :], routed_dram[t * P:(t + 1) * P, :]).then_inc(xg_loaded[p], 16)
                for n, w in enumerate((w1, w3)):
                    sp.dma_start(region2[:, bass.ds(place + n * KT * F1, KT * F1)].rearrange("p (t f) -> p t f", f=F1),
                                 w.rearrange("e (t p) f -> p e t f", p=P)[:, bass.ds(expert, 1), :, :].rearrange("p e t f -> p (e t) f"),
                                 cond=(new > 0)).then_inc(expert_loaded[p], 16)
                sp.dma_start(region2[:, bass.ds(place + 2 * KT * F1, (F1 // P) * D)].rearrange("p (t d) -> p t d", d=D),
                             w2.rearrange("e (t p) d -> p e t d", p=P)[:, bass.ds(expert, 1), :, :].rearrange("p e t d -> p (e t) d"),
                             cond=(new > 0)).then_inc(expert_loaded[p], 16)

            sp.wait_ge(routed_stored, 16 * TOP * B)
            load_tile(0, 0)
            load_tile(1, 1)
            with sp.Fori(0, (NT - 3) // 2) as i:
                load_tile(2 * i + 2, 0, inner=True)
                load_tile(2 * i + 3, 1, inner=True)
            load_tile(NT - 1, 0)
            sp.wait_ge(sum_added, 16 * NT)
            sp.dma_start(out.rearrange("b p d -> (b p) d"), sum_dram[0:B * P, :]).then_inc(out_stored, 16)
            sp.wait_ge(out_stored, 16)

        @block.gpsimd
        def _(pool):
            nc.gpsimd.memset(minus_half[:], -0.5).then_inc(consts_ready, 1)
            nc.gpsimd.memset(ident[:], 0.0).then_inc(consts_ready, 1)
            nc.gpsimd.memset(head_mask[:], 1.0).then_inc(consts_ready, 1)
            pool.wait_ge(consts_ready, 3)
            nc.gpsimd.affine_select(out=ident[:], in_=ident[:], compare_op=ALU.not_equal, fill=1.0, base=0,
                                    pattern=[[-1, P]], channel_multiplier=1).then_inc(consts_ready, 1)
            nc.gpsimd.affine_select(out=head_mask[:], in_=head_mask[:], compare_op=ALU.is_ge, fill=0.0, base=0,
                                    pattern=[[-DH0, HT]], channel_multiplier=1).then_inc(consts_ready, 1)
            pool.wait_ge(consts_ready, 5)
            nc.gpsimd.affine_select(out=head_mask[:], in_=head_mask[:], compare_op=ALU.is_ge, fill=0.0, base=DH0 - 1,
                                    pattern=[[DH0, HT]], channel_multiplier=-1).then_inc(consts_ready, 1)
            nc.gpsimd.memset(empty_row[:], 0.0).then_inc(route_consts, 1)
            pool.wait_ge(route_consts, 1)
            nc.gpsimd.iota(empty_row[:, D:D + 1].bitcast(I32), pattern=[[0, 1]], base=B * P, channel_multiplier=1).then_inc(rows_preset, 2)
            nc.gpsimd.memset(v_ones[:], 0.0).then_inc(v_preset, 1)
            pool.wait_ge(v_preset, 1)
            nc.gpsimd.memset(v_ones[:, :, :, DH0:DH0 + 1], 1.0).then_inc(v_preset, 1)
            pool.wait_ge(consts_ready, 6)
            for i in range(4):
                pool.wait_ge(ln_chain, 12 * i + 12)
                nc.gpsimd.tensor_tensor(rstd[:, 4 * i:4 * i + 4], rstd[:, 4 * i:4 * i + 4], minus_half[:, 0:4],
                                        ALU.pow).then_inc(rstd1_ready, 1)

            def mask_k(b, p, inner=False):
                for m in range(KT):
                    pool.wait_ge(qk_evac, b + 1)
                    if inner or b >= 2:
                        pool.wait_ge(s_done, 2 * (b - 2) + m + 1)
                    nc.gpsimd.tensor_tensor(kbd[:, p, m, :, :],
                                            qkT[:, p, KT + m, :].unsqueeze(1).to_broadcast([P, HT, P]),
                                            head_mask[:].unsqueeze(2).to_broadcast([P, HT, P]),
                                            ALU.mult).then_inc(kbd_ready, 1)

            nc.gpsimd.memset(ones_sb[:], 1.0).then_inc(fw_preset, 1)
            nc.gpsimd.memset(one_col[:], 1.0).then_inc(fw_preset, 1)
            nc.gpsimd.tensor_copy(ident_b[:], ident[:]).then_inc(fw_preset, 1)

            mask_k(0, 0)
            mask_k(1, 1)
            with pool.Fori(0, (B - 2) // 2) as i:
                mask_k(2 * i + 2, 0, inner=True)
                mask_k(2 * i + 3, 1, inner=True)

            pool.wait_ge(ln2_chain, 3 * B + 1)
            nc.gpsimd.tensor_tensor(rstd[:], rstd[:], minus_half[:, 0:B], ALU.pow).then_inc(rstd2_ready, 1)
            for n in range(2):
                pool.wait_ge(amax_ready, n + 1)
                nc.gpsimd.partition_all_reduce(amax_all[:, n:n + 1], amax_col[:, n:n + 1], P, bass.bass_isa.ReduceOp.max).then_inc(amax_all_ready, 1)

            pool.wait_ge(x2_ready, B)
            nc.gpsimd.memset(q_only, 0.0).then_inc(q_preset, 1)
            nc.gpsimd.memset(v_c, 1.0).then_inc(q_preset, 1)
            pool.wait_ge(ln3_chain, 3 * B + 1)
            nc.gpsimd.tensor_tensor(rstd[:], rstd[:], minus_half[:, 0:B], ALU.pow).then_inc(rstd3_ready, 1)

            def causal(b):
                part = neg_max[:, bass.ds(H1 * b, H1), :]
                nc.gpsimd.affine_select(out=part, in_=part, compare_op=ALU.is_ge, fill=NEG, base=0,
                                        pattern=[[0, H1], [1, P]], channel_multiplier=-1).then_inc(masked_ready, 1)

            def mean_square_root(b, p):
                pool.wait_ge(ms_ready, b + 1)
                nc.gpsimd.tensor_scalar(ms_rs[:, p, :], ms[:, p, :], 1e-6, 1.0, ALU.add, ALU.mult).then_inc(ms_eps_ready, 1)
                pool.wait_ge(ms_eps_ready, b + 1)
                nc.gpsimd.tensor_tensor(ms_rs[:, p, :], ms_rs[:, p, :], minus_half[:, 0:H1], ALU.pow).then_inc(rs_ready, 1)

            for b in range(B):
                if b % GB == 0:
                    pool.wait_ge(neg_max_loaded[b // GB], 16)
                causal(b)
            for b in range(B):
                mean_square_root(b, b % 2)

            nc.gpsimd.memset(before[:], 1.0).then_inc(route_consts, 1)
            nc.gpsimd.memset(ones_b[:], 1.0).then_inc(route_consts, 1)
            pool.wait_ge(route_consts, 2)
            nc.gpsimd.affine_select(out=before[:], in_=before[:], compare_op=ALU.is_gt, fill=0.0, base=0,
                                    pattern=[[1, P]], channel_multiplier=-1).then_inc(route_consts, 1)
            pool.wait_ge(ln4_chain, 3 * B + 1)
            nc.gpsimd.tensor_tensor(rstd[:], rstd[:], minus_half[:, 0:B], ALU.pow).then_inc(rstd4_ready, 1)
            nc.gpsimd.iota(int_tmp[:, 0:E], pattern=[[-1, E]], base=E, channel_multiplier=0).then_inc(route_consts, 1)
            nc.gpsimd.iota(int_tmp[:, E:E + NT], pattern=[[1, NT]], base=0, channel_multiplier=0).then_inc(route_consts, 1)
            nc.gpsimd.iota(xrow[:, :, D:D + 1].bitcast(I32), pattern=[[P, B], [0, 1]], base=0, channel_multiplier=1).then_inc(route_consts, 1)
            pool.wait_ge(route_ready, 1)
            pool.wait_ge(rows_emptied, 16)
            for b in range(B):
                for n in range(TOP):
                    pool.indirect_dma_start(routed_dram, bass.IndirectOffsetOnAxis(ap=slots[:, n, b:b + 1], axis=0),
                                            xrow[:, b, :], None).then_inc(routed_stored, 16)
            pool.wait_ge(sum_preset, 32)

            def add_rows(t, p, inner=False):
                pool.wait_ge(y_ready, t + 1)
                if inner or t >= 1:
                    pool.wait_ge(paused, t)
                    pool.wait_ge(sum_added, 16 * t)
                nc.gpsimd.tensor_tensor(pause_p[:], minus_half[:, 0:1], minus_half[:, 0:1], ALU.add).then_inc(paused, 1)
                pool.indirect_dma_start(sum_dram, bass.IndirectOffsetOnAxis(ap=tok_idx[:, p:p + 1], axis=0),
                                        y_d[:, p, :], None, compute_op=ALU.add).then_inc(sum_added, 16)

            add_rows(0, 0)
            with pool.Fori(0, (NT - 1) // 2) as i:
                add_rows(2 * i + 1, 1, inner=True)
                add_rows(2 * i + 2, 0, inner=True)

        @block.tensor
        def _(pe):
            mm = nc.tensor.matmul
            tr = nc.tensor.transpose

            def front_transposes(b, p, loads, inner=False):
                pe.wait_ge(xn_ready, b + 1)
                pe.wait_ge(ctx_loaded[p], 16 * loads)
                if inner or b >= 1:
                    pe.wait_ge(t1_evac, b)
                for k in range(KT):
                    tr(bank0[:, k, :], xn[:, p, k * P:(k + 1) * P], ident[:])
                for k in range(KT):
                    last = tr(bank0[:, KT + k, :], ctx_sb[:, p, k * P:(k + 1) * P], ident[:])
                last.then_inc(t1_done, 1)

            def front_products(b, p, inner=False):
                pe.wait_ge(t1_evac, b + 1)
                if inner or b >= 1:
                    pe.wait_ge(qk_evac, b)
                for m in range(2 * KT):
                    for k in range(KT):
                        w = wq_sb[:, k, m * P:(m + 1) * P] if m < KT else wkv_sb[:, k, (m - KT) * P:(m - KT + 1) * P]
                        last = mm(bank1[:, m, :], w, xcT[:, p, (m // KT) * KT + k, :], start=(k == 0), stop=(k == KT - 1))
                last.then_inc(qk_done, 1)
                if inner or b >= 1:
                    pe.wait_ge(v_evac, b)
                for k in range(KT):
                    last = mm(bank2[:, 0:D], xcT[:, p, KT + k, :], wkv_sb[:, k, D:2 * D], start=(k == 0), stop=(k == KT - 1))
                last.then_inc(v_done, 1)

            def scores(b, p, m, inner=False):
                pe.wait_ge(kbd_ready, 2 * b + m + 1)
                if inner or b >= 1:
                    pe.wait_ge(pt_evac, 2 * (b - 1) + m + 1)
                for c in range(HT // 4):
                    last = mm(S_ps[m][:, 4 * c:4 * c + 4, :], qkT[:, p, m, :], kbd[:, p, m, 4 * c:4 * c + 4, :],
                              start=True, stop=True)
                last.then_inc(s_done, 1)

            def probs_transposes(b, m):
                pe.wait_ge(probs_ready, 2 * b + m + 1)
                for h in range(HT):
                    last = tr(S_ps[m][:, h, :], probs[:, m, h, :], ident[:])
                last.then_inc(pt_done, 1)

            def values(b, p, m, inner=False):
                pe.wait_ge(pt_evac, 2 * b + m + 1)
                if m == 0:
                    pe.wait_ge(v_evac, b + 1)
                    if inner or b >= 1:
                        pe.wait_ge(x1_ready, b)
                for c in range(HT // 4):
                    for q in range(4):
                        h = 4 * c + q
                        last = mm(bank7[VW * q:VW * q + VW, 2 * m + c, :], v_ones[:, p, HT * m + h, :], probsT[:, m, h, :],
                                  start=True, stop=True)
                last.then_inc(pv_done, 1)

            def tail_a(b):
                pe.wait_ge(outT_ready, b + 1)
                for n in range(4):
                    last = tr(bank7[:, n, :], outT[:, n, :], ident[:])
                last.then_inc(to_done, 1)

            def tail_b(b):
                pe.wait_ge(o_ready, b + 1)
                for k in range(KT):
                    last = tr(bank7[:, k, :], o_sb[:, k * P:(k + 1) * P], ident[:])
                last.then_inc(ot_done, 1)

            def tail_c(b):
                pe.wait_ge(oT_ready, b + 1)
                for k in range(KT):
                    last = mm(bank7[:, 0:KT, :], oT[:, k, :], wout_sb[:, k, :], start=(k == 0), stop=(k == KT - 1))
                last.then_inc(wo_done, 1)

            def step(b, p, inner=False, loads=None):
                scores(b, p, 0, inner)
                if inner or b >= 1:
                    tail_a(b - 1)
                if inner or b + 1 < B:
                    front_transposes(b + 1, 1 - p, loads, inner)
                scores(b, p, 1, inner)
                if inner or b >= 1:
                    tail_b(b - 1)
                if inner or b + 1 < B:
                    front_products(b + 1, 1 - p, inner)
                if inner or b >= 1:
                    tail_c(b - 1)
                probs_transposes(b, 0)
                probs_transposes(b, 1)
                values(b, p, 0, inner)
                values(b, p, 1, inner)

            pe.wait_ge(consts_ready, 6)
            front_transposes(0, 0, 1)
            pe.wait_ge(w_loaded, 48)
            front_products(0, 0)
            step(0, 0, loads=1)
            with pe.Fori(0, (B - 2) // 2) as i:
                step(2 * i + 1, 1, inner=True, loads=i + 2)
                step(2 * i + 2, 0, inner=True, loads=i + 2)
            step(B - 1, 1)
            tail_a(B - 1)
            tail_b(B - 1)
            tail_c(B - 1)

            pe.wait_ge(fw_preset, 6)
            pe.wait_ge(wq_ready, 1)
            for n in range(2 * IT):
                for k in range(KT):
                    last = tr(bank(n // 4, 4, KT, P, dt=BF16)[:, n % 4, k, :], wgu_q[:, n, k * P:(k + 1) * P], ident_b[:])
            last.then_inc(wT_done, 1)
            pe.wait_ge(wq_ready, 2)
            for t in range(IT):
                rows = P if t < IT - 1 else IR
                for k in range(KT):
                    last = tr(bank(3 + t // 4, 4, KT, P, dt=BF16)[0:rows, t % 4, k, :], wd_q[:, k, t * P:t * P + rows], ident_b[:])
            last.then_inc(wT_done, 1)
            for k in range(KT):
                last = mm(bank(5, 4, P)[:, k, :], ones_sb[:], wd_diag[:, k, :], start=True, stop=True)
            last.then_inc(wT_done, 1)

            for g in range(G):
                pe.wait_ge(xn4_ready, g + 1)
                if g >= 1:
                    pe.wait_ge(x1nT_ready, g)
                for k in range(KT):
                    for j in range(GB):
                        last = tr(bank(6 + k, GB, P)[:, j, :], xn4[:, g % 2, j, k * P:(k + 1) * P], ident[:])
                last.then_inc(x1t_done, 1)

            def gate_up(g, first=False):
                pe.wait_ge(xq_ready, 3 * g + 3)
                for t in range(IT):
                    for n, done, read in ((0, gate_done, sil_ready), (1, up_done, hT_ready)):
                        if not first or t >= 2:
                            pe.wait_ge(read, IT * g + t - 1)
                        for k in range(KT):
                            last = mm(psum[:, 2 * (t % 2) + n, :], wguT[:, k, n * IT + t, :], xq[:, k, bass.ts(g, TB)],
                                      start=(k == 0), stop=(k == KT - 1))
                        last.then_inc(done, 1)

            pe.wait_ge(wT_evac, 3)
            gate_up(0, first=True)
            with pe.Fori(1, G) as g:
                gate_up(g)

            def down(g, first=False):
                pe.wait_ge(hq_ready, g + 1)
                for j in range(GB):
                    if not first or j >= 2:
                        pe.wait_ge(down_read, GB * g + j - 1)
                    for t in range(IT):
                        last = mm(psum[:, 4 + j % 2, 0:D], hq[:, t, bass.ds(g * TB + j * P, P)], wdT[:, t, :],
                                  start=(t == 0), stop=(t == IT - 1))
                    last.then_inc(down_done, 1)

            down(0, first=True)
            with pe.Fori(1, G) as g:
                down(g)

            def front_c(b, p, loads, inner=False):
                pe.wait_ge(xn_c_ready, b + 1)
                pe.wait_ge(cctx_loaded[p], 16 * loads)
                if inner or b >= 2:
                    pe.wait_ge(ct_evac, 3 * (b - 1))
                for k in range(KT):
                    tr(bank(p, 4, P)[:, k, :], xn_c[:, p, k * P:(k + 1) * P], ident[:])
                for k in range(KT):
                    last = tr(bank(p, 4, P)[:, KT + k, :], ctx_c[:, p, k * P:(k + 1) * P], ident[:])
                last.then_inc(ct_done, 1)

            def gates_and_scores(b, p, inner=False):
                pe.wait_ge(ct_evac, 3 * b + 3)
                if inner or b >= 2:
                    pe.wait_ge(gates_read, b - 1)
                for h in range(H1):
                    mm(psum[0:2 * H1, 2 + p, 0:P], gk[:, h // 2, :], q_only[:, p, h, :], start=(h == 0), stop=False)
                for k in range(KT):
                    last = mm(psum[0:2 * H1, 2 + p, 0:P], gk_ctx[:, k, :], ctxT_c[:, p, k, :], start=False, stop=(k == KT - 1))
                last.then_inc(gates_done, 1)
                if inner or b >= 2:
                    pe.wait_ge(st_read, b - 1)
                for k in range(KT):
                    last = mm(bank(4 + p, H1, P)[:, 2 * k:2 * k + 2, :], ctxT_c[:, p, k, :], q_only[:, p, 2 * k:2 * k + 2, :],
                              start=True, stop=True)
                last.then_inc(st_done, 1)

            pe.wait_ge(gk_ready, 1)
            pe.wait_ge(x2_ready, B)
            front_c(0, 0, 1)
            front_c(1, 1, 1)
            gates_and_scores(0, 0)
            front_c(2, 0, 2)
            gates_and_scores(1, 1)
            with pe.Fori(1, B // 2 - 1) as i:
                front_c(2 * i + 1, 1, i + 1, inner=True)
                gates_and_scores(2 * i, 0, inner=True)
                front_c(2 * i + 2, 0, i + 2, inner=True)
                gates_and_scores(2 * i + 1, 1, inner=True)
            front_c(B - 1, 1, B // 2)
            gates_and_scores(B - 2, 0)
            gates_and_scores(B - 1, 1)

            pe.wait_ge(a_ready, 2)
            tr(psum[:, 6, 0:B * H1], gtmp[0:B * H1, 0, :], ident[0:B * H1, 0:B * H1])
            tr(psum[:, 6, B * H1:2 * B * H1], gtmp[0:B * H1, 1, :], ident[0:B * H1, 0:B * H1]).then_inc(aT_done, 1)

            def values_c(b, p, loads, inner=False):
                pe.wait_ge(decayed_ready, b + 1)
                pe.wait_ge(v_c_loaded[p], 16 * loads)
                if inner or b >= 2:
                    pe.wait_ge(h_c_ready, b - 1)
                for h in range(H1):
                    at = h * (DH1 + 1)
                    last = mm(psum[:, p, at:at + 96], decayed[:, p, h, :], v_c[:, p, at:at + 96], start=True, stop=True)
                last.then_inc(pvc_done, 1)

            values_c(0, 0, 1)
            values_c(1, 1, 1)
            with pe.Fori(0, B // 2 - 1) as i:
                values_c(2 * i + 2, 0, i + 2, inner=True)
                values_c(2 * i + 3, 1, i + 2, inner=True)

            pe.wait_ge(gate_loaded, 16)

            def router_transposes(b):
                pe.wait_ge(xrow_ready, b + 1)
                if b >= 2:
                    pe.wait_ge(dt_evac, b - 1)
                for k in range(KT):
                    last = tr(bank(b % 2, 4, P)[:, k, :], xrow[:, b, k * P:(k + 1) * P], ident[:])
                last.then_inc(dt_done, 1)

            def router_logits(b):
                pe.wait_ge(dt_evac, b + 1)
                for k in range(KT):
                    last = mm(psum[:, 2, b * E:(b + 1) * E], xT_d[:, b % 2, k, :], gate_sb[:, k, :], start=(k == 0), stop=(k == KT - 1))
                last.then_inc(logits_done, 1)

            router_transposes(0)
            for b in range(B):
                if b + 1 < B:
                    router_transposes(b + 1)
                router_logits(b)
            pe.wait_ge(chosen_ready, 1)
            pe.wait_ge(route_consts, 7)
            chosen_v = chosen_b[:].rearrange("p b e -> p (b e)")
            mm(psum[:, 3, 0:B * E], before[:], chosen_v, start=True, stop=True)
            mm(psum[:, 4, 0:B * E], ones_b[:], chosen_v, start=True, stop=True).then_inc(ranks_done, 1)

            def gate_up_half(t, p, f, place, inner=False):
                if inner or t >= 1:
                    pe.wait_ge(h_d_ready, 2 * t + f - 1)
                for n in range(2):
                    for k in range(KT):
                        last = mm(psum[:, 2 * f + n, :], xgT[:, p, k, :],
                                  region2[:, bass.ds(place + ((n * KT + k) * F1 + f * FH), FH)],
                                  start=(k == 0), stop=(k == KT - 1))
                last.then_inc(gu_done, 1)

            def x_transposes(t, p, loads, inner=False):
                pe.wait_ge(xg_loaded[p], 16 * loads)
                for k in range(KT):
                    last = tr(bank(6, 4, P)[:, k, :], xg[:, p, k * P:(k + 1) * P], ident[:])
                last.then_inc(tx_done, 1)

            def h_transposes(t, p):
                pe.wait_ge(h_d_ready, 2 * t + 2)
                for f in range(F1 // P):
                    last = tr(bank(4, F1 // P, P, count=2)[:, f, :], h_d[:, p, f * P:(f + 1) * P], ident[:])
                last.then_inc(th_done, 1)

            def down_d(t, p, place, inner=False):
                pe.wait_ge(hT_d_ready, t + 1)
                if inner or t >= 1:
                    pe.wait_ge(y_ready, t)
                for f in range(F1 // P):
                    last = mm(psum[:, 7, 0:D], hT_d[:, p, f, :], region2[:, bass.ds(place + (2 * KT * F1 + f * D), D)],
                              start=(f == 0), stop=(f == F1 // P - 1))
                last.then_inc(dn_done, 1)

            def place_of(t):
                return pe.value_load(tile_info[0:1, 1, bass.ds(t, 1)], min_val=0, max_val=(SLOTS - 1) * SLOT)

            def tile_step(t, p, loads, loads_next, inner=False):
                place = place_of(t)
                pe.wait_ge(xgT_ready, t + 1)
                pe.wait_ge(expert_loaded[p], 48 * loads)
                gate_up_half(t, p, 0, place, inner)
                if inner or t >= 1:
                    h_transposes(t - 1, 1 - p)
                gate_up_half(t, p, 1, place, inner)
                if inner or t + 1 < NT:
                    x_transposes(t + 1, 1 - p, loads_next, inner)
                if inner or t >= 1:
                    down_d(t - 1, 1 - p, place_of(t - 1), inner)

            pe.wait_ge(info_ready, 1)
            x_transposes(0, 0, 1)
            tile_step(0, 0, 1, 1)
            with pe.Fori(0, (NT - 3) // 2) as i:
                tile_step(2 * i + 1, 1, i + 1, i + 2, inner=True)
                tile_step(2 * i + 2, 0, i + 2, i + 2, inner=True)
            tile_step(NT - 2, 1, NT // 2, NT // 2 + 1)
            tile_step(NT - 1, 0, NT // 2 + 1, None)
            h_transposes(NT - 1, 0)
            down_d(NT - 1, 0, place_of(NT - 1))

        @block.scalar
        def _(act):
            act_fn = nc.scalar.activation

            def front(b, p):
                act.wait_ge(t1_done, b + 1)
                act_fn(xcT[:, p, :, :], bank0[:, :, :], ACT.Copy).then_inc(t1_evac, 1)

            def exps(b, m):
                act.wait_ge(shifted_ready, 2 * b + m + 1)
                act_fn(probs[:, m, :, :], probs[:, m, :, :], ACT.Exp, scale=float(DH0) ** -0.5).then_inc(probs_ready, 1)

            def v_copy(b, p):
                act.wait_ge(v_done, b + 1)
                act_fn(v_ones[:, p, :, 0:DH0], bank2[:, 0:D].rearrange("p (h d) -> p h d", d=DH0), ACT.Copy).then_inc(v_evac, 1)

            def probsT_copy(b, m):
                act.wait_ge(pt_done, 2 * b + m + 1)
                act_fn(probsT[:, m, :, :], S_ps[m][:, :, :], ACT.Copy).then_inc(pt_evac, 1)

            def step(b, p, inner=False):
                if inner or b + 1 < B:
                    front(b + 1, 1 - p)
                exps(b, 0)
                if inner or b >= 1:
                    act.wait_ge(ot_done, b)
                    act_fn(oT[:, :, :], bank7[:, 0:KT, :], ACT.Copy).then_inc(oT_ready, 1)
                if inner or b + 1 < B:
                    v_copy(b + 1, 1 - p)
                exps(b, 1)
                probsT_copy(b, 0)
                probsT_copy(b, 1)
                act.wait_ge(pv_done, 2 * b + 2)
                act_fn(outT[:, :, :], bank7[:, :, :], ACT.Copy).then_inc(outT_ready, 1)

            front(0, 0)
            act.wait_ge(v_preset, 2)
            v_copy(0, 0)
            steps(act, step)
            act.wait_ge(ot_done, B)
            act_fn(oT[:, :, :], bank7[:, 0:KT, :], ACT.Copy).then_inc(oT_ready, 1)

            act.wait_ge(clip_loaded, 32)
            act_fn(clip[:], clip[:], ACT.Exp, scale=-1.0).then_inc(clip_exp, 1)
            act.wait_ge(wT_done, 1)
            for q in range(3):
                last = act_fn(wguT[:, :, 4 * q:4 * q + 4, :].rearrange("p k n c -> p n k c"), bank(q, 4, KT, P, dt=BF16), ACT.Copy)
            last.then_inc(wT_evac, 1)
            act.wait_ge(wT_done, 3)
            act.wait_ge(fw_preset, 6)
            act_fn(wdT[:, 0:4, :], bank(3, 4, D, dt=BF16), ACT.Copy)
            act_fn(wdT[:, 4:5, :], bank(4, 4, D, dt=BF16)[:, 0:1, :], ACT.Copy)
            act_fn(wdT[0:IR, 5:6, :], bank(4, 4, D, dt=BF16)[0:IR, 1:2, :], ACT.Copy).then_inc(wT_evac, 1)
            act_fn(down_scale[:], psum[:, 5, 0:D], ACT.Copy).then_inc(wT_evac, 1)
            for g in range(G):
                act.wait_ge(x1t_done, g + 1)
                act_fn(x1nT[:, :, g * TB:(g + 1) * TB], psum[:, 6:8, :], ACT.Copy).then_inc(x1nT_ready, 1)
            act.wait_ge(gu_ready, 1)

            def silu(g, first=False):
                for t in range(IT):
                    act.wait_ge(gate_done, IT * g + t + 1)
                    if not first or t >= 2:
                        act.wait_ge(hT_ready, IT * g + t - 1)
                    act_fn(sil[:, t % 2, :], psum[:, 2 * (t % 2), :], ACT.Silu, scale=gu_scale[:, t:t + 1]).then_inc(sil_ready, 1)

            silu(0, first=True)
            with act.Fori(1, G) as g:
                silu(g)
            with act.Fori(0, G) as g:
                act.wait_ge(h_clipped, 2 * g + 2)
                act_fn(hq[:, :, bass.ts(g, TB)], hT[:, :, bass.ts(g, TB)], ACT.Copy, bias=-MAGIC).then_inc(hq_ready, 1)

            HALF = P // 2

            def front_c(b, p):
                act.wait_ge(ct_done, b + 1)
                for half in range(2):
                    rows = slice(half * HALF, (half + 1) * HALF)
                    act_fn(q_only[rows, p, half:H1:2, :], bank(p, 4, P)[rows, 0:KT, :], ACT.Copy).then_inc(ct_evac, 1)
                act_fn(ctxT_c[:, p, :, :], bank(p, 4, P)[:, KT:2 * KT, :], ACT.Copy).then_inc(ct_evac, 1)

            act.wait_ge(q_preset, 2)
            front_c(0, 0)
            front_c(1, 1)
            with act.Fori(0, B // 2 - 1) as i:
                for p in range(2):
                    act.wait_ge(st_done, 2 * i + p + 1)
                    front_c(2 * i + (p + 2), p)

            act.wait_ge(soft_abs, 1)
            act_fn(lf[0:B * H1, :], lf[0:B * H1, :], ACT.Exp, scale=-1.0).then_inc(soft_log, 1)
            act.wait_ge(soft_log, 1)
            act_fn(lf[0:B * H1, :], lf[0:B * H1, :], ACT.Ln, bias=one_col[0:B * H1, :]).then_inc(soft_log, 1)
            act.wait_ge(floor_ready, 1)
            act_fn(gtmp[0:B * H1, 1, :], gsum[0:B * H1, :], ACT.Exp, scale=-1.0).then_inc(a_ready, 1)
            act.wait_ge(aT_done, 1)
            act_fn(aT, psum[:, 6, 0:B * H1], ACT.Copy)
            act_fn(floorT, psum[:, 6, B * H1:2 * B * H1], ACT.Copy, bias=1e-6).then_inc(aT_ready, 1)

            def decays(b, p, inner=False):
                act.wait_ge(masked_ready, b + 1)
                if inner or b >= 2:
                    act.wait_ge(decayed_ready, b - 1)
                for h in range(H1):
                    n = H1 * b + h
                    last = act_fn(decay[:, p, h, :], neg_max[:, bass.ds(n, 1), :].rearrange("p o c -> p (o c)"), ACT.Exp,
                                  bias=aT[:, bass.ds(n, 1)])
                last.then_inc(decay_ready, 1)

            def squares(b, p):
                act.wait_ge(h_c_ready, b + 1)
                if not isinstance(b, int) or b >= 1:
                    act.wait_ge(ms_ready, b)
                act_fn(h_sq, h_c[:, p, :, :], ACT.Square, scale=float(DH1) ** -0.5).then_inc(h_sq_ready, 1)

            act.wait_ge(aT_ready, 1)
            decays(0, 0)
            decays(1, 1)
            squares(0, 0)
            with act.Fori(0, B // 2 - 1) as i:
                decays(2 * i + 2, 0, inner=True)
                squares(2 * i + 1, 1)
                decays(2 * i + 3, 1, inner=True)
                squares(2 * i + 2, 0)
            squares(B - 1, 1)

            for b in range(B):
                act.wait_ge(dt_done, b + 1)
                if b >= 2:
                    act.wait_ge(logits_done, b - 1)
                act_fn(xT_d[:, b % 2, :, :], bank(b % 2, 4, P)[:, 0:KT, :], ACT.Copy).then_inc(dt_evac, 1)
            act.wait_ge(gap_ready, 1)
            act_fn(e2, v2, ACT.Exp).then_inc(e2_ready, 1)

            def silu_d(t, f):
                act.wait_ge(gu_done, 2 * t + f + 1)
                act_fn(sil_d[:, f, :], psum[:, 2 * f, :], ACT.Silu).then_inc(sil_d_ready, 1)

            def x_copy(t, p):
                act.wait_ge(tx_done, t + 1)
                act_fn(xgT[:, p, :, :], bank(6, 4, P)[:, 0:KT, :], ACT.Copy).then_inc(xgT_ready, 1)

            def h_copy(t, p):
                act.wait_ge(th_done, t + 1)
                act_fn(hT_d[:, p, :, :], bank(4, F1 // P, P, count=2), ACT.Copy).then_inc(hT_d_ready, 1)

            def tile_step(t, p, inner=False):
                silu_d(t, 0)
                if inner or t >= 1:
                    h_copy(t - 1, 1 - p)
                silu_d(t, 1)
                if inner or t + 1 < NT:
                    x_copy(t + 1, 1 - p)

            x_copy(0, 0)
            tile_step(0, 0)
            with act.Fori(0, (NT - 3) // 2) as i:
                tile_step(2 * i + 1, 1, inner=True)
                tile_step(2 * i + 2, 0, inner=True)
            tile_step(NT - 2, 1)
            tile_step(NT - 1, 0)
            h_copy(NT - 1, 0)

        @block.vector
        def _(dve):
            def row_stats(b, chain):
                nc.vector.bn_stats(stats[:, 0, :], x_sb[:, b, :]).then_inc(ln_chain, 1)
                dve.wait_ge(ln_chain, chain + 1)
                nc.vector.bn_aggr(mv[:, b, :], stats[:, 0, :]).then_inc(ln_chain, 1)
                dve.wait_ge(ln_chain, chain + 2)
                nc.vector.tensor_scalar_add(rstd[:, b:b + 1], mv[:, b, 1:2], LN_EPS).then_inc(ln_chain, 1)

            def norm(b, p, inner=False):
                if inner or b >= 2:
                    dve.wait_ge(t1_done, b - 1)
                nc.vector.tensor_scalar(xn[:, p, :], x_sb[:, b, :], mv[:, b, 0:1], rstd[:, bass.ds(b, 1)] if inner else rstd[:, b:b + 1],
                                        ALU.subtract, ALU.mult).then_inc(xn_ready, 1)

            nc.vector.memset(wgu[IR:P, IT - 1, :], 1.0).then_inc(fw_preset, 1)
            nc.vector.memset(wgu[IR:P, 2 * IT - 1, :], 1.0).then_inc(fw_preset, 1)
            nc.vector.memset(wdT[IR:P, IT - 1, :], 0.0).then_inc(fw_preset, 1)

            for i in range(4):
                dve.wait_ge(x_loaded[i], 16)
                for b in range(4 * i, 4 * i + 4):
                    row_stats(b, 3 * b)
                if i == 0:
                    dve.wait_ge(rstd1_ready, 1)
                    norm(0, 0)
                    norm(1, 1)
            dve.wait_ge(rstd1_ready, 4)

            def qk_copy(b, p):
                dve.wait_ge(qk_done, b + 1)
                nc.vector.tensor_copy(qkT[:, p, :, :], bank1[:, :, :]).then_inc(qk_evac, 1)

            def softmax_shift(b, m):
                dve.wait_ge(s_done, 2 * b + m + 1)
                nc.vector.tensor_reduce(row_max[:, m, :], S_ps[m][:, :, :], AX.X, ALU.max).then_inc(max_ready, 1)
                dve.wait_ge(max_ready, 2 * b + m + 1)
                nc.vector.tensor_tensor(probs[:, m, :, :], S_ps[m][:, :, :],
                                        row_max[:, m, :].unsqueeze(2).to_broadcast([P, HT, P]),
                                        ALU.subtract).then_inc(shifted_ready, 1)

            def tail_norm(b):
                dve.wait_ge(to_done, b + 1)
                o_v = bank7[:, :, :].rearrange("p n (q c) -> p (n q) c", c=VW)
                nc.vector.reciprocal(rec0[:, :, :], o_v[:, :, DH0:DH0 + 1]).then_inc(rec0_ready, 1)
                dve.wait_ge(rec0_ready, b + 1)
                nc.vector.tensor_tensor(o_sb[:].rearrange("p (h d) -> p h d", d=DH0), o_v[:, :, 0:DH0],
                                        rec0[:, :, :].to_broadcast([P, H0, DH0]), ALU.mult).then_inc(o_ready, 1)

            def tail_add(b):
                dve.wait_ge(wo_done, b + 1)
                nc.vector.tensor_tensor(x_sb[:, b, :], x_sb[:, b, :], bank7[:, 0:KT, :].rearrange("p k n -> p (k n)"),
                                        ALU.add).then_inc(x1_ready, 1)
                dve.wait_ge(x1_ready, b + 1)
                token_stats(b, ln2_chain, 3 * b)

            def token_stats(b, chain, n):
                nc.vector.memset(pause[:], 0.0)
                nc.vector.bn_stats(stats[:, 0, :], x_sb[:, b, :]).then_inc(chain, 1)
                dve.wait_ge(chain, n + 1)
                nc.vector.memset(pause[:], 0.0)
                nc.vector.bn_aggr(mv1[:], stats[:, 0, :]).then_inc(chain, 1)
                dve.wait_ge(chain, n + 2)
                nc.vector.tensor_copy(mv[:, b, :], mv1[:]).then_inc(chain, 1)

            def step(b, p, inner=False):
                softmax_shift(b, 0)
                if inner or b >= 1:
                    tail_norm(b - 1)
                if inner or b + 2 < B:
                    norm(b + 2, p, inner)
                softmax_shift(b, 1)
                if inner or b + 1 < B:
                    qk_copy(b + 1, 1 - p)
                if inner or b >= 1:
                    tail_add(b - 1)

            qk_copy(0, 0)
            step(0, 0)
            with dve.Fori(0, (B - 2) // 2 - 1) as i:
                step(2 * i + 1, 1, inner=True)
                step(2 * i + 2, 0, inner=True)
            step(B - 3, 1)
            step(B - 2, 0)
            step(B - 1, 1)
            tail_norm(B - 1)
            tail_add(B - 1)

            counted = [0]

            def link(instruction):
                counted[0] += 1
                instruction.then_inc(b_chain, 1)
                dve.wait_ge(b_chain, counted[0])

            dve.wait_ge(ln2_chain, 3 * B)
            nc.vector.tensor_scalar_add(rstd[:], mv[:, :, 1], LN_EPS).then_inc(ln2_chain, 1)
            dve.wait_ge(fw_loaded, 80)
            dve.wait_ge(fw_preset, 6)
            nc.vector.tensor_reduce(w_amax[:, 0:2 * IT], wgu, AX.X, ALU.max, apply_absolute_value=True)
            link(nc.vector.tensor_reduce(w_amax[:, 2 * IT:2 * IT + KT], wd, AX.X, ALU.max, apply_absolute_value=True))
            link(nc.vector.tensor_scalar_mul(w_scale[:], w_amax[:], 1.0 / QMAX))
            link(nc.vector.reciprocal(w_inv[:], w_scale[:]))
            for n in range(2 * IT):
                last = nc.vector.tensor_scalar(wgu[:, n, :], wgu[:, n, :], w_inv[:, n:n + 1], QMAX, ALU.mult, ALU.min)
            link(last)
            link(nc.vector.tensor_scalar(wgu, wgu, -QMAX - 1.0, MAGIC, ALU.max, ALU.add))
            link(nc.vector.tensor_scalar_add(wgu_q, wgu, -MAGIC))
            nc.vector.memset(wgu_q[IR:P, IT - 1, :], 0.0)
            nc.vector.memset(wgu_q[IR:P, 2 * IT - 1, :], 0.0).then_inc(wq_ready, 1)
            for k in range(KT):
                last = nc.vector.tensor_scalar(wd[:, k, :], wd[:, k, :], w_inv[:, 2 * IT + k:2 * IT + k + 1], QMAX, ALU.mult, ALU.min)
                nc.vector.tensor_scalar(wd_diag[:, k, :], ident[:], w_scale[:, 2 * IT + k:2 * IT + k + 1], None, ALU.mult)
            link(last)
            link(nc.vector.tensor_scalar(wd, wd, -QMAX - 1.0, MAGIC, ALU.max, ALU.add))
            nc.vector.tensor_scalar_add(wd_q, wd, -MAGIC).then_inc(wq_ready, 1)
            dve.wait_ge(clip_exp, 1)
            link(nc.vector.tensor_scalar(clip[:], clip[:], 1.0, QMAX, ALU.add, ALU.mult))
            link(nc.vector.reciprocal(clip[:], clip[:]))

            dve.wait_ge(rstd2_ready, 1)
            for g in range(G):
                if g >= 2:
                    dve.wait_ge(x1t_done, g - 1)
                for j in range(GB):
                    b = g * GB + j
                    last = nc.vector.tensor_scalar(xn4[:, g % 2, j, :], x_sb[:, b, :], mv[:, b, 0:1], rstd[:, b:b + 1],
                                                   ALU.subtract, ALU.mult)
                last.then_inc(xn4_ready, 1)
                dve.wait_ge(xn4_ready, g + 1)
                last = nc.vector.tensor_reduce(amax1[:, g:g + 1], xn4[:, g % 2, :, :], AX.XY, ALU.max, apply_absolute_value=True)
            link(last)

            def activation_scale(n, values):
                nc.vector.tensor_reduce(amax_col[:, n:n + 1], values, AX.X, ALU.max).then_inc(amax_ready, 1)
                dve.wait_ge(amax_all_ready, n + 1)
                link(nc.vector.tensor_tensor(act_scale[:, n:n + 1], amax_all[:, n:n + 1], clip[:, n:n + 1], ALU.mult))
                link(nc.vector.reciprocal(act_inv[:, n:n + 1], act_scale[:, n:n + 1]))

            activation_scale(0, amax1[:])
            nc.vector.tensor_scalar(gu_scale[:], w_scale[:, 0:2 * IT], act_scale[:, 0:1], None, ALU.mult).then_inc(gu_ready, 1)
            dve.wait_ge(x1nT_ready, G)
            for g in range(G):
                part = x1nT[:, :, g * TB:(g + 1) * TB]
                nc.vector.tensor_scalar(part, part, act_inv[:, 0:1], QMAX, ALU.mult, ALU.min).then_inc(xq_ready, 1)
                dve.wait_ge(xq_ready, 3 * g + 1)
                nc.vector.tensor_scalar(part, part, -QMAX - 1.0, MAGIC, ALU.max, ALU.add).then_inc(xq_ready, 1)
                dve.wait_ge(xq_ready, 3 * g + 2)
                nc.vector.tensor_scalar_add(xq[:, :, g * TB:(g + 1) * TB], part, -MAGIC).then_inc(xq_ready, 1)

            def hidden(g):
                for t in range(IT):
                    n = IT * g + t
                    dve.wait_ge(up_done, n + 1)
                    dve.wait_ge(sil_ready, n + 1)
                    part = hT[:, t, bass.ts(g, TB)]
                    nc.vector.scalar_tensor_tensor(out=part, in0=psum[:, 2 * (t % 2) + 1, :],
                                                   scalar=gu_scale[:, IT + t:IT + t + 1], in1=sil[:, t % 2, :],
                                                   op0=ALU.mult, op1=ALU.mult).then_inc(hT_ready, 1)
                    dve.wait_ge(hT_ready, n + 1)
                    nc.vector.tensor_reduce(amax_h[:, bass.ds(n, 1)], part, AX.X, ALU.max,
                                            apply_absolute_value=True).then_inc(amax_h_step, 1)

            with dve.Fori(0, G) as g:
                hidden(g)
            dve.wait_ge(amax_h_step, G * IT)
            activation_scale(1, amax_h[:])
            dve.wait_ge(wT_evac, 3)
            link(nc.vector.tensor_scalar(down_scale[:], down_scale[:], act_scale[:, 1:2], None, ALU.mult))

            def round_hidden(g):
                part = hT[:, :, bass.ts(g, TB)]
                nc.vector.tensor_scalar(part, part, act_inv[:, 1:2], QMAX, ALU.mult, ALU.min).then_inc(h_clipped, 1)
                dve.wait_ge(h_clipped, 2 * g + 1)
                nc.vector.tensor_scalar(part, part, -QMAX - 1.0, MAGIC, ALU.max, ALU.add).then_inc(h_clipped, 1)

            def add_down(g):
                for j in range(GB):
                    b = GB * g + j
                    dve.wait_ge(down_done, b + 1)
                    nc.vector.tensor_tensor(down_out[:, j % 2, :], psum[:, 4 + j % 2, 0:D], down_scale[:], ALU.mult).then_inc(down_read, 1)
                    dve.wait_ge(down_read, b + 1)
                    x_b = x_sb[:, bass.ds(b, 1), :].rearrange("p o d -> p (o d)")
                    nc.vector.tensor_tensor(x_b, x_b, down_out[:, j % 2, :], ALU.add).then_inc(x2_ready, 1)
                    dve.wait_ge(x2_ready, b + 1)
                    token_stats(b, ln3_chain, 3 * b)

            round_hidden(0)
            with dve.Fori(0, G - 1) as g:
                round_hidden(g + 1)
                add_down(g)
            add_down(G - 1)

            dve.wait_ge(ln3_chain, 3 * B)
            nc.vector.tensor_scalar_add(rstd[:], mv[:, :, 1], LN_EPS).then_inc(ln3_chain, 1)
            dve.wait_ge(gk_loaded, 16 * (3 + 2 * B))
            nc.vector.tensor_tensor(gk_ctx, gk[:, KT:2 * KT, :], gk[:, 2 * KT:3 * KT, :], ALU.add).then_inc(gk_ready, 1)
            nc.vector.tensor_scalar_add(rms1, rms1, 1.0)
            dve.wait_ge(rstd3_ready, 1)

            def norm_c(b, p):
                nc.vector.tensor_scalar(xn_c[:, p, :], x_sb[:, b, :], mv[:, b, 0:1], rstd[:, bass.ds(b, 1)],
                                        ALU.subtract, ALU.mult).then_inc(xn_c_ready, 1)

            def read_gates_and_scores(b, p):
                dve.wait_ge(gates_done, b + 1)
                nc.vector.tensor_copy(gates_all[0:2 * H1, bass.ts(b, P)], psum[0:2 * H1, 2 + p, 0:P]).then_inc(gates_read, 1)
                dve.wait_ge(st_done, b + 1)
                nc.vector.tensor_scalar_mul(ST[:, bass.ds(H1 * b, H1), :], bank(4 + p, H1, P), float(DH1) ** -0.5).then_inc(st_read, 1)

            norm_c(0, 0)
            norm_c(1, 1)
            with dve.Fori(0, B // 2 - 1) as i:
                for p in range(2):
                    dve.wait_ge(ct_done, 2 * i + p + 1)
                    norm_c(2 * i + (p + 2), p)
                    read_gates_and_scores(2 * i + p, p)
            read_gates_and_scores(B - 2, 0)
            read_gates_and_scores(B - 1, 1)

            R = B * H1
            counted = [0]

            def link_c(instruction):
                counted[0] += 1
                instruction.then_inc(c_chain, 1)
                dve.wait_ge(c_chain, counted[0])

            dve.wait_ge(gates_loaded, 16 * 2 * B)
            for n in range(2):
                last = nc.vector.tensor_scalar(gates8[0:R, n, :], gates8[0:R, n, :], gbias[0:R, n:n + 1], None, ALU.add)
            link_c(last)
            link_c(nc.vector.tensor_scalar_mul(lf[0:R, :], gates8[0:R, 1, :], -1.0))
            nc.vector.tensor_tensor(lf[0:R, :], lf[0:R, :], gates8[0:R, 1, :], ALU.max).then_inc(soft_abs, 1)
            dve.wait_ge(soft_log, 2)
            link_c(nc.vector.scalar_tensor_tensor(out=lf[0:R, :], in0=gates8[0:R, 1, :], scalar=0.0, in1=lf[0:R, :],
                                                  op0=ALU.min, op1=ALU.subtract))
            link_c(nc.vector.tensor_tensor_scan(gsum[0:R, :], ones_sb[0:R, :], lf[0:R, :], 0.0, ALU.mult, ALU.add))
            nc.vector.tensor_tensor(gtmp[0:R, 0, :], gates8[0:R, 0, :], gsum[0:R, :], ALU.subtract).then_inc(a_ready, 1)
            dve.wait_ge(a_ready, 1)
            link_c(nc.vector.tensor_tensor_scan(gmax[0:R, :], ones_sb[0:R, :], gtmp[0:R, 0, :], NEG, ALU.mult, ALU.max))
            nc.vector.tensor_scalar_mul(ga[0:R, :], gmax[0:R, :], -1.0).then_inc(neg_max_ready, 1)
            nc.vector.tensor_tensor(gsum[0:R, :], gsum[0:R, :], gmax[0:R, :], ALU.add).then_inc(floor_ready, 1)

            def decay_scores(b, p, inner=False):
                dve.wait_ge(decay_ready, b + 1)
                if inner or b >= 2:
                    dve.wait_ge(pvc_done, b - 1)
                nc.vector.tensor_tensor(decayed[:, p, :, :], ST[:, bass.ds(H1 * b, H1), :], decay[:, p, :, :],
                                        ALU.mult).then_inc(decayed_ready, 1)

            def normalise(b, p):
                o_v = psum[:, p, 0:H1 * (DH1 + 1)].rearrange("p (h d) -> p h d", d=DH1 + 1)
                dve.wait_ge(pvc_done, b + 1)
                nc.vector.scalar_tensor_tensor(out=o_rec, in0=o_v[:, :, DH1], scalar=1e-6, in1=floorT[:, bass.ds(H1 * b, H1)],
                                               op0=ALU.add, op1=ALU.max).then_inc(o_rec_ready, 1)
                dve.wait_ge(o_rec_ready, 2 * b + 1)
                nc.vector.reciprocal(o_rec, o_rec).then_inc(o_rec_ready, 1)
                dve.wait_ge(o_rec_ready, 2 * b + 2)
                nc.vector.tensor_tensor(h_c[:, p, :, :], o_v[:, :, 0:DH1], o_rec.unsqueeze(2).to_broadcast([P, H1, DH1]),
                                        ALU.mult).then_inc(h_c_ready, 1)
                dve.wait_ge(h_sq_ready, b + 1)
                nc.vector.tensor_reduce(ms[:, p, :], h_sq, AX.X, ALU.add).then_inc(ms_ready, 1)

            def add_attention(b, p):
                h_v = h_c[:, p, :, :]
                dve.wait_ge(rs_ready, b + 1)
                nc.vector.tensor_tensor(h_v, h_v, ms_rs[:, p, :].unsqueeze(2).to_broadcast([P, H1, DH1]), ALU.mult).then_inc(scaled_ready, 1)
                dve.wait_ge(scaled_ready, 2 * b + 1)
                nc.vector.tensor_tensor(h_v, h_v, rms1.unsqueeze(1).to_broadcast([P, H1, DH1]), ALU.mult).then_inc(scaled_ready, 1)
                dve.wait_ge(scaled_ready, 2 * b + 2)
                x_b = x_sb[:, bass.ds(b, 1), :].rearrange("p o d -> p (o d)")
                nc.vector.tensor_tensor(x_b, x_b, h_v.rearrange("p h d -> p (h d)"), ALU.add).then_inc(x3_ready, 1)
                dve.wait_ge(x3_ready, b + 1)
                token_stats(b, ln4_chain, 3 * b)

            decay_scores(0, 0)
            decay_scores(1, 1)
            normalise(0, 0)
            with dve.Fori(0, B // 2 - 1) as i:
                decay_scores(2 * i + 2, 0, inner=True)
                normalise(2 * i + 1, 1)
                add_attention(2 * i, 0)
                decay_scores(2 * i + 3, 1, inner=True)
                normalise(2 * i + 2, 0)
                add_attention(2 * i + 1, 1)
            normalise(B - 1, 1)
            add_attention(B - 2, 0)
            add_attention(B - 1, 1)

            dve.wait_ge(ln4_chain, 3 * B)
            nc.vector.tensor_scalar_add(rstd[:], mv[:, :, 1], LN_EPS).then_inc(ln4_chain, 1)
            dve.wait_ge(rstd4_ready, 1)
            for b in range(B):
                nc.vector.tensor_scalar(xrow[:, b, 0:D], x_sb[:, b, :], mv[:, b, 0:1], rstd[:, b:b + 1],
                                        ALU.subtract, ALU.mult).then_inc(xrow_ready, 1)
            counted_d = [0]

            def link_d(instruction):
                counted_d[0] += 1
                instruction.then_inc(d_chain, 1)
                dve.wait_ge(d_chain, counted_d[0])

            tt = nc.vector.tensor_tensor
            over_e = lambda v: v.unsqueeze(2).to_broadcast([P, B, E])
            over_b = lambda v: v.unsqueeze(1).to_broadcast([P, B, E])
            dve.wait_ge(route_consts, 7)
            nc.vector.tensor_copy(iota_e, int_tmp[:, 0:E])
            link_d(nc.vector.tensor_copy(iota_t, int_tmp[:, E:E + NT]))
            dve.wait_ge(logits_done, B)
            link_d(nc.vector.tensor_copy(logits, psum[:, 2, 0:B * E].rearrange("p (b e) -> p b e", e=E)))
            left = logits
            for n, (value, one_hot) in enumerate(((v1, oh1), (v2, oh2))):
                link_d(nc.vector.tensor_reduce(value, left, AX.X, ALU.max))
                link_d(tt(rt, left, over_e(value), ALU.is_ge))
                link_d(tt(rt, rt, over_b(iota_e), ALU.mult))
                link_d(nc.vector.tensor_reduce(m12[:, n, :], rt, AX.X, ALU.max))
                link_d(tt(one_hot, over_b(iota_e), over_e(m12[:, n, :]), ALU.is_equal))
                if n == 0:
                    link_d(nc.vector.scalar_tensor_tensor(out=top, in0=one_hot, scalar=NEG, in1=left, op0=ALU.mult, op1=ALU.add))
                    left = top
            nc.vector.tensor_tensor(chosen_b[:], oh1, oh2, ALU.add).then_inc(chosen_ready, 1)
            nc.vector.tensor_tensor(v2, v2, v1, ALU.subtract).then_inc(gap_ready, 1)
            dve.wait_ge(e2_ready, 1)
            link_d(nc.vector.tensor_scalar_add(w12[:, 0, :], e2, 1.0))
            link_d(nc.vector.reciprocal(w12[:, 0, :], w12[:, 0, :]))
            link_d(tt(w12[:, 1, :], e2, w12[:, 0, :], ALU.mult))
            col = lambda c: xrow[:, :, D + c]
            nc.vector.tensor_copy(col(1), m12[:, 0, :])
            tt(col(2), w12[:, 0, :], w12[:, 1, :], ALU.subtract)
            nc.vector.tensor_copy(col(3), w12[:, 1, :])
            dve.wait_ge(ranks_done, 1)
            counts = psum[:, 4, 0:B * E].rearrange("p (b e) -> p b e", e=E)
            link_d(nc.vector.tensor_copy(rt, counts))
            src, dst, step_by = rt, incl, 1
            while step_by < B:
                nc.vector.tensor_copy(dst[:, 0:step_by, :], src[:, 0:step_by, :])
                link_d(tt(dst[:, step_by:B, :], src[:, step_by:B, :], src[:, 0:B - step_by, :], ALU.add))
                src, dst = dst, (incl2 if dst is incl else incl)
                step_by *= 2
            link_d(nc.vector.tensor_scalar(etiles, src[:, B - 1, :], P - 1.0, 1.0 / P, ALU.add, ALU.mult))
            link_d(nc.vector.tensor_scalar(etiles, etiles, -(0.5 - 0.25 / P), MAGIC, ALU.add, ALU.add))
            link_d(nc.vector.tensor_scalar_add(etiles, etiles, -MAGIC))
            esrc, edst, step_by = etiles, eend, 1
            while step_by < E:
                nc.vector.tensor_copy(edst[:, 0:step_by], esrc[:, 0:step_by])
                link_d(tt(edst[:, step_by:E], esrc[:, step_by:E], esrc[:, 0:E - step_by], ALU.add))
                esrc, edst = edst, (eend2 if edst is eend else eend)
                step_by *= 2
            link_d(tt(eoff, esrc, etiles, ALU.subtract))
            link_d(nc.vector.tensor_scalar_mul(eoff, eoff, float(P)))
            link_d(tt(rbase, src, rt, ALU.subtract))
            link_d(tt(rbase, rbase, psum[:, 3, 0:B * E].rearrange("p (b e) -> p b e", e=E), ALU.add))
            link_d(tt(rbase, rbase, over_b(eoff), ALU.add))
            for n, one_hot in enumerate((oh1, oh2)):
                link_d(tt(rt2, one_hot, rbase, ALU.mult))
                link_d(nc.vector.tensor_reduce(slots_f[:, n, :], rt2, AX.X, ALU.add))
            nc.vector.tensor_copy(slots[:], slots_f).then_inc(route_ready, 1)
            link_d(tt(tcmp, esrc.unsqueeze(1).to_broadcast([P, NT, E]), iota_t.unsqueeze(2).to_broadcast([P, NT, E]), ALU.is_le))
            link_d(nc.vector.tensor_reduce(te, tcmp, AX.X, ALU.add))
            link_d(nc.vector.tensor_scalar_min(te, te, E - 1.0))
            nc.vector.memset(tchg[:, 0:1], 1.0)
            link_d(tt(tchg[:, 1:NT], te[:, 1:NT], te[:, 0:NT - 1], ALU.not_equal))
            link_d(nc.vector.tensor_tensor_scan(tcum, ones_sb[:, 0:NT], tchg, -1.0, ALU.mult, ALU.add))
            link_d(nc.vector.tensor_scalar(tslot, tcum, 1.0 / SLOTS, -1.0 / SLOTS, ALU.mult, ALU.add))
            link_d(nc.vector.tensor_scalar_add(tslot, tslot, MAGIC))
            link_d(nc.vector.tensor_scalar(tslot, tslot, -MAGIC, -float(SLOTS), ALU.add, ALU.mult))
            link_d(tt(tslot, tslot, tcum, ALU.add))
            link_d(nc.vector.tensor_scalar_mul(tslot, tslot, float(SLOT)))
            nc.vector.tensor_copy(tile_info[:, 0, :], te)
            nc.vector.tensor_copy(tile_info[:, 1, :], tslot)
            link_d(nc.vector.tensor_copy(tile_info[:, 2, :], tchg))
            nc.vector.tensor_scalar(te, te, -1.0, float(E), ALU.mult, ALU.add).then_inc(info_ready, 1)

            def hidden_d(t, p, f):
                dve.wait_ge(gu_done, 2 * t + f + 1)
                dve.wait_ge(sil_d_ready, 2 * t + f + 1)
                tt(h_d[:, p, f * FH:(f + 1) * FH], psum[:, 2 * f + 1, :], sil_d[:, f, :], ALU.mult).then_inc(h_d_ready, 1)

            def route_of(t, p, loads, inner=False):
                dve.wait_ge(xg_loaded[p], 16 * loads)
                if inner or t >= 2:
                    dve.wait_ge(sum_added, 16 * (t - 1))
                nc.vector.tensor_scalar(w_col[:, p:p + 1], xg[:, p, D + 1:D + 2], te[:, bass.ds(t, 1)],
                                        xg[:, p, D + 2:D + 3], ALU.is_equal, ALU.mult).then_inc(w_part, 1)
                dve.wait_ge(w_part, t + 1)
                tt(w_col[:, p:p + 1], w_col[:, p:p + 1], xg[:, p, D + 3:D + 4], ALU.add)
                dve.wait_ge(tx_done, t + 1)
                nc.vector.tensor_copy(tok_idx[:, p:p + 1], xg[:, p, D:D + 1].bitcast(U32)).then_inc(meta_ready, 1)

            def weighted(t, p):
                dve.wait_ge(dn_done, t + 1)
                dve.wait_ge(meta_ready, t + 1)
                nc.vector.tensor_scalar(y_d[:, p, :], psum[:, 7, 0:D], w_col[:, p:p + 1], None, ALU.mult).then_inc(y_ready, 1)

            def tile_step(t, p, loads, inner=False):
                hidden_d(t, p, 0)
                hidden_d(t, p, 1)
                route_of(t, p, loads, inner)
                if inner or t >= 1:
                    weighted(t - 1, 1 - p)

            tile_step(0, 0, 1)
            tile_step(1, 1, 1)
            tile_step(2, 0, 2)
            with dve.Fori(1, (NT - 1) // 2) as i:
                tile_step(2 * i + 1, 1, i + 1, inner=True)
                tile_step(2 * i + 2, 0, i + 2, inner=True)
            weighted(NT - 1, 0)


def kernel(**inputs):
    import numpy as np
    import concourse.bacc as bacc
    from concourse.bass_utils import run_bass_kernel_spmd

    nc = bacc.Bacc("TRN2", target_bir_lowering=False, num_devices=1)
    arrays, args = {}, []
    for name in INPUTS:
        a = np.ascontiguousarray(inputs[name])
        arrays[f"in_{name}"] = a
        args.append(nc.dram_tensor(f"in_{name}", a.shape, mybir.dt.from_np(a.dtype), kind="ExternalInput").ap())
    out = nc.dram_tensor("out_x", inputs["x"].shape, mybir.dt.float32, kind="ExternalOutput").ap()
    build(nc, *args, out)
    return run_bass_kernel_spmd(nc, [arrays], core_ids=[0]).results[0]["out_x"]
```

```python
from contextlib import ExitStack

import concourse.bass as bass
from concourse import mybir

INPUTS = ['x', 'ctx_1024', 'L0_xattn_Wq', 'L0_xattn_Wkv', 'L0_xattn_Wout', 'L0_ffn_clip_x', 'L0_ffn_clip_down', 'L0_ffn_w_gate', 'L0_ffn_w_up', 'L0_ffn_w_down', 'L1_xattn_igate_kernel', 'L1_xattn_igate_bias', 'L1_xattn_fgate_kernel', 'L1_xattn_fgate_bias', 'L1_xattn_rms_scale', 'L1_ffn_gate_w', 'L1_ffn_w1', 'L1_ffn_w3', 'L1_ffn_w2']


def build(nc, x, ctx_in, wq, wkv, wout, clip_x, clip_down, w_gate, w_up, w_down, ig_k, ig_b, fg_k, fg_b, rms_scale,
          gate_w, w1, w3, w2, out):
    F32 = mybir.dt.float32
    BF16 = mybir.dt.bfloat16
    I32 = mybir.dt.int32
    U32 = mybir.dt.uint32
    ALU = mybir.AluOpType
    ACT = mybir.ActivationFunctionType
    AX = mybir.AxisListType

    B, S, D = x.shape
    P = 128
    KT = D // P
    H0 = 16
    DH0 = D // H0
    HT = P // DH0
    VW = 32
    LN_EPS = 1e-5
    I0 = w_gate.shape[0]
    IT = -(-I0 // P)
    IR = I0 - (IT - 1) * P
    QMAX = 127.0
    E, _, F1 = w1.shape
    FH = F1 // 2
    TOP = 2
    NT = B * S * TOP // P + E - 1
    ROW = D + 4
    SLOTS = 3
    PART = KT * F1
    SLOT = 2 * 3 * PART
    H1 = ig_k.shape[1]
    DH1 = D // H1
    VC = (H1 - 1) * (DH1 + 1) + 96 + 1
    NEG = -0.7 * 3.4028234663852886e38
    MAGIC = 1.5 * 2.0 ** 23
    G = 4
    GB = B // G
    TB = GB * P
    EARLY = B - 4

    stack = ExitStack()
    with stack:
        def sb(name, shape, dt=F32):
            return stack.enter_context(nc.sbuf_tensor(name, shape, dt))

        def ps(name, shape, dt=F32):
            return stack.enter_context(nc.psum_tensor(name, shape, dt))

        def sem(name):
            return stack.enter_context(nc.semaphore(name))

        def lay(region, *specs):
            at, views = 0, []
            for dt, *shape in specs:
                n = 1
                for s in shape:
                    n *= s
                words = n if dt == F32 else n // 2
                view = region[:, at:at + words]
                if dt != F32:
                    view = view.bitcast(dt)
                names = "abcde"[:len(shape)]
                if len(shape) > 1:
                    view = view.rearrange(f"p ({' '.join(names)}) -> p {' '.join(names)}", **dict(zip(names[1:], shape[1:])))
                views.append(view)
                at += words
            assert at <= region.shape[1], (at, region.shape)
            return views

        x_sb = sb("x_sb", [P, B, D])
        ident = sb("ident", [P, P])
        ident_b = sb("ident_b", [P, P], BF16)
        head_mask = sb("head_mask", [P, HT])
        stats = sb("stats", [P, 2, 6])
        mv = sb("mv", [P, B, 2])
        mv1 = sb("mv1", [P, 2])
        pause = sb("pause", [P, 1])
        pause_p = sb("pause_p", [P, 1])
        pause_a = sb("pause_a", [P, 6])
        pause_d = sb("pause_d", [P, 6])
        one_col = sb("one_col", [P, 1])
        rstd = sb("rstd", [P, B])
        minus_half = sb("minus_half", [P, 64])
        clip = sb("clip", [P, 2])
        w_amax = sb("w_amax", [P, 2 * IT + KT])
        w_scale = sb("w_scale", [P, 2 * IT + KT])
        w_inv = sb("w_inv", [P, 2 * IT + KT])
        gu_scale = sb("gu_scale", [P, 2 * IT])
        wd_diag = sb("wd_diag", [P, KT, P])
        ones_sb = sb("ones_sb", [P, P])
        down_scale = sb("down_scale", [P, D])
        x1_range = sb("x1_range", [P, 2, B])
        amax_h = sb("amax_h", [P, G * IT])
        amax_col = sb("amax_col", [P, 2])
        amax_all = sb("amax_all", [P, 2])
        act_scale = sb("act_scale", [P, 2])
        act_inv = sb("act_inv", [P, 2])
        slots = sb("slots", [P, 2, B], U32)
        tile_info = sb("tile_info", [P, 3, NT], I32)
        tok_idx = sb("tok_idx", [P, 2], U32)
        int_tmp = sb("int_tmp", [P, 64], I32)
        empty_row = sb("empty_row", [P, ROW])
        before = sb("before", [P, P], BF16)
        ones_b = sb("ones_b", [P, P], BF16)
        chosen_b = sb("chosen_b", [P, B, E], BF16)
        gate_sb = sb("gate_sb", [P, KT, E])
        x1_q = sb("x1_q", [P, B, D], BF16)
        sil = sb("sil", [P, 2, TB])
        down_out = sb("down_out", [P, 2, D])

        gk = sb("gk", [P, 3 * KT, 2 * H1])
        gk_ctx = sb("gk_ctx", [P, KT, 2 * H1])
        rms1 = sb("rms1", [P, DH1])
        gbias = sb("gbias", [P, 2])

        region1 = sb("region1", [P, 24500])
        region2 = sb("region2", [P, 18432])

        (wq_sb, wkv_sb, wout_sb, xn, ctx_sb, xcT, qkT, kbd, v_ones, probs, probsT, row_max, outT, rec0, o_sb,
         oT, wgu, wgu_q, wguT, wd, wd_q, wdT, wtmp) = lay(
            region1,
            (F32, KT, D), (F32, KT, 2 * D), (F32, KT, D),
            (F32, 2, D),
            (F32, 2, D),
            (F32, 2, 2 * KT, P),
            (F32, 2, 2 * KT, P),
            (F32, 2, KT, HT, P),
            (F32, 2, H0, VW),
            (F32, KT, HT, P), (F32, KT, HT, P),
            (F32, KT, HT), (F32, 4, P), (F32, H0, 1), (F32, D), (F32, KT, P),
            (F32, 2 * IT, D), (BF16, 2 * IT, D), (BF16, KT, 2 * IT, P),
            (F32, KT, I0), (BF16, KT, I0), (BF16, IT, D), (F32, 8))
        hT, x1n, xq = lay(region2, (F32, IT, B * P), (F32, B, D), (BF16, KT, B * P))
        _, hq = lay(region2, (F32, IT, B * P), (BF16, IT, B * P))

        (ST, neg_max, xn_c, ctx_c, ctxT_c, q_only, v_c, decay, decayed, h_c, h_sq, gates8, lf, gsum, gmax, ga, gtmp,
         aT, floorT, o_rec, ms, ms_rs) = lay(
            region1,
            (F32, B * H1, P), (F32, B * H1, P), (F32, 2, D), (F32, 2, D), (F32, 2, KT, P),
            (F32, 2, H1, P),
            (F32, 2, VC), (F32, 2, H1, P), (F32, 2, H1, P), (F32, 2, H1, DH1), (F32, H1, DH1),
            (F32, 3, P), (F32, P), (F32, P), (F32, P), (F32, P), (F32, 2, P),
            (F32, B * H1), (F32, B * H1), (F32, H1), (F32, 2, H1), (F32, 2, H1))
        gates_all = lay(region2, (F32, B * P))[0]
        gates_dram = nc.dram_tensor("gates_dram", (2, B, H1, P), F32, kind="Internal").ap()
        neg_max_dram = nc.dram_tensor("neg_max_dram", (B * H1, P), F32, kind="Internal").ap()

        (xrow, xT_d, logits, top, oh1, oh2, rt, rt2, rbase, incl, incl2, v1, v2, m12, e2, w12, etiles, eend, eend2, eoff,
         iota_e, iota_t, tcmp, te, tchg, tcum, tslot, slots_f, xg, xT_hi, xT_lo, sil_d, h_d,
         hT_hi, hT_lo, y_d, w_col, stage) = lay(
            region1,
            (F32, B, ROW), (F32, 2, KT, P), (F32, B, E), (F32, B, E), (F32, B, E), (F32, B, E), (F32, B, E),
            (F32, B, E), (F32, B, E), (F32, B, E), (F32, B, E), (F32, B), (F32, B), (F32, 2, B), (F32, B), (F32, 2, B),
            (F32, E), (F32, E), (F32, E), (F32, E), (F32, E), (F32, NT), (F32, NT, E), (F32, NT), (F32, NT), (F32, NT), (F32, NT),
            (F32, 2, B), (F32, 2, ROW), (BF16, 2, KT, P), (BF16, 2, KT, P), (F32, 2, FH), (F32, 2, F1),
            (BF16, F1 // P, P), (BF16, F1 // P, P), (F32, 2, D), (F32, 2),
            (F32, 2, 3, PART))
        expert_w = region2[:, :].bitcast(BF16)
        routed_dram = nc.dram_tensor("routed_dram", (NT * P, ROW), F32, kind="Internal").ap()
        sum_dram = nc.dram_tensor("sum_dram", (B * P + P, D), F32, kind="Internal").ap()

        psum = ps("psum", [P, 8, 512])

        def bank(n, *shape, count=1, dt=F32):
            view = psum[:, n, :] if count == 1 else psum[:, n:n + count, :].rearrange("p n c -> p (n c)")
            if dt != F32:
                view = view.bitcast(dt)
            names = "abcde"[:len(shape)]
            return view.rearrange(f"p ({' '.join(names)}) -> p {' '.join(names)}", **dict(zip(names[1:], shape[1:])))

        bank0 = bank(0, 4, P)
        bank1 = bank(1, 4, P)
        bank2 = psum[:, 2, :]
        S_ps = [bank(3, HT, P, count=2), bank(5, HT, P, count=2)]
        bank7 = bank(7, 4, P)

        w_loaded = sem("w_loaded")
        x_loaded = [sem(f"x_loaded{i}") for i in range(4)]
        ctx_loaded = [sem(f"ctx_loaded{i}") for i in range(2)]
        out_stored = sem("out_stored")
        consts_ready = sem("consts_ready")
        v_preset = sem("v_preset")
        ln_chain = sem("ln_chain")
        rstd1_ready = sem("rstd1_ready")
        xn_ready = sem("xn_ready")
        t1_done = sem("t1_done")
        t1_evac = sem("t1_evac")
        qk_done = sem("qk_done")
        qk_evac = sem("qk_evac")
        v_done = sem("v_done")
        v_evac = sem("v_evac")
        kbd_ready = sem("kbd_ready")
        s_done = sem("s_done")
        max_ready = sem("max_ready")
        shifted_ready = sem("shifted_ready")
        probs_ready = sem("probs_ready")
        pt_done = sem("pt_done")
        pt_evac = sem("pt_evac")
        pv_done = sem("pv_done")
        outT_ready = sem("outT_ready")
        to_done = sem("to_done")
        rec0_ready = sem("rec0_ready")
        o_ready = sem("o_ready")
        ot_done = sem("ot_done")
        oT_ready = sem("oT_ready")
        wo_done = sem("wo_done")
        x1_ready = sem("x1_ready")

        b_chain = sem("b_chain")
        ln2_chain = sem("ln2_chain")
        ln2_eps = sem("ln2_eps")
        rstd2_ready = sem("rstd2_ready")
        fw_loaded = sem("fw_loaded")
        fw_preset = sem("fw_preset")
        clip_loaded = sem("clip_loaded")
        clip_exp = sem("clip_exp")
        wq_ready = sem("wq_ready")
        wT_done = sem("wT_done")
        wT_evac = sem("wT_evac")
        x1_range_step = sem("x1_range_step")
        x1n_step = sem("x1n_step")
        x1_clipped = sem("x1_clipped")
        x1_q_ready = sem("x1_q_ready")
        x1t_done = sem("x1t_done")
        amax_ready = sem("amax_ready")
        amax_all_ready = sem("amax_all_ready")
        xq_ready = sem("xq_ready")
        gate_done = sem("gate_done")
        up_done = sem("up_done")
        sil_ready = sem("sil_ready")
        gu_ready = sem("gu_ready")
        hT_ready = sem("hT_ready")
        amax_h_step = sem("amax_h_step")
        h_clipped = sem("h_clipped")
        hq_ready = sem("hq_ready")
        down_done = sem("down_done")
        down_read = sem("down_read")
        x2_ready = sem("x2_ready")
        ln3_chain = sem("ln3_chain")

        gk_loaded = sem("gk_loaded")
        gk_ready = sem("gk_ready")
        q_preset = sem("q_preset")
        rstd3_ready = sem("rstd3_ready")
        c_chain = sem("c_chain")
        cctx_loaded = [sem(f"cctx_loaded{i}") for i in range(2)]
        xn_c_ready = sem("xn_c_ready")
        ct_done = sem("ct_done")
        ct_evac = sem("ct_evac")
        gates_done = sem("gates_done")
        gates_read = sem("gates_read")
        st_done = sem("st_done")
        st_read = sem("st_read")
        gates_stored = sem("gates_stored")
        gates_loaded = sem("gates_loaded")
        soft_abs = sem("soft_abs")
        soft_log = sem("soft_log")
        neg_max_ready = sem("neg_max_ready")
        neg_max_stored = sem("neg_max_stored")
        neg_max_loaded = [sem(f"neg_max_loaded{i}") for i in range(4)]
        floor_ready = sem("floor_ready")
        a_ready = sem("a_ready")
        aT_done = sem("aT_done")
        aT_ready = sem("aT_ready")
        masked_ready = sem("masked_ready")
        decay_ready = sem("decay_ready")
        decayed_ready = sem("decayed_ready")
        v_c_loaded = [sem(f"v_c_loaded{i}") for i in range(2)]
        pvc_done = sem("pvc_done")
        o_rec_ready = sem("o_rec_ready")
        h_c_ready = sem("h_c_ready")
        h_sq_ready = sem("h_sq_ready")
        ms_ready = sem("ms_ready")
        ms_eps_ready = sem("ms_eps_ready")
        rs_ready = sem("rs_ready")
        scaled_ready = sem("scaled_ready")
        x3_ready = sem("x3_ready")
        ln4_chain = sem("ln4_chain")

        rows_preset = sem("rows_preset")
        rows_emptied = sem("rows_emptied")
        gate_loaded = sem("gate_loaded")
        route_consts = sem("route_consts")
        rstd4_ready = sem("rstd4_ready")
        xrow_ready = sem("xrow_ready")
        dt_done = sem("dt_done")
        dt_evac = sem("dt_evac")
        logits_done = sem("logits_done")
        d_chain = sem("d_chain")
        gap_ready = sem("gap_ready")
        e2_ready = sem("e2_ready")
        chosen_ready = sem("chosen_ready")
        ranks_done = sem("ranks_done")
        route_ready = sem("route_ready")
        info_ready = sem("info_ready")
        routed_stored = sem("routed_stored")
        sum_preset = sem("sum_preset")
        xg_loaded = [sem(f"xg_loaded{i}") for i in range(2)]
        part_loaded = [[sem(f"part_loaded{i}_{p}") for p in range(2)] for i in range(3)]
        part_high = [sem(f"part_high{i}") for i in range(3)]
        part_low = [sem(f"part_low{i}") for i in range(3)]
        tx_done = sem("tx_done")
        xT_high = sem("xT_high")
        xT_low = sem("xT_low")
        gu_done = sem("gu_done")
        sil_d_ready = sem("sil_d_ready")
        h_d_ready = sem("h_d_ready")
        th_done = sem("th_done")
        hT_high = sem("hT_high")
        hT_low = sem("hT_low")
        dn_done = sem("dn_done")
        w_part = sem("w_part")
        meta_ready = sem("meta_ready")
        y_ready = sem("y_ready")
        sum_added = sem("sum_added")
        paused = sem("paused")

        block = stack.enter_context(nc.Block())

        def steps(engine, step):
            step(0, 0)
            with engine.Fori(0, (B - 2) // 2) as i:
                step(2 * i + 1, 1, inner=True)
                step(2 * i + 2, 0, inner=True)
            step(B - 1, 1)

        @block.sync
        def _(sp):
            x_v = x.rearrange("b p d -> p b d")
            sp.dma_start(x_sb[:, 0:4, :], x_v[:, 0:4, :]).then_inc(x_loaded[0], 16)
            sp.dma_start(wq_sb[:], wq.rearrange("(t p) n -> p t n", p=P)).then_inc(w_loaded, 16)
            sp.dma_start(ctx_sb[:, 0, :], ctx_in[0, :, :]).then_inc(ctx_loaded[0], 16)
            sp.dma_start(wkv_sb[:], wkv.rearrange("(t p) n -> p t n", p=P)).then_inc(w_loaded, 16)
            sp.dma_start(ctx_sb[:, 1, :], ctx_in[1, :, :]).then_inc(ctx_loaded[1], 16)
            for i in range(1, 4):
                sp.dma_start(x_sb[:, 4 * i:4 * i + 4, :], x_v[:, 4 * i:4 * i + 4, :]).then_inc(x_loaded[i], 16)
            sp.dma_start(wout_sb[:], wout.rearrange("(t p) n -> p t n", p=P)).then_inc(w_loaded, 16)
            whole = (IT - 1) * P
            for n, w in enumerate((w_gate, w_up)):
                sp.dma_start(wgu[:, n * IT:n * IT + IT - 1, :], w[0:whole, :].rearrange("(t p) d -> p t d", p=P)).then_inc(fw_loaded, 16)
                sp.dma_start(wgu[0:IR, n * IT + IT - 1, :], w[whole:I0, :]).then_inc(fw_loaded, 16)
            sp.dma_start(wd, w_down.rearrange("(t p) i -> p t i", p=P)).then_inc(fw_loaded, 16)
            sp.dma_start(clip[:, 0:1], clip_x.unsqueeze(0).to_broadcast([P, 1])).then_inc(clip_loaded, 16)
            sp.dma_start(clip[:, 1:2], clip_down.unsqueeze(0).to_broadcast([P, 1])).then_inc(clip_loaded, 16)
            for n, w in enumerate((ig_k, fg_k)):
                sp.dma_start(gk[:, :, n * H1:(n + 1) * H1], w.rearrange("(t p) h -> p t h", p=P)).then_inc(gk_loaded, 16)
            sp.dma_start(rms1[:], rms_scale.unsqueeze(0).to_broadcast([P, DH1])).then_inc(gk_loaded, 16)
            for n, w in enumerate((ig_b, fg_b)):
                for b in range(B):
                    sp.dma_start(gbias[b * H1:(b + 1) * H1, n:n + 1], w.unsqueeze(1)).then_inc(gk_loaded, 16)
            sp.wait_ge(rows_preset, 2)
            sp.dma_start(routed_dram.rearrange("(t p) c -> p t c", p=P), empty_row[:].unsqueeze(1).to_broadcast([P, NT, ROW])).then_inc(rows_emptied, 16)
            sp.dma_start(sum_dram[B * P:B * P + P, :], empty_row[:, 0:D]).then_inc(sum_preset, 16)
            sp.dma_start(gate_sb[:], gate_w.rearrange("(t p) e -> p t e", p=P)).then_inc(gate_loaded, 16)
            with sp.Fori(0, B // 2 - 1) as i:
                for p in range(2):
                    sp.wait_ge(t1_done, 2 * i + p + 1)
                    sp.dma_start(ctx_sb[:, p, :], ctx_in[2 * i + (p + 2), :, :]).then_inc(ctx_loaded[p], 16)
            sp.wait_ge(x2_ready, B)
            for b in range(2):
                sp.dma_start(ctx_c[:, b, :], ctx_in[b, :, :]).then_inc(cctx_loaded[b], 16)
            with sp.Fori(0, B // 2 - 1) as i:
                for p in range(2):
                    sp.wait_ge(ct_done, 2 * i + p + 1)
                    sp.dma_start(ctx_c[:, p, :], ctx_in[2 * i + (p + 2), :, :]).then_inc(cctx_loaded[p], 16)
            sp.wait_ge(gates_read, B)
            for n in range(2):
                sp.dma_start(gates_dram[n, :, :, :].rearrange("b h n -> h b n"),
                             gates_all[n * H1:(n + 1) * H1, :].rearrange("h (b n) -> h b n", n=P)).then_inc(gates_stored, 16)
            sp.wait_ge(gates_stored, 32)
            sp.dma_start(gates8[0:B * H1, 0:2, :], gates_dram.rearrange("g b h n -> (b h) g n")).then_inc(gates_loaded, 16)
            v_v = v_c[:, :, 0:H1 * (DH1 + 1)].rearrange("p b (h d) -> p b h d", d=DH1 + 1)

            def load_v(p, b):
                sp.dma_start(v_v[:, p, :, 0:DH1], ctx_in[b, :, :].rearrange("p (h d) -> p h d", d=DH1)).then_inc(v_c_loaded[p], 16)

            load_v(0, 0)
            load_v(1, 1)
            sp.wait_ge(neg_max_ready, 1)
            sp.dma_start(neg_max_dram, ga[0:B * H1, :]).then_inc(neg_max_stored, 16)
            sp.wait_ge(neg_max_stored, 16)
            for g in range(G):
                rows = slice(g * GB * H1, (g + 1) * GB * H1)
                sp.dma_start(neg_max[:, rows, :], neg_max_dram[rows, :].unsqueeze(0).to_broadcast([P, GB * H1, P])).then_inc(neg_max_loaded[g], 16)
            with sp.Fori(0, B // 2 - 1) as i:
                for p in range(2):
                    sp.wait_ge(pvc_done, 2 * i + p + 1)
                    load_v(p, 2 * i + (p + 2))
            sp.wait_ge(x3_ready, B)
            sp.dma_start(sum_dram[0:B * P, :].rearrange("(b p) d -> p b d", p=P), x_sb[:]).then_inc(sum_preset, 16)
            sp.wait_ge(info_ready, 1)

            def load_rows(t, p, inner=False):
                if inner or t >= 2:
                    sp.wait_ge(meta_ready, t - 1)
                    sp.dma_start(xg[:, p, :], routed_dram[bass.ts(t, P), :]).then_inc(xg_loaded[p], 16)
                else:
                    sp.dma_start(xg[:, p, :], routed_dram[t * P:(t + 1) * P, :]).then_inc(xg_loaded[p], 16)

            def load_part(n, t, p, inner=False):
                expert = sp.value_load(tile_info[0:1, 0, bass.ds(t, 1)], min_val=0, max_val=E - 1)
                new = sp.value_load(tile_info[0:1, 2, bass.ds(t, 1)], min_val=0, max_val=1)
                if inner or t >= 2:
                    sp.wait_ge(part_low[n], t - 1)
                w, width = ((w1, F1), (w3, F1), (w2, D))[n]
                sp.dma_start(stage[:, p, n, :].rearrange("p (t f) -> p t f", f=width),
                             w.rearrange("e (t p) f -> p e t f", p=P)[:, bass.ds(expert, 1), :, :].rearrange("p e t f -> p (e t) f"),
                             cond=(new > 0)).then_inc(part_loaded[n][p], 16)

            for t in range(2):
                for n in range(3):
                    load_part(n, t, t)
            sp.wait_ge(routed_stored, 16 * TOP * B)
            load_rows(0, 0)
            load_rows(1, 1)
            for n in range(3):
                load_part(n, 2, 0)
            load_part(0, 3, 1)
            load_part(1, 3, 1)

            def load_step(t, p, inner=False):
                if inner or t + 4 < NT:
                    load_part(0, t + 4, p, inner)
                    load_part(1, t + 4, p, inner)
                if inner or t + 2 < NT:
                    load_rows(t + 2, p, inner)
                if inner or t + 3 < NT:
                    load_part(2, t + 3, 1 - p, inner)

            load_step(0, 0)
            with sp.Fori(0, (NT - 5) // 2) as i:
                load_step(2 * i + 1, 1, inner=True)
                load_step(2 * i + 2, 0, inner=True)
            for t in range(NT - 4, NT):
                load_step(t, t % 2)
            sp.wait_ge(sum_added, 16 * NT)
            sp.dma_start(out.rearrange("b p d -> (b p) d"), sum_dram[0:B * P, :]).then_inc(out_stored, 16)
            sp.wait_ge(out_stored, 16)

        @block.gpsimd
        def _(pool):
            nc.gpsimd.memset(minus_half[:], -0.5).then_inc(consts_ready, 1)
            nc.gpsimd.memset(ident[:], 0.0).then_inc(consts_ready, 1)
            nc.gpsimd.memset(head_mask[:], 1.0).then_inc(consts_ready, 1)
            pool.wait_ge(consts_ready, 3)
            nc.gpsimd.affine_select(out=ident[:], in_=ident[:], compare_op=ALU.not_equal, fill=1.0, base=0,
                                    pattern=[[-1, P]], channel_multiplier=1).then_inc(consts_ready, 1)
            nc.gpsimd.affine_select(out=head_mask[:], in_=head_mask[:], compare_op=ALU.is_ge, fill=0.0, base=0,
                                    pattern=[[-DH0, HT]], channel_multiplier=1).then_inc(consts_ready, 1)
            pool.wait_ge(consts_ready, 5)
            nc.gpsimd.affine_select(out=head_mask[:], in_=head_mask[:], compare_op=ALU.is_ge, fill=0.0, base=DH0 - 1,
                                    pattern=[[DH0, HT]], channel_multiplier=-1).then_inc(consts_ready, 1)
            nc.gpsimd.memset(empty_row[:], 0.0).then_inc(route_consts, 1)
            pool.wait_ge(route_consts, 1)
            nc.gpsimd.iota(empty_row[:, D:D + 1].bitcast(I32), pattern=[[0, 1]], base=B * P, channel_multiplier=1).then_inc(rows_preset, 2)
            nc.gpsimd.memset(v_ones[:], 0.0).then_inc(v_preset, 1)
            pool.wait_ge(v_preset, 1)
            nc.gpsimd.memset(v_ones[:, :, :, DH0:DH0 + 1], 1.0).then_inc(v_preset, 1)
            pool.wait_ge(consts_ready, 6)
            for i in range(4):
                pool.wait_ge(ln_chain, 12 * i + 12)
                nc.gpsimd.tensor_tensor(rstd[:, 4 * i:4 * i + 4], rstd[:, 4 * i:4 * i + 4], minus_half[:, 0:4],
                                        ALU.pow).then_inc(rstd1_ready, 1)

            def mask_k(b, p, inner=False):
                for m in range(KT):
                    pool.wait_ge(qk_evac, b + 1)
                    if inner or b >= 2:
                        pool.wait_ge(s_done, 2 * (b - 2) + m + 1)
                    nc.gpsimd.tensor_tensor(kbd[:, p, m, :, :],
                                            qkT[:, p, KT + m, :].unsqueeze(1).to_broadcast([P, HT, P]),
                                            head_mask[:].unsqueeze(2).to_broadcast([P, HT, P]),
                                            ALU.mult).then_inc(kbd_ready, 1)

            nc.gpsimd.memset(ones_sb[:], 1.0).then_inc(fw_preset, 1)
            nc.gpsimd.memset(one_col[:], 1.0).then_inc(fw_preset, 1)
            nc.gpsimd.tensor_copy(ident_b[:], ident[:]).then_inc(fw_preset, 1)

            mask_k(0, 0)
            mask_k(1, 1)
            with pool.Fori(0, (B - 2) // 2) as i:
                mask_k(2 * i + 2, 0, inner=True)
                mask_k(2 * i + 3, 1, inner=True)

            for n, part in enumerate((slice(0, EARLY), slice(EARLY, B))):
                pool.wait_ge(ln2_eps, n + 1)
                nc.gpsimd.tensor_tensor(rstd[:, part], rstd[:, part], minus_half[:, part], ALU.pow).then_inc(rstd2_ready, 1)

            def max_over_partitions(n):
                pool.wait_ge(amax_ready, n + 1)
                nc.gpsimd.partition_all_reduce(amax_all[:, n:n + 1], amax_col[:, n:n + 1], P, bass.bass_isa.ReduceOp.max).then_inc(amax_all_ready, 1)

            max_over_partitions(0)
            max_over_partitions(1)

            pool.wait_ge(x2_ready, B)
            nc.gpsimd.memset(q_only, 0.0).then_inc(q_preset, 1)
            nc.gpsimd.memset(v_c, 1.0).then_inc(q_preset, 1)
            pool.wait_ge(ln3_chain, 3 * B + 1)
            nc.gpsimd.tensor_tensor(rstd[:], rstd[:], minus_half[:, 0:B], ALU.pow).then_inc(rstd3_ready, 1)

            def causal(b):
                part = neg_max[:, bass.ds(H1 * b, H1), :]
                nc.gpsimd.affine_select(out=part, in_=part, compare_op=ALU.is_ge, fill=NEG, base=0,
                                        pattern=[[0, H1], [1, P]], channel_multiplier=-1).then_inc(masked_ready, 1)

            def mean_square_root(b, p):
                pool.wait_ge(ms_ready, b + 1)
                nc.gpsimd.tensor_scalar(ms_rs[:, p, :], ms[:, p, :], 1e-6, 1.0, ALU.add, ALU.mult).then_inc(ms_eps_ready, 1)
                pool.wait_ge(ms_eps_ready, b + 1)
                nc.gpsimd.tensor_tensor(ms_rs[:, p, :], ms_rs[:, p, :], minus_half[:, 0:H1], ALU.pow).then_inc(rs_ready, 1)

            for b in range(B):
                if b % GB == 0:
                    pool.wait_ge(neg_max_loaded[b // GB], 16)
                causal(b)
            for b in range(B):
                mean_square_root(b, b % 2)

            nc.gpsimd.memset(before[:], 1.0).then_inc(route_consts, 1)
            nc.gpsimd.memset(ones_b[:], 1.0).then_inc(route_consts, 1)
            pool.wait_ge(route_consts, 2)
            nc.gpsimd.affine_select(out=before[:], in_=before[:], compare_op=ALU.is_gt, fill=0.0, base=0,
                                    pattern=[[1, P]], channel_multiplier=-1).then_inc(route_consts, 1)
            pool.wait_ge(ln4_chain, 3 * B + 1)
            nc.gpsimd.tensor_tensor(rstd[:], rstd[:], minus_half[:, 0:B], ALU.pow).then_inc(rstd4_ready, 1)
            nc.gpsimd.iota(int_tmp[:, 0:E], pattern=[[-1, E]], base=E, channel_multiplier=0).then_inc(route_consts, 1)
            nc.gpsimd.iota(int_tmp[:, E:E + NT], pattern=[[1, NT]], base=0, channel_multiplier=0).then_inc(route_consts, 1)
            nc.gpsimd.iota(xrow[:, :, D:D + 1].bitcast(I32), pattern=[[P, B], [0, 1]], base=0, channel_multiplier=1).then_inc(route_consts, 1)
            pool.wait_ge(route_ready, 1)
            pool.wait_ge(rows_emptied, 16)
            for b in range(B):
                for n in range(TOP):
                    pool.indirect_dma_start(routed_dram, bass.IndirectOffsetOnAxis(ap=slots[:, n, b:b + 1], axis=0),
                                            xrow[:, b, :], None).then_inc(routed_stored, 16)
            pool.wait_ge(sum_preset, 32)

            def add_rows(t, p, inner=False):
                pool.wait_ge(y_ready, t + 1)
                if inner or t >= 1:
                    pool.wait_ge(paused, t)
                    pool.wait_ge(sum_added, 16 * t)
                nc.gpsimd.tensor_tensor(pause_p[:], minus_half[:, 0:1], minus_half[:, 0:1], ALU.add).then_inc(paused, 1)
                pool.indirect_dma_start(sum_dram, bass.IndirectOffsetOnAxis(ap=tok_idx[:, p:p + 1], axis=0),
                                        y_d[:, p, :], None, compute_op=ALU.add).then_inc(sum_added, 16)

            add_rows(0, 0)
            with pool.Fori(0, (NT - 1) // 2) as i:
                add_rows(2 * i + 1, 1, inner=True)
                add_rows(2 * i + 2, 0, inner=True)

        @block.tensor
        def _(pe):
            mm = nc.tensor.matmul
            tr = nc.tensor.transpose

            def front_transposes(b, p, loads, inner=False):
                pe.wait_ge(xn_ready, b + 1)
                pe.wait_ge(ctx_loaded[p], 16 * loads)
                if inner or b >= 1:
                    pe.wait_ge(t1_evac, b)
                for k in range(KT):
                    tr(bank0[:, k, :], xn[:, p, k * P:(k + 1) * P], ident[:])
                for k in range(KT):
                    last = tr(bank0[:, KT + k, :], ctx_sb[:, p, k * P:(k + 1) * P], ident[:])
                last.then_inc(t1_done, 1)

            def front_products(b, p, inner=False):
                pe.wait_ge(t1_evac, b + 1)
                if inner or b >= 1:
                    pe.wait_ge(qk_evac, b)
                for m in range(2 * KT):
                    for k in range(KT):
                        w = wq_sb[:, k, m * P:(m + 1) * P] if m < KT else wkv_sb[:, k, (m - KT) * P:(m - KT + 1) * P]
                        last = mm(bank1[:, m, :], w, xcT[:, p, (m // KT) * KT + k, :], start=(k == 0), stop=(k == KT - 1))
                last.then_inc(qk_done, 1)
                if inner or b >= 1:
                    pe.wait_ge(v_evac, b)
                for k in range(KT):
                    last = mm(bank2[:, 0:D], xcT[:, p, KT + k, :], wkv_sb[:, k, D:2 * D], start=(k == 0), stop=(k == KT - 1))
                last.then_inc(v_done, 1)

            def scores(b, p, m, inner=False):
                pe.wait_ge(kbd_ready, 2 * b + m + 1)
                if inner or b >= 1:
                    pe.wait_ge(pt_evac, 2 * (b - 1) + m + 1)
                for c in range(HT // 4):
                    last = mm(S_ps[m][:, 4 * c:4 * c + 4, :], qkT[:, p, m, :], kbd[:, p, m, 4 * c:4 * c + 4, :],
                              start=True, stop=True)
                last.then_inc(s_done, 1)

            def probs_transposes(b, m):
                pe.wait_ge(probs_ready, 2 * b + m + 1)
                for h in range(HT):
                    last = tr(S_ps[m][:, h, :], probs[:, m, h, :], ident[:])
                last.then_inc(pt_done, 1)

            def values(b, p, m, inner=False):
                pe.wait_ge(pt_evac, 2 * b + m + 1)
                if m == 0:
                    pe.wait_ge(v_evac, b + 1)
                    if inner or b >= 1:
                        pe.wait_ge(x1_ready, b)
                for c in range(HT // 4):
                    for q in range(4):
                        h = 4 * c + q
                        last = mm(bank7[VW * q:VW * q + VW, 2 * m + c, :], v_ones[:, p, HT * m + h, :], probsT[:, m, h, :],
                                  start=True, stop=True)
                last.then_inc(pv_done, 1)

            def tail_a(b):
                pe.wait_ge(outT_ready, b + 1)
                for n in range(4):
                    last = tr(bank7[:, n, :], outT[:, n, :], ident[:])
                last.then_inc(to_done, 1)

            def tail_b(b):
                pe.wait_ge(o_ready, b + 1)
                for k in range(KT):
                    last = tr(bank7[:, k, :], o_sb[:, k * P:(k + 1) * P], ident[:])
                last.then_inc(ot_done, 1)

            def tail_c(b):
                pe.wait_ge(oT_ready, b + 1)
                for k in range(KT):
                    last = mm(bank7[:, 0:KT, :], oT[:, k, :], wout_sb[:, k, :], start=(k == 0), stop=(k == KT - 1))
                last.then_inc(wo_done, 1)

            def step(b, p, inner=False, loads=None):
                scores(b, p, 0, inner)
                if inner or b >= 1:
                    tail_a(b - 1)
                if inner or b + 1 < B:
                    front_transposes(b + 1, 1 - p, loads, inner)
                scores(b, p, 1, inner)
                if inner or b >= 1:
                    tail_b(b - 1)
                if inner or b + 1 < B:
                    front_products(b + 1, 1 - p, inner)
                if inner or b >= 1:
                    tail_c(b - 1)
                probs_transposes(b, 0)
                probs_transposes(b, 1)
                values(b, p, 0, inner)
                values(b, p, 1, inner)

            pe.wait_ge(consts_ready, 6)
            front_transposes(0, 0, 1)
            pe.wait_ge(w_loaded, 48)
            front_products(0, 0)
            step(0, 0, loads=1)
            with pe.Fori(0, (B - 2) // 2) as i:
                step(2 * i + 1, 1, inner=True, loads=i + 2)
                step(2 * i + 2, 0, inner=True, loads=i + 2)
            step(B - 1, 1)
            tail_a(B - 1)
            pe.wait_ge(fw_preset, 6)
            pe.wait_ge(wq_ready, 2)
            for n in range(2 * IT):
                for k in range(KT):
                    last = tr(bank(n // 4, 4, KT, P, dt=BF16)[:, n % 4, k, :], wgu_q[:, n, k * P:(k + 1) * P], ident_b[:])
            last.then_inc(wT_done, 1)
            tail_b(B - 1)
            for t in range(IT):
                rows = P if t < IT - 1 else IR
                for k in range(KT):
                    last = tr(bank(3 + t // 4, 4, KT, P, dt=BF16)[0:rows, t % 4, k, :], wd_q[:, k, t * P:t * P + rows], ident_b[:])
            last.then_inc(wT_done, 1)
            for k in range(KT):
                last = mm(bank(5, 4, P)[:, k, :], ones_sb[:], wd_diag[:, k, :], start=True, stop=True)
            last.then_inc(wT_done, 1)
            tail_c(B - 1)

            def group_transposes(g):
                pe.wait_ge(x1_q_ready, g + 1)
                if g >= 2:
                    pe.wait_ge(xq_ready, g - 1)
                for k in range(KT):
                    for j in range(GB):
                        last = tr(bank(6 + g % 2, KT, GB, P, dt=BF16)[:, k, j, :], x1_q[:, g * GB + j, k * P:(k + 1) * P], ident_b[:])
                last.then_inc(x1t_done, 1)

            def gate_up(g, first=False):
                if not first:
                    pe.wait_ge(xq_ready, g + 1)
                for t in range(IT):
                    for n, done, read in ((0, gate_done, sil_ready), (1, up_done, hT_ready)):
                        if not first or t >= 2:
                            pe.wait_ge(read, IT * g + t - 1)
                        for k in range(KT):
                            last = mm(psum[:, 2 * (t % 2) + n, :], wguT[:, k, n * IT + t, :], xq[:, k, bass.ts(g, TB)],
                                      start=(k == 0), stop=(k == KT - 1))
                        last.then_inc(done, 1)
                    if first and t % 2 == 1:
                        group_transposes(t // 2 + 1)

            pe.wait_ge(wT_evac, 3)
            group_transposes(0)
            pe.wait_ge(xq_ready, 1)
            gate_up(0, first=True)
            with pe.Fori(1, G) as g:
                gate_up(g)

            def down(g, first=False):
                pe.wait_ge(hq_ready, g + 1)
                for j in range(GB // 2):
                    if not first:
                        pe.wait_ge(down_read, GB // 2 * g + j - 1)
                    for t in range(IT):
                        last = mm(psum[:, 4 + j % 2, 0:D], hq[:, t, bass.ds(g * (TB // 2) + j * P, P)], wdT[:, t, :],
                                  start=(t == 0), stop=(t == IT - 1))
                    last.then_inc(down_done, 1)

            down(0, first=True)
            with pe.Fori(1, 2 * G) as g:
                down(g)

            def front_c(b, p, loads, inner=False):
                pe.wait_ge(xn_c_ready, b + 1)
                pe.wait_ge(cctx_loaded[p], 16 * loads)
                if inner or b >= 2:
                    pe.wait_ge(ct_evac, 3 * (b - 1))
                for k in range(KT):
                    tr(bank(p, 4, P)[:, k, :], xn_c[:, p, k * P:(k + 1) * P], ident[:])
                for k in range(KT):
                    last = tr(bank(p, 4, P)[:, KT + k, :], ctx_c[:, p, k * P:(k + 1) * P], ident[:])
                last.then_inc(ct_done, 1)

            def gates_and_scores(b, p, inner=False):
                pe.wait_ge(ct_evac, 3 * b + 3)
                if inner or b >= 2:
                    pe.wait_ge(gates_read, b - 1)
                for h in range(H1):
                    mm(psum[0:2 * H1, 2 + p, 0:P], gk[:, h // 2, :], q_only[:, p, h, :], start=(h == 0), stop=False)
                for k in range(KT):
                    last = mm(psum[0:2 * H1, 2 + p, 0:P], gk_ctx[:, k, :], ctxT_c[:, p, k, :], start=False, stop=(k == KT - 1))
                last.then_inc(gates_done, 1)
                if inner or b >= 2:
                    pe.wait_ge(st_read, b - 1)
                for k in range(KT):
                    last = mm(bank(4 + p, H1, P)[:, 2 * k:2 * k + 2, :], ctxT_c[:, p, k, :], q_only[:, p, 2 * k:2 * k + 2, :],
                              start=True, stop=True)
                last.then_inc(st_done, 1)

            pe.wait_ge(gk_ready, 1)
            pe.wait_ge(x2_ready, B)
            front_c(0, 0, 1)
            front_c(1, 1, 1)
            gates_and_scores(0, 0)
            front_c(2, 0, 2)
            gates_and_scores(1, 1)
            with pe.Fori(1, B // 2 - 1) as i:
                front_c(2 * i + 1, 1, i + 1, inner=True)
                gates_and_scores(2 * i, 0, inner=True)
                front_c(2 * i + 2, 0, i + 2, inner=True)
                gates_and_scores(2 * i + 1, 1, inner=True)
            front_c(B - 1, 1, B // 2)
            gates_and_scores(B - 2, 0)
            gates_and_scores(B - 1, 1)

            pe.wait_ge(a_ready, 2)
            tr(psum[:, 6, 0:B * H1], gtmp[0:B * H1, 0, :], ident[0:B * H1, 0:B * H1])
            tr(psum[:, 6, B * H1:2 * B * H1], gtmp[0:B * H1, 1, :], ident[0:B * H1, 0:B * H1]).then_inc(aT_done, 1)

            def values_c(b, p, loads, inner=False):
                pe.wait_ge(decayed_ready, b + 1)
                pe.wait_ge(v_c_loaded[p], 16 * loads)
                if inner or b >= 2:
                    pe.wait_ge(h_c_ready, b - 1)
                for h in range(H1):
                    at = h * (DH1 + 1)
                    last = mm(psum[:, p, at:at + 96], decayed[:, p, h, :], v_c[:, p, at:at + 96], start=True, stop=True)
                last.then_inc(pvc_done, 1)

            values_c(0, 0, 1)
            values_c(1, 1, 1)
            with pe.Fori(0, B // 2 - 1) as i:
                values_c(2 * i + 2, 0, i + 2, inner=True)
                values_c(2 * i + 3, 1, i + 2, inner=True)

            pe.wait_ge(gate_loaded, 16)

            def router_transposes(b):
                pe.wait_ge(xrow_ready, b + 1)
                if b >= 2:
                    pe.wait_ge(dt_evac, b - 1)
                for k in range(KT):
                    last = tr(bank(b % 2, 4, P)[:, k, :], xrow[:, b, k * P:(k + 1) * P], ident[:])
                last.then_inc(dt_done, 1)

            def router_logits(b):
                pe.wait_ge(dt_evac, b + 1)
                for k in range(KT):
                    last = mm(psum[:, 2, b * E:(b + 1) * E], xT_d[:, b % 2, k, :], gate_sb[:, k, :], start=(k == 0), stop=(k == KT - 1))
                last.then_inc(logits_done, 1)

            router_transposes(0)
            for b in range(B):
                if b + 1 < B:
                    router_transposes(b + 1)
                router_logits(b)
            pe.wait_ge(chosen_ready, 1)
            pe.wait_ge(route_consts, 7)
            chosen_v = chosen_b[:].rearrange("p b e -> p (b e)")
            mm(psum[:, 3, 0:B * E], before[:], chosen_v, start=True, stop=True)
            mm(psum[:, 4, 0:B * E], ones_b[:], chosen_v, start=True, stop=True).then_inc(ranks_done, 1)

            def weights_at(place, low, n, at, width):
                return expert_w[:, bass.ds(place + ((3 * low + n) * PART + at), width)]

            PAIRS = ((0, 0), (0, 1), (1, 0))

            def gate_up_half(t, p, f, place, inner=False):
                if inner or t >= 1:
                    pe.wait_ge(h_d_ready, 2 * t + f - 1)
                for n in range(2):
                    if f == 0:
                        pe.wait_ge(part_low[n], t + 1)
                    for i, (k, (xl, wl)) in enumerate((k, pair) for k in range(KT) for pair in PAIRS):
                        last = mm(psum[:, 2 * f + n, :], (xT_lo if xl else xT_hi)[:, p, k, :],
                                  weights_at(place, wl, n, k * F1 + f * FH, FH), start=(i == 0), stop=(i == 3 * KT - 1))
                last.then_inc(gu_done, 1)

            def x_transposes(t, p, loads, inner=False):
                pe.wait_ge(xg_loaded[p], 16 * loads)
                for k in range(KT):
                    last = tr(bank(6, 4, P)[:, k, :], xg[:, p, k * P:(k + 1) * P], ident[:])
                last.then_inc(tx_done, 1)

            def h_transposes(t, p):
                pe.wait_ge(h_d_ready, 2 * t + 2)
                for f in range(F1 // P):
                    last = tr(bank(4, F1 // P, P, count=2)[:, f, :], h_d[:, p, f * P:(f + 1) * P], ident[:])
                last.then_inc(th_done, 1)

            def down_d(t, place, inner=False):
                pe.wait_ge(hT_low, t + 1)
                pe.wait_ge(part_low[2], t + 1)
                if inner or t >= 1:
                    pe.wait_ge(y_ready, t)
                for i, (f, (hl, wl)) in enumerate((f, pair) for f in range(F1 // P) for pair in PAIRS):
                    last = mm(psum[:, 7, 0:D], (hT_lo if hl else hT_hi)[:, f, :], weights_at(place, wl, 2, f * D, D),
                              start=(i == 0), stop=(i == 3 * (F1 // P) - 1))
                last.then_inc(dn_done, 1)

            def place_of(t):
                return pe.value_load(tile_info[0:1, 1, bass.ds(t, 1)], min_val=0, max_val=(SLOTS - 1) * SLOT)

            def tile_step(t, p, loads_next, inner=False):
                place = place_of(t)
                pe.wait_ge(xT_low, t + 1)
                gate_up_half(t, p, 0, place, inner)
                if inner or t >= 1:
                    h_transposes(t - 1, 1 - p)
                gate_up_half(t, p, 1, place, inner)
                if inner or t + 1 < NT:
                    x_transposes(t + 1, 1 - p, loads_next, inner)
                if inner or t >= 1:
                    down_d(t - 1, place_of(t - 1), inner)

            pe.wait_ge(info_ready, 1)
            x_transposes(0, 0, 1)
            tile_step(0, 0, 1)
            with pe.Fori(0, (NT - 3) // 2) as i:
                tile_step(2 * i + 1, 1, i + 2, inner=True)
                tile_step(2 * i + 2, 0, i + 2, inner=True)
            tile_step(NT - 2, 1, NT // 2 + 1)
            tile_step(NT - 1, 0, None)
            h_transposes(NT - 1, 0)
            down_d(NT - 1, place_of(NT - 1))

        @block.scalar
        def _(act):
            act_fn = nc.scalar.activation

            def front(b, p):
                act.wait_ge(t1_done, b + 1)
                act_fn(xcT[:, p, :, :], bank0[:, :, :], ACT.Copy).then_inc(t1_evac, 1)

            def exps(b, m):
                act.wait_ge(shifted_ready, 2 * b + m + 1)
                act_fn(probs[:, m, :, :], probs[:, m, :, :], ACT.Exp, scale=float(DH0) ** -0.5).then_inc(probs_ready, 1)

            def v_copy(b, p):
                act.wait_ge(v_done, b + 1)
                act_fn(v_ones[:, p, :, 0:DH0], bank2[:, 0:D].rearrange("p (h d) -> p h d", d=DH0), ACT.Copy).then_inc(v_evac, 1)

            def probsT_copy(b, m):
                act.wait_ge(pt_done, 2 * b + m + 1)
                act_fn(probsT[:, m, :, :], S_ps[m][:, :, :], ACT.Copy).then_inc(pt_evac, 1)

            def step(b, p, inner=False):
                if inner or b + 1 < B:
                    front(b + 1, 1 - p)
                exps(b, 0)
                if inner or b >= 1:
                    act.wait_ge(ot_done, b)
                    act_fn(oT[:, :, :], bank7[:, 0:KT, :], ACT.Copy).then_inc(oT_ready, 1)
                if inner or b + 1 < B:
                    v_copy(b + 1, 1 - p)
                exps(b, 1)
                probsT_copy(b, 0)
                probsT_copy(b, 1)
                act.wait_ge(pv_done, 2 * b + 2)
                act_fn(outT[:, :, :], bank7[:, :, :], ACT.Copy).then_inc(outT_ready, 1)

            front(0, 0)
            act.wait_ge(v_preset, 2)
            v_copy(0, 0)
            steps(act, step)
            act.wait_ge(ot_done, B)
            act_fn(oT[:, :, :], bank7[:, 0:KT, :], ACT.Copy).then_inc(oT_ready, 1)

            act.wait_ge(clip_loaded, 32)
            act_fn(clip[:], clip[:], ACT.Exp, scale=-1.0).then_inc(clip_exp, 1)
            act.wait_ge(wT_done, 1)
            for q in range(3):
                last = act_fn(wguT[:, :, 4 * q:4 * q + 4, :].rearrange("p k n c -> p n k c"), bank(q, 4, KT, P, dt=BF16), ACT.Copy)
            last.then_inc(wT_evac, 1)
            act.wait_ge(wT_done, 3)
            act.wait_ge(fw_preset, 6)
            act_fn(wdT[:, 0:4, :], bank(3, 4, D, dt=BF16), ACT.Copy)
            act_fn(wdT[:, 4:5, :], bank(4, 4, D, dt=BF16)[:, 0:1, :], ACT.Copy)
            act_fn(wdT[0:IR, 5:6, :], bank(4, 4, D, dt=BF16)[0:IR, 1:2, :], ACT.Copy).then_inc(wT_evac, 1)
            act_fn(down_scale[:], psum[:, 5, 0:D], ACT.Copy).then_inc(wT_evac, 1)

            def round_group(g):
                act.wait_ge(x1_clipped, 2 * g + 2)
                act_fn(x1_q[:, g * GB:(g + 1) * GB, :], x1n[:, g * GB:(g + 1) * GB, :], ACT.Copy, bias=-MAGIC).then_inc(x1_q_ready, 1)

            def group_copy(g):
                act.wait_ge(x1t_done, g + 1)
                act_fn(xq[:, :, g * TB:(g + 1) * TB], bank(6 + g % 2, KT, TB, dt=BF16), ACT.Copy).then_inc(xq_ready, 1)

            round_group(0)
            group_copy(0)
            act.wait_ge(gu_ready, 1)

            def silu(g, first=False):
                for t in range(IT):
                    act.wait_ge(gate_done, IT * g + t + 1)
                    if not first or t >= 2:
                        act.wait_ge(hT_ready, IT * g + t - 1)
                    act_fn(sil[:, t % 2, :], psum[:, 2 * (t % 2), :], ACT.Silu, scale=gu_scale[:, t:t + 1]).then_inc(sil_ready, 1)
                    if first and t % 2 == 0:
                        round_group(t // 2 + 1)
                    elif first:
                        group_copy(t // 2 + 1)

            silu(0, first=True)
            with act.Fori(1, G) as g:
                silu(g)
            with act.Fori(0, 2 * G) as g:
                act.wait_ge(h_clipped, 2 * g + 2)
                act_fn(hq[:, :, bass.ts(g, TB // 2)], hT[:, :, bass.ts(g, TB // 2)], ACT.Copy, bias=-MAGIC).then_inc(hq_ready, 1)

            HALF = P // 2

            def front_c(b, p):
                act.wait_ge(ct_done, b + 1)
                for half in range(2):
                    rows = slice(half * HALF, (half + 1) * HALF)
                    act_fn(q_only[rows, p, half:H1:2, :], bank(p, 4, P)[rows, 0:KT, :], ACT.Copy).then_inc(ct_evac, 1)
                act_fn(ctxT_c[:, p, :, :], bank(p, 4, P)[:, KT:2 * KT, :], ACT.Copy).then_inc(ct_evac, 1)

            act.wait_ge(q_preset, 2)
            front_c(0, 0)
            front_c(1, 1)
            with act.Fori(0, B // 2 - 1) as i:
                for p in range(2):
                    act.wait_ge(st_done, 2 * i + p + 1)
                    front_c(2 * i + (p + 2), p)

            act.wait_ge(soft_abs, 1)
            act_fn(lf[0:B * H1, :], lf[0:B * H1, :], ACT.Exp, scale=-1.0).then_inc(soft_log, 1)
            act.wait_ge(soft_log, 1)
            act_fn(lf[0:B * H1, :], lf[0:B * H1, :], ACT.Ln, bias=one_col[0:B * H1, :]).then_inc(soft_log, 1)
            act.wait_ge(floor_ready, 1)
            act_fn(gtmp[0:B * H1, 1, :], gsum[0:B * H1, :], ACT.Exp, scale=-1.0).then_inc(a_ready, 1)
            act.wait_ge(aT_done, 1)
            act_fn(aT, psum[:, 6, 0:B * H1], ACT.Copy)
            act_fn(floorT, psum[:, 6, B * H1:2 * B * H1], ACT.Copy, bias=1e-6).then_inc(aT_ready, 1)

            def decays(b, p, inner=False):
                act.wait_ge(masked_ready, b + 1)
                if inner or b >= 2:
                    act.wait_ge(decayed_ready, b - 1)
                for h in range(H1):
                    n = H1 * b + h
                    last = act_fn(decay[:, p, h, :], neg_max[:, bass.ds(n, 1), :].rearrange("p o c -> p (o c)"), ACT.Exp,
                                  bias=aT[:, bass.ds(n, 1)])
                last.then_inc(decay_ready, 1)

            def squares(b, p):
                act.wait_ge(h_c_ready, b + 1)
                if not isinstance(b, int) or b >= 1:
                    act.wait_ge(ms_ready, b)
                act_fn(h_sq, h_c[:, p, :, :], ACT.Square, scale=float(DH1) ** -0.5).then_inc(h_sq_ready, 1)

            act.wait_ge(aT_ready, 1)
            decays(0, 0)
            decays(1, 1)
            squares(0, 0)
            with act.Fori(0, B // 2 - 1) as i:
                decays(2 * i + 2, 0, inner=True)
                squares(2 * i + 1, 1)
                decays(2 * i + 3, 1, inner=True)
                squares(2 * i + 2, 0)
            squares(B - 1, 1)

            for b in range(B):
                act.wait_ge(dt_done, b + 1)
                if b >= 2:
                    act.wait_ge(logits_done, b - 1)
                act_fn(xT_d[:, b % 2, :, :], bank(b % 2, 4, P)[:, 0:KT, :], ACT.Copy).then_inc(dt_evac, 1)
            act.wait_ge(gap_ready, 1)
            act_fn(e2, v2, ACT.Exp).then_inc(e2_ready, 1)

            def silu_d(t, f):
                act.wait_ge(gu_done, 2 * t + f + 1)
                act_fn(sil_d[:, f, :], psum[:, 2 * f, :], ACT.Silu).then_inc(sil_d_ready, 1)

            def x_high(t, p):
                act.wait_ge(tx_done, t + 1)
                act_fn(xT_hi[:, p, :, :], bank(6, 4, P)[:, 0:KT, :], ACT.Copy).then_inc(xT_high, 1)

            def h_high(t):
                act.wait_ge(th_done, t + 1)
                act_fn(hT_hi, bank(4, F1 // P, P, count=2), ACT.Copy).then_inc(hT_high, 1)

            def weights_high(n, t, p, loads, inner=False):
                place = act.value_load(tile_info[0:1, 1, bass.ds(t, 1)], min_val=0, max_val=(SLOTS - 1) * SLOT)
                new = act.value_load(tile_info[0:1, 2, bass.ds(t, 1)], min_val=0, max_val=1)
                if inner or t >= 1:
                    act.wait_ge(part_high[n], t)
                act.wait_ge(part_loaded[n][p], 16 * loads)
                act_fn(pause_a[:, 3 + n:4 + n], one_col[:], ACT.Copy)
                with act.If(new > 0):
                    act_fn(expert_w[:, bass.ds(place + n * PART, PART)], stage[:, p, n, :], ACT.Copy)
                act_fn(pause_a[:, n:n + 1], one_col[:], ACT.Copy).then_inc(part_high[n], 1)

            def tile_step(t, p, pair, inner=False):
                silu_d(t, 0)
                if inner or t >= 1:
                    h_high(t - 1)
                if inner or t + 2 < NT:
                    weights_high(0, t + 2, p, pair + 2, inner)
                silu_d(t, 1)
                if inner or t + 1 < NT:
                    x_high(t + 1, 1 - p)
                if inner or t + 2 < NT:
                    weights_high(1, t + 2, p, pair + 2, inner)
                if inner or t + 1 < NT:
                    weights_high(2, t + 1, 1 - p, pair + 1 + p, inner)

            act.wait_ge(info_ready, 1)
            for t in range(2):
                weights_high(0, t, t, 1)
                weights_high(1, t, t, 1)
            weights_high(2, 0, 0, 1)
            x_high(0, 0)
            tile_step(0, 0, 0)
            with act.Fori(0, (NT - 3) // 2) as i:
                tile_step(2 * i + 1, 1, i, inner=True)
                tile_step(2 * i + 2, 0, i + 1, inner=True)
            tile_step(NT - 2, 1, (NT - 2) // 2)
            tile_step(NT - 1, 0, (NT - 1) // 2)
            h_high(NT - 1)

        @block.vector
        def _(dve):
            def row_stats(b, chain):
                nc.vector.bn_stats(stats[:, 0, :], x_sb[:, b, :]).then_inc(ln_chain, 1)
                dve.wait_ge(ln_chain, chain + 1)
                nc.vector.bn_aggr(mv[:, b, :], stats[:, 0, :]).then_inc(ln_chain, 1)
                dve.wait_ge(ln_chain, chain + 2)
                nc.vector.tensor_scalar_add(rstd[:, b:b + 1], mv[:, b, 1:2], LN_EPS).then_inc(ln_chain, 1)

            def norm(b, p, inner=False):
                if inner or b >= 2:
                    dve.wait_ge(t1_done, b - 1)
                nc.vector.tensor_scalar(xn[:, p, :], x_sb[:, b, :], mv[:, b, 0:1], rstd[:, bass.ds(b, 1)] if inner else rstd[:, b:b + 1],
                                        ALU.subtract, ALU.mult).then_inc(xn_ready, 1)

            nc.vector.memset(wgu[IR:P, IT - 1, :], 1.0).then_inc(fw_preset, 1)
            nc.vector.memset(wgu[IR:P, 2 * IT - 1, :], 1.0).then_inc(fw_preset, 1)
            nc.vector.memset(wdT[IR:P, IT - 1, :], 0.0).then_inc(fw_preset, 1)

            for i in range(4):
                dve.wait_ge(x_loaded[i], 16)
                for b in range(4 * i, 4 * i + 4):
                    row_stats(b, 3 * b)
                if i == 0:
                    dve.wait_ge(rstd1_ready, 1)
                    norm(0, 0)
                    norm(1, 1)
            dve.wait_ge(rstd1_ready, 4)

            def qk_copy(b, p):
                dve.wait_ge(qk_done, b + 1)
                nc.vector.tensor_copy(qkT[:, p, :, :], bank1[:, :, :]).then_inc(qk_evac, 1)

            def softmax_shift(b, m):
                dve.wait_ge(s_done, 2 * b + m + 1)
                nc.vector.tensor_reduce(row_max[:, m, :], S_ps[m][:, :, :], AX.X, ALU.max).then_inc(max_ready, 1)
                dve.wait_ge(max_ready, 2 * b + m + 1)
                nc.vector.tensor_tensor(probs[:, m, :, :], S_ps[m][:, :, :],
                                        row_max[:, m, :].unsqueeze(2).to_broadcast([P, HT, P]),
                                        ALU.subtract).then_inc(shifted_ready, 1)

            def tail_norm(b):
                dve.wait_ge(to_done, b + 1)
                o_v = bank7[:, :, :].rearrange("p n (q c) -> p (n q) c", c=VW)
                nc.vector.reciprocal(rec0[:, :, :], o_v[:, :, DH0:DH0 + 1]).then_inc(rec0_ready, 1)
                dve.wait_ge(rec0_ready, b + 1)
                nc.vector.tensor_tensor(o_sb[:].rearrange("p (h d) -> p h d", d=DH0), o_v[:, :, 0:DH0],
                                        rec0[:, :, :].to_broadcast([P, H0, DH0]), ALU.mult).then_inc(o_ready, 1)

            def tail_add(b):
                dve.wait_ge(wo_done, b + 1)
                nc.vector.tensor_tensor(x_sb[:, b, :], x_sb[:, b, :], bank7[:, 0:KT, :].rearrange("p k n -> p (k n)"),
                                        ALU.add).then_inc(x1_ready, 1)
                dve.wait_ge(x1_ready, b + 1)
                token_stats(b, ln2_chain, 3 * b)
                for n, op in enumerate((ALU.max, ALU.min)):
                    nc.vector.tensor_reduce(x1_range[:, n, bass.ds(b, 1)], x_sb[:, b, :], AX.X, op).then_inc(x1_range_step, 1)

            def token_stats(b, chain, n):
                nc.vector.memset(pause[:], 0.0)
                nc.vector.bn_stats(stats[:, 0, :], x_sb[:, b, :]).then_inc(chain, 1)
                dve.wait_ge(chain, n + 1)
                nc.vector.memset(pause[:], 0.0)
                nc.vector.bn_aggr(mv1[:], stats[:, 0, :]).then_inc(chain, 1)
                dve.wait_ge(chain, n + 2)
                nc.vector.tensor_copy(mv[:, b, :], mv1[:]).then_inc(chain, 1)

            def step(b, p, inner=False, late=None):
                softmax_shift(b, 0)
                if inner or b >= 1:
                    tail_norm(b - 1)
                if inner or b + 2 < B:
                    norm(b + 2, p, inner)
                softmax_shift(b, 1)
                if inner or b + 1 < B:
                    qk_copy(b + 1, 1 - p)
                if inner or b >= 1:
                    tail_add(b - 1)
                if late:
                    late()

            counted = [0]

            def link(instruction):
                counted[0] += 1
                instruction.then_inc(b_chain, 1)
                dve.wait_ge(b_chain, counted[0])

            def gate_up_maxima():
                dve.wait_ge(fw_loaded, 80)
                dve.wait_ge(fw_preset, 6)
                nc.vector.tensor_reduce(w_amax[:, 0:2 * IT], wgu, AX.X, ALU.max, apply_absolute_value=True)

            def weight_scales():
                link(nc.vector.tensor_reduce(w_amax[:, 2 * IT:2 * IT + KT], wd, AX.X, ALU.max, apply_absolute_value=True))
                link(nc.vector.tensor_scalar_mul(w_scale[:], w_amax[:], 1.0 / QMAX))
                link(nc.vector.reciprocal(w_inv[:], w_scale[:]))

            def gate_up_scaled():
                for n in range(2 * IT):
                    last = nc.vector.tensor_scalar(wgu[:, n, :], wgu[:, n, :], w_inv[:, n:n + 1], QMAX, ALU.mult, ALU.min)
                link(last)

            def gate_up_shifted():
                link(nc.vector.tensor_scalar(wgu, wgu, -QMAX - 1.0, MAGIC, ALU.max, ALU.add))

            def gate_up_rounded():
                link(nc.vector.tensor_scalar_add(wgu_q, wgu, -MAGIC))
                nc.vector.memset(wgu_q[IR:P, IT - 1, :], 0.0)
                nc.vector.memset(wgu_q[IR:P, 2 * IT - 1, :], 0.0).then_inc(wq_ready, 1)
                dve.wait_ge(ln2_chain, 3 * (B - 2))
                nc.vector.tensor_scalar_add(rstd[:, 0:EARLY], mv[:, 0:EARLY, 1], LN_EPS).then_inc(ln2_eps, 1)

            def down_rounded():
                for k in range(KT):
                    last = nc.vector.tensor_scalar(wd[:, k, :], wd[:, k, :], w_inv[:, 2 * IT + k:2 * IT + k + 1], QMAX, ALU.mult, ALU.min)
                    nc.vector.tensor_scalar(wd_diag[:, k, :], ident[:], w_scale[:, 2 * IT + k:2 * IT + k + 1], None, ALU.mult)
                link(last)
                link(nc.vector.tensor_scalar(wd, wd, -QMAX - 1.0, MAGIC, ALU.max, ALU.add))
                nc.vector.tensor_scalar_add(wd_q, wd, -MAGIC).then_inc(wq_ready, 1)

            def norm_x1(batches):
                for b in batches:
                    nc.vector.tensor_scalar(x1n[:, b, :], x_sb[:, b, :], mv[:, b, 0:1], rstd[:, b:b + 1],
                                            ALU.subtract, ALU.mult).then_inc(x1n_step, 1)

            def early_norms():
                dve.wait_ge(rstd2_ready, 1)
                norm_x1(range(EARLY))

            qk_copy(0, 0)
            step(0, 0)
            rest = (gate_up_maxima, weight_scales, down_rounded, gate_up_scaled, gate_up_shifted, gate_up_rounded, early_norms)
            with dve.Fori(0, (B - 1 - len(rest)) // 2) as i:
                step(2 * i + 1, 1, inner=True)
                step(2 * i + 2, 0, inner=True)
            for b in range(B - len(rest), B):
                step(b, b % 2, late=rest[b - (B - len(rest))])
            tail_norm(B - 1)
            tail_add(B - 1)

            dve.wait_ge(ln2_chain, 3 * B)
            nc.vector.tensor_scalar_add(rstd[:, EARLY:B], mv[:, EARLY:B, 1], LN_EPS).then_inc(ln2_eps, 1)
            dve.wait_ge(clip_exp, 1)
            link(nc.vector.tensor_scalar(clip[:], clip[:], 1.0, QMAX, ALU.add, ALU.mult))
            link(nc.vector.reciprocal(clip[:], clip[:]))

            dve.wait_ge(x1_range_step, 2 * B)
            link(nc.vector.tensor_tensor(x1_range[:], x1_range[:], mv[:, :, 0].unsqueeze(1).to_broadcast([P, 2, B]), ALU.subtract))
            dve.wait_ge(rstd2_ready, 2)
            link(nc.vector.tensor_tensor(x1_range[:], x1_range[:], rstd[:].unsqueeze(1).to_broadcast([P, 2, B]), ALU.mult))

            def activation_scale(n, values, meanwhile=None):
                nc.vector.tensor_reduce(amax_col[:, n:n + 1], values, AX.X, ALU.max, apply_absolute_value=True).then_inc(amax_ready, 1)
                if meanwhile:
                    meanwhile()
                dve.wait_ge(amax_all_ready, n + 1)
                link(nc.vector.tensor_tensor(act_scale[:, n:n + 1], amax_all[:, n:n + 1], clip[:, n:n + 1], ALU.mult))
                link(nc.vector.reciprocal(act_inv[:, n:n + 1], act_scale[:, n:n + 1]))

            activation_scale(0, x1_range[:].rearrange("p n b -> p (n b)"), meanwhile=lambda: norm_x1(range(EARLY, B)))
            nc.vector.tensor_scalar(gu_scale[:], w_scale[:, 0:2 * IT], act_scale[:, 0:1], None, ALU.mult).then_inc(gu_ready, 1)

            def clip_group(g):
                part = x1n[:, g * GB:(g + 1) * GB, :]
                dve.wait_ge(x1n_step, B)
                nc.vector.tensor_scalar(part, part, act_inv[:, 0:1], QMAX, ALU.mult, ALU.min).then_inc(x1_clipped, 1)
                dve.wait_ge(x1_clipped, 2 * g + 1)
                nc.vector.tensor_scalar(part, part, -QMAX - 1.0, MAGIC, ALU.max, ALU.add).then_inc(x1_clipped, 1)

            clip_group(0)
            clip_group(1)

            def hidden(g, first=False):
                for t in range(IT):
                    n = IT * g + t
                    dve.wait_ge(up_done, n + 1)
                    dve.wait_ge(sil_ready, n + 1)
                    part = hT[:, t, bass.ts(g, TB)]
                    nc.vector.scalar_tensor_tensor(out=part, in0=psum[:, 2 * (t % 2) + 1, :],
                                                   scalar=gu_scale[:, IT + t:IT + t + 1], in1=sil[:, t % 2, :],
                                                   op0=ALU.mult, op1=ALU.mult).then_inc(hT_ready, 1)
                    dve.wait_ge(hT_ready, n + 1)
                    nc.vector.tensor_reduce(amax_h[:, bass.ds(n, 1)], part, AX.X, ALU.max,
                                            apply_absolute_value=True).then_inc(amax_h_step, 1)
                    if first and t < G - 2:
                        clip_group(t + 2)

            hidden(0, first=True)
            with dve.Fori(1, G) as g:
                hidden(g)
            dve.wait_ge(amax_h_step, G * IT)
            activation_scale(1, amax_h[:])
            dve.wait_ge(wT_evac, 3)
            link(nc.vector.tensor_scalar(down_scale[:], down_scale[:], act_scale[:, 1:2], None, ALU.mult))

            def round_hidden(g):
                part = hT[:, :, bass.ts(g, TB // 2)]
                nc.vector.tensor_scalar(part, part, act_inv[:, 1:2], QMAX, ALU.mult, ALU.min).then_inc(h_clipped, 1)
                dve.wait_ge(h_clipped, 2 * g + 1)
                nc.vector.tensor_scalar(part, part, -QMAX - 1.0, MAGIC, ALU.max, ALU.add).then_inc(h_clipped, 1)

            def add_down(g):
                for j in range(GB // 2):
                    b = GB // 2 * g + j
                    dve.wait_ge(down_done, b + 1)
                    nc.vector.tensor_tensor(down_out[:, j % 2, :], psum[:, 4 + j % 2, 0:D], down_scale[:], ALU.mult).then_inc(down_read, 1)
                    dve.wait_ge(down_read, b + 1)
                    x_b = x_sb[:, bass.ds(b, 1), :].rearrange("p o d -> p (o d)")
                    nc.vector.tensor_tensor(x_b, x_b, down_out[:, j % 2, :], ALU.add).then_inc(x2_ready, 1)
                    dve.wait_ge(x2_ready, b + 1)
                    token_stats(b, ln3_chain, 3 * b)

            round_hidden(0)
            round_hidden(1)
            with dve.Fori(0, 2 * G - 2) as g:
                round_hidden(g + 2)
                add_down(g)
            add_down(2 * G - 2)
            add_down(2 * G - 1)

            dve.wait_ge(ln3_chain, 3 * B)
            nc.vector.tensor_scalar_add(rstd[:], mv[:, :, 1], LN_EPS).then_inc(ln3_chain, 1)
            dve.wait_ge(gk_loaded, 16 * (3 + 2 * B))
            nc.vector.tensor_tensor(gk_ctx[:], gk[:, KT:2 * KT, :], gk[:, 2 * KT:3 * KT, :], ALU.add).then_inc(gk_ready, 1)
            nc.vector.tensor_scalar_add(rms1[:], rms1[:], 1.0)
            dve.wait_ge(rstd3_ready, 1)

            def norm_c(b, p):
                nc.vector.tensor_scalar(xn_c[:, p, :], x_sb[:, b, :], mv[:, b, 0:1], rstd[:, bass.ds(b, 1)],
                                        ALU.subtract, ALU.mult).then_inc(xn_c_ready, 1)

            def read_gates_and_scores(b, p):
                dve.wait_ge(gates_done, b + 1)
                nc.vector.tensor_copy(gates_all[0:2 * H1, bass.ts(b, P)], psum[0:2 * H1, 2 + p, 0:P]).then_inc(gates_read, 1)
                dve.wait_ge(st_done, b + 1)
                nc.vector.tensor_scalar_mul(ST[:, bass.ds(H1 * b, H1), :], bank(4 + p, H1, P), float(DH1) ** -0.5).then_inc(st_read, 1)

            norm_c(0, 0)
            norm_c(1, 1)
            with dve.Fori(0, B // 2 - 1) as i:
                for p in range(2):
                    dve.wait_ge(ct_done, 2 * i + p + 1)
                    norm_c(2 * i + (p + 2), p)
                    read_gates_and_scores(2 * i + p, p)
            read_gates_and_scores(B - 2, 0)
            read_gates_and_scores(B - 1, 1)

            R = B * H1
            counted = [0]

            def link_c(instruction):
                counted[0] += 1
                instruction.then_inc(c_chain, 1)
                dve.wait_ge(c_chain, counted[0])

            dve.wait_ge(gates_loaded, 16)
            for n in range(2):
                last = nc.vector.tensor_scalar(gates8[0:R, n, :], gates8[0:R, n, :], gbias[0:R, n:n + 1], None, ALU.add)
            link_c(last)
            link_c(nc.vector.tensor_scalar_mul(lf[0:R, :], gates8[0:R, 1, :], -1.0))
            nc.vector.tensor_tensor(lf[0:R, :], lf[0:R, :], gates8[0:R, 1, :], ALU.max).then_inc(soft_abs, 1)
            dve.wait_ge(soft_log, 2)
            link_c(nc.vector.scalar_tensor_tensor(out=lf[0:R, :], in0=gates8[0:R, 1, :], scalar=0.0, in1=lf[0:R, :],
                                                  op0=ALU.min, op1=ALU.subtract))
            link_c(nc.vector.tensor_tensor_scan(gsum[0:R, :], ones_sb[0:R, :], lf[0:R, :], 0.0, ALU.mult, ALU.add))
            nc.vector.tensor_tensor(gtmp[0:R, 0, :], gates8[0:R, 0, :], gsum[0:R, :], ALU.subtract).then_inc(a_ready, 1)
            dve.wait_ge(a_ready, 1)
            link_c(nc.vector.tensor_tensor_scan(gmax[0:R, :], ones_sb[0:R, :], gtmp[0:R, 0, :], NEG, ALU.mult, ALU.max))
            nc.vector.tensor_scalar_mul(ga[0:R, :], gmax[0:R, :], -1.0).then_inc(neg_max_ready, 1)
            nc.vector.tensor_tensor(gsum[0:R, :], gsum[0:R, :], gmax[0:R, :], ALU.add).then_inc(floor_ready, 1)

            def decay_scores(b, p, inner=False):
                dve.wait_ge(decay_ready, b + 1)
                if inner or b >= 2:
                    dve.wait_ge(pvc_done, b - 1)
                nc.vector.tensor_tensor(decayed[:, p, :, :], ST[:, bass.ds(H1 * b, H1), :], decay[:, p, :, :],
                                        ALU.mult).then_inc(decayed_ready, 1)

            def normalise(b, p):
                o_v = psum[:, p, 0:H1 * (DH1 + 1)].rearrange("p (h d) -> p h d", d=DH1 + 1)
                dve.wait_ge(pvc_done, b + 1)
                nc.vector.scalar_tensor_tensor(out=o_rec, in0=o_v[:, :, DH1], scalar=1e-6, in1=floorT[:, bass.ds(H1 * b, H1)],
                                               op0=ALU.add, op1=ALU.max).then_inc(o_rec_ready, 1)
                dve.wait_ge(o_rec_ready, 2 * b + 1)
                nc.vector.reciprocal(o_rec, o_rec).then_inc(o_rec_ready, 1)
                dve.wait_ge(o_rec_ready, 2 * b + 2)
                nc.vector.tensor_tensor(h_c[:, p, :, :], o_v[:, :, 0:DH1], o_rec.unsqueeze(2).to_broadcast([P, H1, DH1]),
                                        ALU.mult).then_inc(h_c_ready, 1)
                dve.wait_ge(h_sq_ready, b + 1)
                nc.vector.tensor_reduce(ms[:, p, :], h_sq, AX.X, ALU.add).then_inc(ms_ready, 1)

            def add_attention(b, p):
                h_v = h_c[:, p, :, :]
                dve.wait_ge(rs_ready, b + 1)
                nc.vector.tensor_tensor(h_v, h_v, ms_rs[:, p, :].unsqueeze(2).to_broadcast([P, H1, DH1]), ALU.mult).then_inc(scaled_ready, 1)
                dve.wait_ge(scaled_ready, 2 * b + 1)
                nc.vector.tensor_tensor(h_v, h_v, rms1[:].unsqueeze(1).to_broadcast([P, H1, DH1]), ALU.mult).then_inc(scaled_ready, 1)
                dve.wait_ge(scaled_ready, 2 * b + 2)
                x_b = x_sb[:, bass.ds(b, 1), :].rearrange("p o d -> p (o d)")
                nc.vector.tensor_tensor(x_b, x_b, h_v.rearrange("p h d -> p (h d)"), ALU.add).then_inc(x3_ready, 1)
                dve.wait_ge(x3_ready, b + 1)
                token_stats(b, ln4_chain, 3 * b)

            decay_scores(0, 0)
            decay_scores(1, 1)
            normalise(0, 0)
            with dve.Fori(0, B // 2 - 1) as i:
                decay_scores(2 * i + 2, 0, inner=True)
                normalise(2 * i + 1, 1)
                add_attention(2 * i, 0)
                decay_scores(2 * i + 3, 1, inner=True)
                normalise(2 * i + 2, 0)
                add_attention(2 * i + 1, 1)
            normalise(B - 1, 1)
            add_attention(B - 2, 0)
            add_attention(B - 1, 1)

            dve.wait_ge(ln4_chain, 3 * B)
            nc.vector.tensor_scalar_add(rstd[:], mv[:, :, 1], LN_EPS).then_inc(ln4_chain, 1)
            dve.wait_ge(rstd4_ready, 1)
            for b in range(B):
                nc.vector.tensor_scalar(xrow[:, b, 0:D], x_sb[:, b, :], mv[:, b, 0:1], rstd[:, b:b + 1],
                                        ALU.subtract, ALU.mult).then_inc(xrow_ready, 1)
            counted_d = [0]

            def link_d(instruction):
                counted_d[0] += 1
                instruction.then_inc(d_chain, 1)
                dve.wait_ge(d_chain, counted_d[0])

            tt = nc.vector.tensor_tensor
            over_e = lambda v: v.unsqueeze(2).to_broadcast([P, B, E])
            over_b = lambda v: v.unsqueeze(1).to_broadcast([P, B, E])
            dve.wait_ge(route_consts, 7)
            nc.vector.tensor_copy(iota_e, int_tmp[:, 0:E])
            link_d(nc.vector.tensor_copy(iota_t, int_tmp[:, E:E + NT]))
            dve.wait_ge(logits_done, B)
            link_d(nc.vector.tensor_copy(logits, psum[:, 2, 0:B * E].rearrange("p (b e) -> p b e", e=E)))
            left = logits
            for n, (value, one_hot) in enumerate(((v1, oh1), (v2, oh2))):
                link_d(nc.vector.tensor_reduce(value, left, AX.X, ALU.max))
                link_d(tt(rt, left, over_e(value), ALU.is_ge))
                link_d(tt(rt, rt, over_b(iota_e), ALU.mult))
                link_d(nc.vector.tensor_reduce(m12[:, n, :], rt, AX.X, ALU.max))
                link_d(tt(one_hot, over_b(iota_e), over_e(m12[:, n, :]), ALU.is_equal))
                if n == 0:
                    link_d(nc.vector.scalar_tensor_tensor(out=top, in0=one_hot, scalar=NEG, in1=left, op0=ALU.mult, op1=ALU.add))
                    left = top
            nc.vector.tensor_tensor(chosen_b[:], oh1, oh2, ALU.add).then_inc(chosen_ready, 1)
            nc.vector.tensor_tensor(v2, v2, v1, ALU.subtract).then_inc(gap_ready, 1)
            dve.wait_ge(e2_ready, 1)
            link_d(nc.vector.tensor_scalar_add(w12[:, 0, :], e2, 1.0))
            link_d(nc.vector.reciprocal(w12[:, 0, :], w12[:, 0, :]))
            link_d(tt(w12[:, 1, :], e2, w12[:, 0, :], ALU.mult))
            col = lambda c: xrow[:, :, D + c]
            nc.vector.tensor_copy(col(1), m12[:, 0, :])
            tt(col(2), w12[:, 0, :], w12[:, 1, :], ALU.subtract)
            nc.vector.tensor_copy(col(3), w12[:, 1, :])
            dve.wait_ge(ranks_done, 1)
            counts = psum[:, 4, 0:B * E].rearrange("p (b e) -> p b e", e=E)
            link_d(nc.vector.tensor_copy(rt, counts))
            src, dst, step_by = rt, incl, 1
            while step_by < B:
                nc.vector.tensor_copy(dst[:, 0:step_by, :], src[:, 0:step_by, :])
                link_d(tt(dst[:, step_by:B, :], src[:, step_by:B, :], src[:, 0:B - step_by, :], ALU.add))
                src, dst = dst, (incl2 if dst is incl else incl)
                step_by *= 2
            link_d(nc.vector.tensor_scalar(etiles, src[:, B - 1, :], P - 1.0, 1.0 / P, ALU.add, ALU.mult))
            link_d(nc.vector.tensor_scalar(etiles, etiles, -(0.5 - 0.25 / P), MAGIC, ALU.add, ALU.add))
            link_d(nc.vector.tensor_scalar_add(etiles, etiles, -MAGIC))
            esrc, edst, step_by = etiles, eend, 1
            while step_by < E:
                nc.vector.tensor_copy(edst[:, 0:step_by], esrc[:, 0:step_by])
                link_d(tt(edst[:, step_by:E], esrc[:, step_by:E], esrc[:, 0:E - step_by], ALU.add))
                esrc, edst = edst, (eend2 if edst is eend else eend)
                step_by *= 2
            link_d(tt(eoff, esrc, etiles, ALU.subtract))
            link_d(nc.vector.tensor_scalar_mul(eoff, eoff, float(P)))
            link_d(tt(rbase, src, rt, ALU.subtract))
            link_d(tt(rbase, rbase, psum[:, 3, 0:B * E].rearrange("p (b e) -> p b e", e=E), ALU.add))
            link_d(tt(rbase, rbase, over_b(eoff), ALU.add))
            for n, one_hot in enumerate((oh1, oh2)):
                link_d(tt(rt2, one_hot, rbase, ALU.mult))
                link_d(nc.vector.tensor_reduce(slots_f[:, n, :], rt2, AX.X, ALU.add))
            nc.vector.tensor_copy(slots[:], slots_f).then_inc(route_ready, 1)
            link_d(tt(tcmp, esrc.unsqueeze(1).to_broadcast([P, NT, E]), iota_t.unsqueeze(2).to_broadcast([P, NT, E]), ALU.is_le))
            link_d(nc.vector.tensor_reduce(te, tcmp, AX.X, ALU.add))
            link_d(nc.vector.tensor_scalar_min(te, te, E - 1.0))
            nc.vector.memset(tchg[:, 0:1], 1.0)
            link_d(tt(tchg[:, 1:NT], te[:, 1:NT], te[:, 0:NT - 1], ALU.not_equal))
            link_d(nc.vector.tensor_tensor_scan(tcum, ones_sb[:, 0:NT], tchg, -1.0, ALU.mult, ALU.add))
            link_d(nc.vector.tensor_scalar(tslot, tcum, 1.0 / SLOTS, -1.0 / SLOTS, ALU.mult, ALU.add))
            link_d(nc.vector.tensor_scalar_add(tslot, tslot, MAGIC))
            link_d(nc.vector.tensor_scalar(tslot, tslot, -MAGIC, -float(SLOTS), ALU.add, ALU.mult))
            link_d(tt(tslot, tslot, tcum, ALU.add))
            link_d(nc.vector.tensor_scalar_mul(tslot, tslot, float(SLOT)))
            nc.vector.tensor_copy(tile_info[:, 0, :], te)
            nc.vector.tensor_copy(tile_info[:, 1, :], tslot)
            link_d(nc.vector.tensor_copy(tile_info[:, 2, :], tchg))
            nc.vector.tensor_scalar(te, te, -1.0, float(E), ALU.mult, ALU.add).then_inc(info_ready, 1)

            def hidden_d(t, p, f):
                dve.wait_ge(gu_done, 2 * t + f + 1)
                dve.wait_ge(sil_d_ready, 2 * t + f + 1)
                tt(h_d[:, p, f * FH:(f + 1) * FH], psum[:, 2 * f + 1, :], sil_d[:, f, :], ALU.mult).then_inc(h_d_ready, 1)

            def route_of(t, p, loads, inner=False):
                dve.wait_ge(xg_loaded[p], 16 * loads)
                if inner or t >= 2:
                    dve.wait_ge(sum_added, 16 * (t - 1))
                nc.vector.tensor_scalar(w_col[:, p:p + 1], xg[:, p, D + 1:D + 2], te[:, bass.ds(t, 1)],
                                        xg[:, p, D + 2:D + 3], ALU.is_equal, ALU.mult).then_inc(w_part, 1)
                dve.wait_ge(w_part, t + 1)
                tt(w_col[:, p:p + 1], w_col[:, p:p + 1], xg[:, p, D + 3:D + 4], ALU.add)
                dve.wait_ge(tx_done, t + 1)
                nc.vector.tensor_copy(tok_idx[:, p:p + 1], xg[:, p, D:D + 1].bitcast(U32)).then_inc(meta_ready, 1)

            def weighted(t, p):
                dve.wait_ge(dn_done, t + 1)
                dve.wait_ge(meta_ready, t + 1)
                nc.vector.tensor_scalar(y_d[:, p, :], psum[:, 7, 0:D], w_col[:, p:p + 1], None, ALU.mult).then_inc(y_ready, 1)

            def x_low(t, p):
                dve.wait_ge(xT_high, t + 1)
                tt(xT_lo[:, p, :, :], bank(6, 4, P)[:, 0:KT, :], xT_hi[:, p, :, :], ALU.subtract).then_inc(xT_low, 1)

            def h_low(t):
                dve.wait_ge(hT_high, t + 1)
                tt(hT_lo, bank(4, F1 // P, P, count=2), hT_hi, ALU.subtract).then_inc(hT_low, 1)

            def weights_low(n, t, p, inner=False):
                place = dve.value_load(tile_info[0:1, 1, bass.ds(t, 1)], min_val=0, max_val=(SLOTS - 1) * SLOT)
                new = dve.value_load(tile_info[0:1, 2, bass.ds(t, 1)], min_val=0, max_val=1)
                if inner or t >= 1:
                    dve.wait_ge(part_low[n], t)
                dve.wait_ge(part_high[n], t + 1)
                nc.vector.memset(pause_d[:, 3 + n:4 + n], 0.0)
                with dve.If(new > 0):
                    tt(expert_w[:, bass.ds(place + (3 + n) * PART, PART)], stage[:, p, n, :],
                       expert_w[:, bass.ds(place + n * PART, PART)], ALU.subtract)
                nc.vector.memset(pause_d[:, n:n + 1], 0.0).then_inc(part_low[n], 1)

            def tile_step(t, p, loads, inner=False):
                hidden_d(t, p, 0)
                if inner or t >= 1:
                    h_low(t - 1)
                if inner or t + 2 < NT:
                    weights_low(0, t + 2, p, inner)
                hidden_d(t, p, 1)
                if inner or t + 1 < NT:
                    x_low(t + 1, 1 - p)
                if inner or t + 2 < NT:
                    weights_low(1, t + 2, p, inner)
                route_of(t, p, loads, inner)
                if inner or t >= 1:
                    weighted(t - 1, 1 - p)
                if inner or t + 1 < NT:
                    weights_low(2, t + 1, 1 - p, inner)

            for t in range(2):
                weights_low(0, t, t)
                weights_low(1, t, t)
            weights_low(2, 0, 0)
            x_low(0, 0)
            tile_step(0, 0, 1)
            tile_step(1, 1, 1)
            tile_step(2, 0, 2)
            with dve.Fori(1, (NT - 3) // 2) as i:
                tile_step(2 * i + 1, 1, i + 1, inner=True)
                tile_step(2 * i + 2, 0, i + 2, inner=True)
            tile_step(NT - 2, 1, NT // 2)
            tile_step(NT - 1, 0, NT // 2 + 1)
            h_low(NT - 1)
            weighted(NT - 1, 0)


def kernel(**inputs):
    import numpy as np
    import concourse.bacc as bacc
    from concourse.bass_utils import run_bass_kernel_spmd

    nc = bacc.Bacc("TRN2", target_bir_lowering=False, num_devices=1)
    arrays, args = {}, []
    for name in INPUTS:
        a = np.ascontiguousarray(inputs[name])
        arrays[f"in_{name}"] = a
        args.append(nc.dram_tensor(f"in_{name}", a.shape, mybir.dt.from_np(a.dtype), kind="ExternalInput").ap())
    out = nc.dram_tensor("out_x", inputs["x"].shape, mybir.dt.float32, kind="ExternalOutput").ap()
    build(nc, *args, out)
    return run_bass_kernel_spmd(nc, [arrays], core_ids=[0]).results[0]["out_x"]
```

```python
from contextlib import ExitStack

import concourse.bass as bass
from concourse import mybir

INPUTS = ['x', 'ctx_1024', 'L0_xattn_Wq', 'L0_xattn_Wkv', 'L0_xattn_Wout', 'L0_ffn_clip_x', 'L0_ffn_clip_down', 'L0_ffn_w_gate', 'L0_ffn_w_up', 'L0_ffn_w_down', 'L1_xattn_igate_kernel', 'L1_xattn_igate_bias', 'L1_xattn_fgate_kernel', 'L1_xattn_fgate_bias', 'L1_xattn_rms_scale', 'L1_ffn_gate_w', 'L1_ffn_w1', 'L1_ffn_w3', 'L1_ffn_w2']


def build(nc, x, ctx_in, wq, wkv, wout, clip_x, clip_down, w_gate, w_up, w_down, ig_k, ig_b, fg_k, fg_b, rms_scale,
          gate_w, w1, w3, w2, out):
    F32 = mybir.dt.float32
    BF16 = mybir.dt.bfloat16
    I32 = mybir.dt.int32
    U32 = mybir.dt.uint32
    ALU = mybir.AluOpType
    ACT = mybir.ActivationFunctionType
    AX = mybir.AxisListType

    B, S, D = x.shape
    P = 128
    KT = D // P
    H0 = 16
    DH0 = D // H0
    HT = P // DH0
    VW = 32
    LN_EPS = 1e-5
    I0 = w_gate.shape[0]
    IT = -(-I0 // P)
    IR = I0 - (IT - 1) * P
    QMAX = 127.0
    E, _, F1 = w1.shape
    FH = F1 // 2
    TOP = 2
    NT = B * S * TOP // P + E - 1
    ROW = D + 4
    SLOTS = 3
    PART = KT * F1
    SLOT = 2 * 3 * PART
    H1 = ig_k.shape[1]
    DH1 = D // H1
    VC = (H1 - 1) * (DH1 + 1) + 96 + 1
    NEG = -0.7 * 3.4028234663852886e38
    MAGIC = 1.5 * 2.0 ** 23
    G = 4
    GB = B // G
    TB = GB * P
    HOT = 4
    PEEL = 4
    EARLY = B - 4

    stack = ExitStack()
    with stack:
        def sb(name, shape, dt=F32):
            return stack.enter_context(nc.sbuf_tensor(name, shape, dt))

        def ps(name, shape, dt=F32):
            return stack.enter_context(nc.psum_tensor(name, shape, dt))

        def sem(name):
            return stack.enter_context(nc.semaphore(name))

        def lay(region, *specs):
            at, views = 0, []
            for dt, *shape in specs:
                n = 1
                for s in shape:
                    n *= s
                words = n if dt == F32 else n // 2
                view = region[:, at:at + words]
                if dt != F32:
                    view = view.bitcast(dt)
                names = "abcde"[:len(shape)]
                if len(shape) > 1:
                    view = view.rearrange(f"p ({' '.join(names)}) -> p {' '.join(names)}", **dict(zip(names[1:], shape[1:])))
                views.append(view)
                at += words
            assert at <= region.shape[1], (at, region.shape)
            return views

        x_sb = sb("x_sb", [P, B, D])
        ident = sb("ident", [P, P])
        ident_b = sb("ident_b", [P, P], BF16)
        head_mask = sb("head_mask", [P, HT])
        stats = sb("stats", [P, 2, 6])
        mv = sb("mv", [P, B, 2])
        mv1 = sb("mv1", [P, 2])
        mv2 = sb("mv2", [P, 2, 2])
        pause = sb("pause", [P, 1])
        pause_p = sb("pause_p", [P, 4])
        pause_a = sb("pause_a", [P, 6])
        pause_d = sb("pause_d", [P, 6])
        one_col = sb("one_col", [P, 1])
        rstd = sb("rstd", [P, B])
        minus_half = sb("minus_half", [P, 64])
        clip = sb("clip", [P, 2])
        w_amax = sb("w_amax", [P, 2 * IT + KT])
        w_scale = sb("w_scale", [P, 2 * IT + KT])
        w_inv = sb("w_inv", [P, 2 * IT + KT])
        gu_scale = sb("gu_scale", [P, 2 * IT])
        wd_diag = sb("wd_diag", [P, KT, P])
        ones_sb = sb("ones_sb", [P, P])
        down_scale = sb("down_scale", [P, D])
        x1_range = sb("x1_range", [P, 2, B])
        amax_h = sb("amax_h", [P, G * IT])
        amax_col = sb("amax_col", [P, 2])
        amax_all = sb("amax_all", [P, 2])
        act_scale = sb("act_scale", [P, 2])
        act_inv = sb("act_inv", [P, 2])
        row_token = sb("row_token", [P, NT], U32)
        next_token = sb("next_token", [P, 2], U32)
        row_token_f = sb("row_token_f", [P, NT])
        row_empty = sb("row_empty", [P, NT])
        place_tile = sb("place_tile", [P, 2, B])
        place_row = sb("place_row", [P, 2, B])
        iota_row = sb("iota_row", [P, P])
        scan_keep = sb("scan_keep", [P, E, B])
        token_p = sb("token_p", [P, 1])
        empty_p = sb("empty_p", [P, 1])
        batch_no = sb("batch_no", [P, B])
        tile_info = sb("tile_info", [P, 3, NT], I32)
        tok_idx = sb("tok_idx", [P, 2], U32)
        int_tmp = sb("int_tmp", [P, E + NT + P + B + 2], I32)
        empty_row = sb("empty_row", [P, ROW])
        before = sb("before", [P, P], BF16)
        ones_b = sb("ones_b", [P, P], BF16)
        chosen_b = sb("chosen_b", [P, B, E], BF16)
        gate_sb = sb("gate_sb", [P, KT, E])
        x1_q = sb("x1_q", [P, B, D], BF16)
        sil = sb("sil", [P, 2, TB])
        down_out = sb("down_out", [P, 2, D])

        gk = sb("gk", [P, 3 * KT, 2 * H1])
        gk_ctx = sb("gk_ctx", [P, KT, 2 * H1])
        rms1 = sb("rms1", [P, DH1])
        gbias = sb("gbias", [P, 2])

        region1 = sb("region1", [P, 24480])
        region2 = sb("region2", [P, 18432])

        (wq_sb, wkv_sb, wout_sb, xn, ctx_sb, xcT, qkT, kbd, v_ones, probs, probsT, row_max, outT, rec0, o_sb,
         oT, wgu, wgu_q, wguT, wd, wd_q, wdT, wtmp) = lay(
            region1,
            (F32, KT, D), (F32, KT, 2 * D), (F32, KT, D),
            (F32, 2, D),
            (F32, 2, D),
            (F32, 2, 2 * KT, P),
            (F32, 2, 2 * KT, P),
            (F32, 2, KT, HT, P),
            (F32, 2, H0, VW),
            (F32, KT, HT, P), (F32, KT, HT, P),
            (F32, KT, HT), (F32, 4, P), (F32, H0, 1), (F32, D), (F32, KT, P),
            (F32, 2 * IT, D), (BF16, 2 * IT, D), (BF16, KT, 2 * IT, P),
            (F32, KT, I0), (BF16, KT, I0), (BF16, IT, D), (F32, 8))
        hT, x1n, xq = lay(region2, (F32, IT, B * P), (F32, B, D), (BF16, KT, B * P))
        _, hq = lay(region2, (F32, IT, B * P), (BF16, IT, B * P))

        (ST, neg_max, xn_c, ctx_c, ctxT_c, q_only, v_c, decay, decayed, h_c, h_sq, gates8, lf, gsum, gmax, ga, gtmp,
         aT, floorT, o_rec, ms, ms_rs) = lay(
            region1,
            (F32, B * H1, P), (F32, B * H1, P), (F32, 2, D), (F32, 2, D), (F32, 2, KT, P),
            (F32, 2, H1, P),
            (F32, 2, VC), (F32, 2, H1, P), (F32, 2, H1, P), (F32, 2, H1, DH1), (F32, H1, DH1),
            (F32, 3, P), (F32, P), (F32, P), (F32, P), (F32, P), (F32, 2, P),
            (F32, B * H1), (F32, B * H1), (F32, H1), (F32, 2, H1), (F32, 2, H1))
        gates_all, qT_c = lay(region2, (F32, B * P), (F32, 2, KT, P))
        gates_dram = nc.dram_tensor("gates_dram", (2, B, H1, P), F32, kind="Internal").ap()
        neg_max_dram = nc.dram_tensor("neg_max_dram", (B * H1, P), F32, kind="Internal").ap()

        (top, oh1, oh2, rt, rt2, rbase, incl, incl2, v1, v2, m12, e2, w12, etiles, eend, eend2, eoff,
         iota_e, iota_t, tcmp, te, tchg, tcum, tslot, slots_f, xg, xT_hi, xT_lo, sil_d, h_d,
         hT_hi, hT_lo, y_d, w_col, stage) = lay(
            region1,
            (F32, B, E), (F32, B, E), (F32, B, E), (F32, B, E),
            (F32, B, E), (F32, B, E), (F32, B, E), (F32, B, E), (F32, B), (F32, B), (F32, 2, B), (F32, B), (F32, 2, B),
            (F32, E), (F32, E), (F32, E), (F32, E), (F32, E), (F32, NT), (F32, NT, E), (F32, NT), (F32, NT), (F32, NT), (F32, NT),
            (F32, 2, B), (F32, 2, ROW), (BF16, 2, KT, P), (BF16, 2, KT, P), (F32, 2, FH), (F32, 2, F1),
            (BF16, F1 // P, P), (BF16, F1 // P, P), (F32, 2, D), (F32, 2),
            (F32, 2, 3, PART))
        xrow, xn_r, xT_r, logits = lay(region2[:, 2 * SLOT // 2:], (F32, B, ROW), (F32, 2, D), (F32, 2, KT, P), (F32, B, E))
        expert_w = region2[:, :].bitcast(BF16)
        xrow_dram = nc.dram_tensor("xrow_dram", (B * P + P, ROW), F32, kind="Internal").ap()
        row_hot = x1_q[:].rearrange("p b (k c) -> p (b k) c", c=P)
        tile_hot = sil[:].rearrange("p n c -> p (n c)").bitcast(BF16)[:, 0:TOP * B * NT].rearrange("p (i t) -> p i t", t=NT)
        tile_num = h_d.rearrange("p n c -> p (n c)").bitcast(BF16)[:, 0:TOP * B * 2 * NT].rearrange("p (i n t) -> p i n t", n=2, t=NT)
        sum_dram = nc.dram_tensor("sum_dram", (B * P + P, D), F32, kind="Internal").ap()

        psum = ps("psum", [P, 8, 512])

        def bank(n, *shape, count=1, dt=F32):
            view = psum[:, n, :] if count == 1 else psum[:, n:n + count, :].rearrange("p n c -> p (n c)")
            if dt != F32:
                view = view.bitcast(dt)
            names = "abcde"[:len(shape)]
            return view.rearrange(f"p ({' '.join(names)}) -> p {' '.join(names)}", **dict(zip(names[1:], shape[1:])))

        bank0 = bank(0, 4, P)
        bank1 = bank(1, 4, P)
        bank2 = psum[:, 2, :]
        S_ps = [bank(3, HT, P, count=2), bank(5, HT, P, count=2)]
        bank7 = bank(7, 4, P)

        w_loaded = sem("w_loaded")
        x_loaded = [sem(f"x_loaded{i}") for i in range(4)]
        ctx_loaded = [sem(f"ctx_loaded{i}") for i in range(2)]
        out_stored = sem("out_stored")
        consts_ready = sem("consts_ready")
        v_preset = sem("v_preset")
        ln_chain = sem("ln_chain")
        rstd1_ready = sem("rstd1_ready")
        xn_ready = sem("xn_ready")
        t1_done = sem("t1_done")
        t1_evac = sem("t1_evac")
        qk_done = sem("qk_done")
        qk_evac = sem("qk_evac")
        v_done = sem("v_done")
        v_evac = sem("v_evac")
        kbd_ready = sem("kbd_ready")
        s_done = sem("s_done")
        max_ready = sem("max_ready")
        shifted_ready = sem("shifted_ready")
        probs_ready = sem("probs_ready")
        pt_done = sem("pt_done")
        pt_evac = sem("pt_evac")
        pv_done = sem("pv_done")
        outT_ready = sem("outT_ready")
        to_done = sem("to_done")
        rec0_ready = sem("rec0_ready")
        o_ready = sem("o_ready")
        ot_done = sem("ot_done")
        oT_ready = sem("oT_ready")
        wo_done = sem("wo_done")
        x1_ready = sem("x1_ready")

        b_chain = sem("b_chain")
        ln2_chain = sem("ln2_chain")
        ln2_eps = sem("ln2_eps")
        rstd2_ready = sem("rstd2_ready")
        fw_loaded = sem("fw_loaded")
        fw_preset = sem("fw_preset")
        clip_exp = sem("clip_exp")
        wq_ready = sem("wq_ready")
        wT_done = sem("wT_done")
        wT_evac = sem("wT_evac")
        x1_range_step = sem("x1_range_step")
        x1n_step = sem("x1n_step")
        x1_clipped = sem("x1_clipped")
        x1_q_ready = sem("x1_q_ready")
        x1t_done = sem("x1t_done")
        amax_ready = sem("amax_ready")
        amax_all_ready = sem("amax_all_ready")
        xq_ready = sem("xq_ready")
        gate_done = sem("gate_done")
        up_done = sem("up_done")
        sil_ready = sem("sil_ready")
        gu_ready = sem("gu_ready")
        hT_ready = sem("hT_ready")
        amax_h_step = sem("amax_h_step")
        h_clipped = sem("h_clipped")
        hq_ready = sem("hq_ready")
        down_done = sem("down_done")
        down_read = sem("down_read")
        x2_ready = sem("x2_ready")
        ln3_chain = sem("ln3_chain")
        ln3_eps = sem("ln3_eps")

        gk_loaded = sem("gk_loaded")
        gk_ready = sem("gk_ready")
        q_preset = sem("q_preset")
        rstd3_ready = sem("rstd3_ready")
        c_chain = sem("c_chain")
        cctx_loaded = [sem(f"cctx_loaded{i}") for i in range(2)]
        xn_c_ready = sem("xn_c_ready")
        ct_done = sem("ct_done")
        ct_evac = sem("ct_evac")
        gates_done = sem("gates_done")
        gates_read = sem("gates_read")
        st_done = sem("st_done")
        st_read = sem("st_read")
        gates_stored = sem("gates_stored")
        gates_loaded = sem("gates_loaded")
        soft_abs = sem("soft_abs")
        soft_log = sem("soft_log")
        neg_max_ready = sem("neg_max_ready")
        neg_max_loaded = [sem(f"neg_max_loaded{i}") for i in range(4)]
        floor_ready = sem("floor_ready")
        a_ready = sem("a_ready")
        aT_done = sem("aT_done")
        aT_ready = sem("aT_ready")
        masked_ready = sem("masked_ready")
        decay_ready = sem("decay_ready")
        decayed_ready = sem("decayed_ready")
        v_c_loaded = [sem(f"v_c_loaded{i}") for i in range(2)]
        pvc_done = sem("pvc_done")
        o_rec_ready = sem("o_rec_ready")
        h_c_ready = sem("h_c_ready")
        h_sq_ready = sem("h_sq_ready")
        ms_ready = sem("ms_ready")
        ms_eps_ready = sem("ms_eps_ready")
        rs_ready = sem("rs_ready")
        scaled_ready = sem("scaled_ready")
        x3_ready = sem("x3_ready")
        ln4_chain = sem("ln4_chain")

        rows_preset = sem("rows_preset")
        rows_stored = sem("rows_stored")
        xrow_routed = sem("xrow_routed")
        hot_ready = sem("hot_ready")
        tokens_placed = sem("tokens_placed")
        route_consts = sem("route_consts")
        rstd4_ready = sem("rstd4_ready")
        xn_r_ready = sem("xn_r_ready")
        dt_done = sem("dt_done")
        dt_evac = sem("dt_evac")
        logits_done = sem("logits_done")
        logits_copied = sem("logits_copied")
        d_chain = sem("d_chain")
        gap_ready = sem("gap_ready")
        e2_ready = sem("e2_ready")
        chosen_ready = sem("chosen_ready")
        ranks_done = sem("ranks_done")
        places_done = sem("places_done")
        info_ready = sem("info_ready")
        xg_loaded = [sem(f"xg_loaded{i}") for i in range(2)]
        part_loaded = [[sem(f"part_loaded{i}_{p}") for p in range(2)] for i in range(3)]
        part_high = [sem(f"part_high{i}") for i in range(3)]
        part_low = [sem(f"part_low{i}") for i in range(3)]
        tx_done = sem("tx_done")
        xT_high = sem("xT_high")
        xT_low = sem("xT_low")
        gu_done = sem("gu_done")
        sil_d_ready = sem("sil_d_ready")
        h_d_ready = sem("h_d_ready")
        th_done = sem("th_done")
        hT_high = sem("hT_high")
        hT_low = sem("hT_low")
        dn_done = sem("dn_done")
        w_part = sem("w_part")
        meta_ready = sem("meta_ready")
        y_ready = sem("y_ready")
        sum_added = sem("sum_added")
        paused = sem("paused")
        paused_gather = sem("paused_gather")

        block = stack.enter_context(nc.Block())

        def steps(engine, step):
            step(0, 0)
            with engine.Fori(0, (B - 2) // 2) as i:
                step(2 * i + 1, 1, inner=True)
                step(2 * i + 2, 0, inner=True)
            step(B - 1, 1)

        @block.sync
        def _(sp):
            x_v = x.rearrange("b p d -> p b d")
            sp.dma_start(x_sb[:, 0:4, :], x_v[:, 0:4, :]).then_inc(x_loaded[0], 16)
            sp.dma_start(wq_sb[:], wq.rearrange("(t p) n -> p t n", p=P)).then_inc(w_loaded, 16)
            sp.dma_start(ctx_sb[:, 0, :], ctx_in[0, :, :]).then_inc(ctx_loaded[0], 16)
            sp.dma_start(wkv_sb[:], wkv.rearrange("(t p) n -> p t n", p=P)).then_inc(w_loaded, 16)
            sp.dma_start(ctx_sb[:, 1, :], ctx_in[1, :, :]).then_inc(ctx_loaded[1], 16)
            for i in range(1, 4):
                sp.dma_start(x_sb[:, 4 * i:4 * i + 4, :], x_v[:, 4 * i:4 * i + 4, :]).then_inc(x_loaded[i], 16)
            sp.dma_start(wout_sb[:], wout.rearrange("(t p) n -> p t n", p=P)).then_inc(w_loaded, 16)
            whole = (IT - 1) * P
            for n, w in enumerate((w_gate, w_up)):
                sp.dma_start(wgu[:, n * IT:n * IT + IT - 1, :], w[0:whole, :].rearrange("(t p) d -> p t d", p=P)).then_inc(fw_loaded, 16)
                sp.dma_start(wgu[0:IR, n * IT + IT - 1, :], w[whole:I0, :]).then_inc(fw_loaded, 16)
            sp.dma_start(wd, w_down.rearrange("(t p) i -> p t i", p=P)).then_inc(fw_loaded, 16)
            sp.dma_start(clip[:, 0:1], clip_x.unsqueeze(0).to_broadcast([P, 1])).then_inc(fw_loaded, 16)
            sp.dma_start(clip[:, 1:2], clip_down.unsqueeze(0).to_broadcast([P, 1])).then_inc(fw_loaded, 16)
            for n, w in enumerate((ig_k, fg_k)):
                sp.dma_start(gk[:, :, n * H1:(n + 1) * H1], w.rearrange("(t p) h -> p t h", p=P)).then_inc(gk_loaded, 16)
            sp.dma_start(rms1[:], rms_scale.unsqueeze(0).to_broadcast([P, DH1])).then_inc(gk_loaded, 16)
            for n, w in enumerate((ig_b, fg_b)):
                for b in range(B):
                    sp.dma_start(gbias[b * H1:(b + 1) * H1, n:n + 1], w.unsqueeze(1)).then_inc(gk_loaded, 16)
            sp.wait_ge(rows_preset, 2)
            sp.dma_start(xrow_dram[B * P:B * P + P, :], empty_row[:]).then_inc(rows_stored, 16)
            sp.dma_start(sum_dram[B * P:B * P + P, :], empty_row[:, 0:D]).then_inc(rows_stored, 16)
            sp.dma_start(gate_sb[:], gate_w.rearrange("(t p) e -> p t e", p=P)).then_inc(gk_loaded, 16)
            with sp.Fori(0, B // 2 - 1) as i:
                for p in range(2):
                    sp.wait_ge(t1_done, 2 * i + p + 1)
                    sp.dma_start(ctx_sb[:, p, :], ctx_in[2 * i + (p + 2), :, :]).then_inc(ctx_loaded[p], 16)
            sp.wait_ge(x2_ready, B // 2)
            for b in range(2):
                sp.dma_start(ctx_c[:, b, :], ctx_in[b, :, :]).then_inc(cctx_loaded[b], 16)
            with sp.Fori(0, B // 2 - 1) as i:
                for p in range(2):
                    sp.wait_ge(ct_done, 2 * i + p + 1)
                    sp.dma_start(ctx_c[:, p, :], ctx_in[2 * i + (p + 2), :, :]).then_inc(cctx_loaded[p], 16)
            sp.wait_ge(gates_read, B)
            for n in range(2):
                sp.dma_start(gates_dram[n, :, :, :].rearrange("b h n -> h b n"),
                             gates_all[n * H1:(n + 1) * H1, :].rearrange("h (b n) -> h b n", n=P)).then_inc(gates_stored, 16)
            sp.wait_ge(gates_stored, 32)
            sp.dma_start(gates8[0:B * H1, 0:2, :], gates_dram.rearrange("g b h n -> (b h) g n")).then_inc(gates_loaded, 16)
            v_v = v_c[:, :, 0:H1 * (DH1 + 1)].rearrange("p b (h d) -> p b h d", d=DH1 + 1)

            def load_v(p, b):
                sp.dma_start(v_v[:, p, :, 0:DH1], ctx_in[b, :, :].rearrange("p (h d) -> p h d", d=DH1)).then_inc(v_c_loaded[p], 16)

            load_v(0, 0)
            load_v(1, 1)
            sp.wait_ge(neg_max_ready, 1)
            sp.dma_start(neg_max_dram, ga[0:B * H1, :]).then_inc(gates_stored, 16)
            sp.wait_ge(gates_stored, 48)
            for g in range(G):
                rows = slice(g * GB * H1, (g + 1) * GB * H1)
                sp.dma_start(neg_max[:, rows, :], neg_max_dram[rows, :].unsqueeze(0).to_broadcast([P, GB * H1, P])).then_inc(neg_max_loaded[g], 16)
            with sp.Fori(0, B // 2 - 1) as i:
                for p in range(2):
                    sp.wait_ge(pvc_done, 2 * i + p + 1)
                    load_v(p, 2 * i + (p + 2))
            sp.wait_ge(x3_ready, B)
            sp.dma_start(sum_dram[0:B * P, :].rearrange("(b p) d -> p b d", p=P), x_sb[:]).then_inc(rows_stored, 16)
            sp.wait_ge(xrow_routed, 1)
            sp.wait_ge(route_consts, 12)
            sp.dma_start(xrow_dram[0:B * P, :].rearrange("(b p) c -> p b c", p=P), xrow).then_inc(rows_stored, 16)
            sp.wait_ge(info_ready, 1)

            def load_part(n, t, p, inner=False):
                expert = sp.value_load(tile_info[0:1, 0, bass.ds(t, 1)], min_val=0, max_val=E - 1)
                new = sp.value_load(tile_info[0:1, 2, bass.ds(t, 1)], min_val=0, max_val=1)
                if inner or t >= 2:
                    sp.wait_ge(part_low[n], t - 1)
                w, width = ((w1, F1), (w3, F1), (w2, D))[n]
                sp.dma_start(stage[:, p, n, :].rearrange("p (t f) -> p t f", f=width),
                             w.rearrange("e (t p) f -> p e t f", p=P)[:, bass.ds(expert, 1), :, :].rearrange("p e t f -> p (e t) f"),
                             cond=(new > 0)).then_inc(part_loaded[n][p], 16)

            for t in range(2):
                for n in range(3):
                    load_part(n, t, t)
            for n in range(3):
                load_part(n, 2, 0)
            load_part(0, 3, 1)
            load_part(1, 3, 1)

            def load_step(t, p, inner=False):
                if inner or t + 4 < NT:
                    load_part(0, t + 4, p, inner)
                    load_part(1, t + 4, p, inner)
                if inner or t + 3 < NT:
                    load_part(2, t + 3, 1 - p, inner)

            load_step(0, 0)
            with sp.Fori(0, (NT - 5) // 2) as i:
                load_step(2 * i + 1, 1, inner=True)
                load_step(2 * i + 2, 0, inner=True)
            for t in range(NT - 4, NT):
                load_step(t, t % 2)
            sp.wait_ge(sum_added, 16 * NT)
            sp.dma_start(out.rearrange("b p d -> (b p) d"), sum_dram[0:B * P, :]).then_inc(out_stored, 16)
            sp.wait_ge(out_stored, 16)

        @block.gpsimd
        def _(pool):
            nc.gpsimd.memset(minus_half[:], -0.5).then_inc(consts_ready, 1)
            nc.gpsimd.memset(ident[:], 0.0).then_inc(consts_ready, 1)
            nc.gpsimd.memset(head_mask[:], 1.0).then_inc(consts_ready, 1)
            pool.wait_ge(consts_ready, 3)
            nc.gpsimd.affine_select(out=ident[:], in_=ident[:], compare_op=ALU.not_equal, fill=1.0, base=0,
                                    pattern=[[-1, P]], channel_multiplier=1).then_inc(consts_ready, 1)
            nc.gpsimd.affine_select(out=head_mask[:], in_=head_mask[:], compare_op=ALU.is_ge, fill=0.0, base=0,
                                    pattern=[[-DH0, HT]], channel_multiplier=1).then_inc(consts_ready, 1)
            pool.wait_ge(consts_ready, 5)
            nc.gpsimd.affine_select(out=head_mask[:], in_=head_mask[:], compare_op=ALU.is_ge, fill=0.0, base=DH0 - 1,
                                    pattern=[[DH0, HT]], channel_multiplier=-1).then_inc(consts_ready, 1)
            nc.gpsimd.memset(empty_row[:], 0.0).then_inc(route_consts, 1)
            pool.wait_ge(route_consts, 1)
            nc.gpsimd.iota(empty_row[:, D:D + 1].bitcast(I32), pattern=[[0, 1]], base=B * P, channel_multiplier=1).then_inc(rows_preset, 2)
            nc.gpsimd.memset(v_ones[:], 0.0).then_inc(v_preset, 1)
            pool.wait_ge(v_preset, 1)
            nc.gpsimd.memset(v_ones[:, :, :, DH0:DH0 + 1], 1.0).then_inc(v_preset, 1)
            pool.wait_ge(consts_ready, 6)
            for i in range(4):
                pool.wait_ge(ln_chain, 12 * i + 12)
                nc.gpsimd.tensor_tensor(rstd[:, 4 * i:4 * i + 4], rstd[:, 4 * i:4 * i + 4], minus_half[:, 0:4],
                                        ALU.pow).then_inc(rstd1_ready, 1)

            def mask_k(b, p, inner=False):
                for m in range(KT):
                    pool.wait_ge(qk_evac, b + 1)
                    if inner or b >= 2:
                        pool.wait_ge(s_done, 2 * (b - 2) + m + 1)
                    nc.gpsimd.tensor_tensor(kbd[:, p, m, :, :],
                                            qkT[:, p, KT + m, :].unsqueeze(1).to_broadcast([P, HT, P]),
                                            head_mask[:].unsqueeze(2).to_broadcast([P, HT, P]),
                                            ALU.mult).then_inc(kbd_ready, 1)

            nc.gpsimd.memset(ones_sb[:], 1.0).then_inc(fw_preset, 1)
            nc.gpsimd.memset(one_col[:], 1.0).then_inc(fw_preset, 1)
            nc.gpsimd.tensor_copy(ident_b[:], ident[:]).then_inc(fw_preset, 1)

            mask_k(0, 0)
            mask_k(1, 1)
            with pool.Fori(0, (B - 2) // 2) as i:
                mask_k(2 * i + 2, 0, inner=True)
                mask_k(2 * i + 3, 1, inner=True)

            for n, part in enumerate((slice(0, EARLY), slice(EARLY, B))):
                pool.wait_ge(ln2_eps, n + 1)
                nc.gpsimd.tensor_tensor(rstd[:, part], rstd[:, part], minus_half[:, part], ALU.pow).then_inc(rstd2_ready, 1)

            def max_over_partitions(n):
                pool.wait_ge(amax_ready, n + 1)
                nc.gpsimd.partition_all_reduce(amax_all[:, n:n + 1], amax_col[:, n:n + 1], P, bass.bass_isa.ReduceOp.max).then_inc(amax_all_ready, 1)

            max_over_partitions(0)
            max_over_partitions(1)

            for n, part in enumerate((slice(0, EARLY), slice(EARLY, B))):
                pool.wait_ge(ln3_eps, n + 1)
                nc.gpsimd.tensor_tensor(rstd[:, part], rstd[:, part], minus_half[:, part], ALU.pow).then_inc(rstd3_ready, 1)
            pool.wait_ge(x2_ready, B // 2)
            nc.gpsimd.memset(q_only, 0.0).then_inc(q_preset, 1)
            nc.gpsimd.memset(v_c, 1.0).then_inc(q_preset, 1)

            def causal(b):
                part = neg_max[:, bass.ds(H1 * b, H1), :]
                nc.gpsimd.affine_select(out=part, in_=part, compare_op=ALU.is_ge, fill=NEG, base=0,
                                        pattern=[[0, H1], [1, P]], channel_multiplier=-1).then_inc(masked_ready, 1)

            def mean_square_root(b, p):
                pool.wait_ge(ms_ready, b + 1)
                nc.gpsimd.tensor_scalar(ms_rs[:, p, :], ms[:, p, :], 1e-6, 1.0, ALU.add, ALU.mult).then_inc(ms_eps_ready, 1)
                pool.wait_ge(ms_eps_ready, b + 1)
                nc.gpsimd.tensor_tensor(ms_rs[:, p, :], ms_rs[:, p, :], minus_half[:, 0:H1], ALU.pow).then_inc(rs_ready, 1)

            for b in range(B):
                if b % GB == 0:
                    pool.wait_ge(neg_max_loaded[b // GB], 16)
                causal(b)
            def router_rstd(b):
                pool.wait_ge(ln4_chain, 4 * b + 4)
                nc.gpsimd.tensor_tensor(rstd[:, b:b + 1], rstd[:, b:b + 1], minus_half[:, 0:1], ALU.pow).then_inc(rstd4_ready, 1)

            for b in range(B):
                mean_square_root(b, b % 2)
                if b >= 1:
                    router_rstd(b - 1)
            router_rstd(B - 1)

            nc.gpsimd.memset(scan_keep[:], 1.0).then_inc(route_consts, 1)
            nc.gpsimd.memset(before[:], 1.0).then_inc(route_consts, 1)
            nc.gpsimd.memset(ones_b[:], 1.0).then_inc(route_consts, 1)
            pool.wait_ge(route_consts, 4)
            nc.gpsimd.memset(scan_keep[:, :, 0:1], 0.0).then_inc(route_consts, 1)
            nc.gpsimd.affine_select(out=before[:], in_=before[:], compare_op=ALU.is_gt, fill=0.0, base=0,
                                    pattern=[[1, P]], channel_multiplier=-1).then_inc(route_consts, 1)
            nc.gpsimd.iota(int_tmp[:, 0:E], pattern=[[-1, E]], base=E, channel_multiplier=0).then_inc(route_consts, 1)
            nc.gpsimd.iota(int_tmp[:, E:E + NT], pattern=[[1, NT]], base=0, channel_multiplier=0).then_inc(route_consts, 1)
            at = E + NT
            nc.gpsimd.iota(int_tmp[:, at:at + P], pattern=[[1, P]], base=0, channel_multiplier=0).then_inc(route_consts, 1)
            at += P
            nc.gpsimd.iota(int_tmp[:, at:at + B], pattern=[[1, B]], base=1, channel_multiplier=0).then_inc(route_consts, 1)
            at += B
            nc.gpsimd.iota(int_tmp[:, at:at + 2], pattern=[[B * P + P, 2]], base=0, channel_multiplier=1).then_inc(route_consts, 1)
            nc.gpsimd.iota(xrow[:, :, D:D + 1].bitcast(I32), pattern=[[P, B], [0, 1]], base=0, channel_multiplier=1).then_inc(route_consts, 1)
            def gather_rows(t, p, inner=False):
                if inner or t >= 2:
                    if inner or t >= 3:
                        pool.wait_ge(paused_gather, t - 2)
                    pool.wait_ge(meta_ready, t - 1)
                    nc.gpsimd.tensor_tensor(pause_p[:, 1:2], minus_half[:, 0:1], minus_half[:, 0:1], ALU.add).then_inc(paused_gather, 1)
                pool.indirect_dma_start(xg[:, p, :], None, xrow_dram,
                                        bass.IndirectOffsetOnAxis(ap=next_token[:, p:p + 1], axis=0)).then_inc(xg_loaded[p], 16)

            def add_rows(t, p, inner=False):
                pool.wait_ge(y_ready, t + 1)
                if inner or t >= 1:
                    pool.wait_ge(paused, t)
                    pool.wait_ge(sum_added, 16 * t)
                nc.gpsimd.tensor_tensor(pause_p[:, 0:1], minus_half[:, 0:1], minus_half[:, 0:1], ALU.add).then_inc(paused, 1)
                pool.indirect_dma_start(sum_dram, bass.IndirectOffsetOnAxis(ap=tok_idx[:, p:p + 1], axis=0),
                                        y_d[:, p, :], None, compute_op=ALU.add).then_inc(sum_added, 16)

            pool.wait_ge(tokens_placed, 1)
            pool.wait_ge(rows_stored, 64)
            gather_rows(0, 0)
            gather_rows(1, 1)

            def weights_low(t, p, inner=False):
                place = pool.value_load(tile_info[0:1, 1, bass.ds(t, 1)], min_val=0, max_val=(SLOTS - 1) * SLOT)
                new = pool.value_load(tile_info[0:1, 2, bass.ds(t, 1)], min_val=0, max_val=1)
                pool.wait_ge(part_low[0], t)
                pool.wait_ge(part_high[0], t + 1)
                nc.gpsimd.tensor_tensor(pause_p[:, 2:3], minus_half[:, 0:1], minus_half[:, 0:1], ALU.add)
                with pool.If(new > 0):
                    nc.gpsimd.tensor_tensor(expert_w[:, bass.ds(place + 3 * PART, PART)], stage[:, p, 0, :],
                                            expert_w[:, bass.ds(place, PART)], ALU.subtract)
                nc.gpsimd.tensor_tensor(pause_p[:, 3:4], minus_half[:, 0:1], minus_half[:, 0:1], ALU.add).then_inc(part_low[0], 1)

            def step_d(t, p, inner=False):
                gather_rows(t + 2, p, inner)
                if inner or t >= 1:
                    add_rows(t - 1, 1 - p, inner)
                weights_low(t + 2, p, inner)

            pool.wait_ge(info_ready, 1)
            for t in range(3):
                step_d(t, t % 2)
            with pool.Fori(1, (NT - 3) // 2) as i:
                step_d(2 * i + 1, 1, inner=True)
                step_d(2 * i + 2, 0, inner=True)
            for t in range(NT - 3, NT):
                add_rows(t, t % 2)

        @block.tensor
        def _(pe):
            mm = nc.tensor.matmul
            tr = nc.tensor.transpose

            def front_transposes(b, p, loads, inner=False):
                pe.wait_ge(xn_ready, b + 1)
                pe.wait_ge(ctx_loaded[p], 16 * loads)
                if inner or b >= 1:
                    pe.wait_ge(t1_evac, b)
                for k in range(KT):
                    tr(bank0[:, k, :], xn[:, p, k * P:(k + 1) * P], ident[:])
                for k in range(KT):
                    last = tr(bank0[:, KT + k, :], ctx_sb[:, p, k * P:(k + 1) * P], ident[:])
                last.then_inc(t1_done, 1)

            def front_products(b, p, inner=False):
                pe.wait_ge(t1_evac, b + 1)
                if inner or b >= 1:
                    pe.wait_ge(qk_evac, b)
                for m in range(2 * KT):
                    for k in range(KT):
                        w = wq_sb[:, k, m * P:(m + 1) * P] if m < KT else wkv_sb[:, k, (m - KT) * P:(m - KT + 1) * P]
                        last = mm(bank1[:, m, :], w, xcT[:, p, (m // KT) * KT + k, :], start=(k == 0), stop=(k == KT - 1))
                last.then_inc(qk_done, 1)
                if inner or b >= 1:
                    pe.wait_ge(v_evac, b)
                for k in range(KT):
                    last = mm(bank2[:, 0:D], xcT[:, p, KT + k, :], wkv_sb[:, k, D:2 * D], start=(k == 0), stop=(k == KT - 1))
                last.then_inc(v_done, 1)

            def scores(b, p, m, inner=False):
                pe.wait_ge(kbd_ready, 2 * b + m + 1)
                if inner or b >= 1:
                    pe.wait_ge(pt_evac, 2 * (b - 1) + m + 1)
                for c in range(HT // 4):
                    last = mm(S_ps[m][:, 4 * c:4 * c + 4, :], qkT[:, p, m, :], kbd[:, p, m, 4 * c:4 * c + 4, :],
                              start=True, stop=True)
                last.then_inc(s_done, 1)

            def probs_transposes(b, m):
                pe.wait_ge(probs_ready, 2 * b + m + 1)
                for h in range(HT):
                    last = tr(S_ps[m][:, h, :], probs[:, m, h, :], ident[:])
                last.then_inc(pt_done, 1)

            def values(b, p, m, inner=False):
                pe.wait_ge(pt_evac, 2 * b + m + 1)
                if m == 0:
                    pe.wait_ge(v_evac, b + 1)
                    if inner or b >= 1:
                        pe.wait_ge(x1_ready, b)
                for c in range(HT // 4):
                    for q in range(4):
                        h = 4 * c + q
                        last = mm(bank7[VW * q:VW * q + VW, 2 * m + c, :], v_ones[:, p, HT * m + h, :], probsT[:, m, h, :],
                                  start=True, stop=True)
                last.then_inc(pv_done, 1)

            def tail_a(b):
                pe.wait_ge(outT_ready, b + 1)
                for n in range(4):
                    last = tr(bank7[:, n, :], outT[:, n, :], ident[:])
                last.then_inc(to_done, 1)

            def tail_b(b):
                pe.wait_ge(o_ready, b + 1)
                for k in range(KT):
                    last = tr(bank7[:, k, :], o_sb[:, k * P:(k + 1) * P], ident[:])
                last.then_inc(ot_done, 1)

            def tail_c(b):
                pe.wait_ge(oT_ready, b + 1)
                for k in range(KT):
                    last = mm(bank7[:, 0:KT, :], oT[:, k, :], wout_sb[:, k, :], start=(k == 0), stop=(k == KT - 1))
                last.then_inc(wo_done, 1)

            def step(b, p, inner=False, loads=None):
                scores(b, p, 0, inner)
                if inner or b >= 1:
                    values(b - 1, 1 - p, 1, inner)
                if inner or b + 1 < B:
                    front_transposes(b + 1, 1 - p, loads, inner)
                scores(b, p, 1, inner)
                if inner or b >= 1:
                    tail_a(b - 1)
                if inner or b + 1 < B:
                    front_products(b + 1, 1 - p, inner)
                if inner or b >= 1:
                    tail_b(b - 1)
                probs_transposes(b, 0)
                if inner or b >= 1:
                    tail_c(b - 1)
                probs_transposes(b, 1)
                values(b, p, 0, inner)

            pe.wait_ge(consts_ready, 6)
            front_transposes(0, 0, 1)
            pe.wait_ge(w_loaded, 48)
            front_products(0, 0)
            step(0, 0, loads=1)
            with pe.Fori(0, (B - 2) // 2) as i:
                step(2 * i + 1, 1, inner=True, loads=i + 2)
                step(2 * i + 2, 0, inner=True, loads=i + 2)
            step(B - 1, 1)
            values(B - 1, 1, 1)
            tail_a(B - 1)
            pe.wait_ge(fw_preset, 6)
            pe.wait_ge(wq_ready, 2)
            for n in range(2 * IT):
                for k in range(KT):
                    last = tr(bank(n // 4, 4, KT, P, dt=BF16)[:, n % 4, k, :], wgu_q[:, n, k * P:(k + 1) * P], ident_b[:])
            last.then_inc(wT_done, 1)
            tail_b(B - 1)
            for t in range(IT):
                rows = P if t < IT - 1 else IR
                for k in range(KT):
                    last = tr(bank(3 + t // 4, 4, KT, P, dt=BF16)[0:rows, t % 4, k, :], wd_q[:, k, t * P:t * P + rows], ident_b[:])
            last.then_inc(wT_done, 1)
            for k in range(KT):
                last = mm(bank(5, 4, P)[:, k, :], ones_sb[:], wd_diag[:, k, :], start=True, stop=True)
            last.then_inc(wT_done, 1)
            tail_c(B - 1)

            def group_transposes(g):
                pe.wait_ge(x1_q_ready, g + 1)
                if g >= 2:
                    pe.wait_ge(xq_ready, g - 1)
                for k in range(KT):
                    for j in range(GB):
                        last = tr(bank(6 + g % 2, KT, GB, P, dt=BF16)[:, k, j, :], x1_q[:, g * GB + j, k * P:(k + 1) * P], ident_b[:])
                last.then_inc(x1t_done, 1)

            def gate_up(g, first=False):
                if not first:
                    pe.wait_ge(xq_ready, g + 1)
                for t in range(IT):
                    for n, done, read in ((0, gate_done, sil_ready), (1, up_done, hT_ready)):
                        if not first or t >= 2:
                            pe.wait_ge(read, IT * g + t - 1)
                        for k in range(KT):
                            last = mm(psum[:, 2 * (t % 2) + n, :], wguT[:, k, n * IT + t, :], xq[:, k, bass.ts(g, TB)],
                                      start=(k == 0), stop=(k == KT - 1))
                        last.then_inc(done, 1)
                    if first and t % 2 == 1:
                        group_transposes(t // 2 + 1)

            pe.wait_ge(wT_evac, 3)
            group_transposes(0)
            pe.wait_ge(xq_ready, 1)
            gate_up(0, first=True)
            with pe.Fori(1, G) as g:
                gate_up(g)

            def down(g, first=False):
                for q in range(2):
                    pe.wait_ge(hq_ready, 2 * g + q + 1)
                    if not first:
                        pe.wait_ge(down_read, 2 * g + q - 1)
                    for j in range(GB // 2):
                        for t in range(IT):
                            last = mm(bank(4 + q, 2, D)[:, j, :], hq[:, t, bass.ds(g * TB + (q * GB // 2 + j) * P, P)], wdT[:, t, :],
                                      start=(t == 0), stop=(t == IT - 1))
                    last.then_inc(down_done, 1)

            down(0, first=True)
            with pe.Fori(1, G) as g:
                down(g)

            def front_c(b, p, loads, inner=False):
                pe.wait_ge(xn_c_ready, b + 1)
                pe.wait_ge(cctx_loaded[p], 16 * loads)
                if inner or b >= 2:
                    pe.wait_ge(ct_evac, 3 * (b - 1))
                for k in range(KT):
                    tr(bank(p, 4, P)[:, k, :], xn_c[:, p, k * P:(k + 1) * P], ident[:])
                for k in range(KT):
                    last = tr(bank(p, 4, P)[:, KT + k, :], ctx_c[:, p, k * P:(k + 1) * P], ident[:])
                last.then_inc(ct_done, 1)

            def gates_and_scores(b, p, inner=False):
                pe.wait_ge(ct_evac, 3 * b + 3)
                if inner or b >= 2:
                    pe.wait_ge(gates_read, b - 1)
                for k in range(KT):
                    mm(psum[0:2 * H1, 2 + p, 0:P], gk[:, k, :], qT_c[:, p, k, :], start=(k == 0), stop=False)
                for k in range(KT):
                    last = mm(psum[0:2 * H1, 2 + p, 0:P], gk_ctx[:, k, :], ctxT_c[:, p, k, :], start=False, stop=(k == KT - 1))
                last.then_inc(gates_done, 1)
                if inner or b >= 2:
                    pe.wait_ge(st_read, b - 1)
                for k in range(KT):
                    last = mm(bank(4 + p, H1, P)[:, 2 * k:2 * k + 2, :], ctxT_c[:, p, k, :], q_only[:, p, 2 * k:2 * k + 2, :],
                              start=True, stop=True)
                last.then_inc(st_done, 1)

            pe.wait_ge(gk_ready, 1)
            pe.wait_ge(x2_ready, B // 2)
            front_c(0, 0, 1)
            front_c(1, 1, 1)
            gates_and_scores(0, 0)
            front_c(2, 0, 2)
            gates_and_scores(1, 1)
            with pe.Fori(1, B // 2 - 1) as i:
                front_c(2 * i + 1, 1, i + 1, inner=True)
                gates_and_scores(2 * i, 0, inner=True)
                front_c(2 * i + 2, 0, i + 2, inner=True)
                gates_and_scores(2 * i + 1, 1, inner=True)
            front_c(B - 1, 1, B // 2)
            gates_and_scores(B - 2, 0)
            gates_and_scores(B - 1, 1)

            pe.wait_ge(a_ready, 2)
            tr(psum[:, 6, 0:B * H1], gtmp[0:B * H1, 0, :], ident[0:B * H1, 0:B * H1])
            tr(psum[:, 6, B * H1:2 * B * H1], gtmp[0:B * H1, 1, :], ident[0:B * H1, 0:B * H1]).then_inc(aT_done, 1)

            def values_c(b, p, loads, inner=False):
                pe.wait_ge(decayed_ready, b + 1)
                pe.wait_ge(v_c_loaded[p], 16 * loads)
                if inner or b >= 2:
                    pe.wait_ge(h_c_ready, b - 1)
                for h in range(H1):
                    at = h * (DH1 + 1)
                    last = mm(psum[:, p, at:at + 96], decayed[:, p, h, :], v_c[:, p, at:at + 96], start=True, stop=True)
                last.then_inc(pvc_done, 1)

            def router_transposes(b, p, inner=False):
                pe.wait_ge(xn_r_ready, b + 1)
                if inner or b >= 2:
                    pe.wait_ge(dt_evac, b - 1)
                for k in range(KT):
                    last = tr(bank(2 + p, 4, P)[:, k, :], xn_r[:, p, k * P:(k + 1) * P], ident[:])
                last.then_inc(dt_done, 1)

            def router_logits(b, p, inner=False):
                pe.wait_ge(dt_evac, b + 1)
                if inner or b >= 2:
                    pe.wait_ge(logits_copied, b - 1)
                for k in range(KT):
                    last = mm(psum[:, 4 + p, 0:E], xT_r[:, p, k, :], gate_sb[:, k, :], start=(k == 0), stop=(k == KT - 1))
                last.then_inc(logits_done, 1)

            def step_c(b, p, loads=None, inner=False):
                if inner or 0 <= b - 2 < B:
                    router_transposes(b - 2, p, inner)
                if inner or 0 <= b - 3 < B:
                    router_logits(b - 3, 1 - p, inner)
                if inner or b + 2 < B:
                    values_c(b + 2, p, loads, inner)

            pe.wait_ge(gk_loaded, 16 * (4 + 2 * B))
            values_c(0, 0, 1)
            values_c(1, 1, 1)
            for b in range(PEEL):
                step_c(b, b % 2, loads=b // 2 + 2)
            with pe.Fori(PEEL // 2, B // 2 - 1) as i:
                for p in range(2):
                    step_c(2 * i + p, p, loads=i + 2, inner=True)
            for b in range(B - 2, B + 3):
                step_c(b, b % 2)
            pe.wait_ge(chosen_ready, 1)
            pe.wait_ge(route_consts, 12)
            chosen_v = chosen_b[:].rearrange("p b e -> p (b e)")
            mm(psum[:, 3, 0:B * E], before[:], chosen_v, start=True, stop=True)
            mm(psum[:, 4, 0:B * E], ones_b[:], chosen_v, start=True, stop=True).then_inc(ranks_done, 1)
            for i in range(TOP * B):
                if i % (TOP * B // HOT) == 0:
                    pe.wait_ge(hot_ready, i // (TOP * B // HOT) + 1)
                last = mm(psum[:, 5, 0:2 * NT], row_hot[:, i, :], tile_num[:, i, :, :].rearrange("p n t -> p (n t)"),
                          start=(i == 0), stop=(i == TOP * B - 1))
            last.then_inc(places_done, 1)

            def weights_at(place, low, n, at, width):
                return expert_w[:, bass.ds(place + ((3 * low + n) * PART + at), width)]

            PAIRS = ((0, 0), (0, 1), (1, 0))

            def gate_up_half(t, p, f, place, inner=False):
                if inner or t >= 1:
                    pe.wait_ge(h_d_ready, 2 * t + f - 1)
                for n in range(2):
                    if f == 0:
                        pe.wait_ge(part_low[n], t + 1)
                    for i, (k, (xl, wl)) in enumerate((k, pair) for k in range(KT) for pair in PAIRS):
                        last = mm(psum[:, 2 * f + n, :], (xT_lo if xl else xT_hi)[:, p, k, :],
                                  weights_at(place, wl, n, k * F1 + f * FH, FH), start=(i == 0), stop=(i == 3 * KT - 1))
                last.then_inc(gu_done, 1)

            def x_transposes(t, p, loads, inner=False):
                pe.wait_ge(xg_loaded[p], 16 * loads)
                for k in range(KT):
                    last = tr(bank(6, 4, P)[:, k, :], xg[:, p, k * P:(k + 1) * P], ident[:])
                last.then_inc(tx_done, 1)

            def h_transposes(t, p):
                pe.wait_ge(h_d_ready, 2 * t + 2)
                for f in range(F1 // P):
                    last = tr(bank(4, F1 // P, P, count=2)[:, f, :], h_d[:, p, f * P:(f + 1) * P], ident[:])
                last.then_inc(th_done, 1)

            def down_d(t, place, inner=False):
                pe.wait_ge(hT_low, t + 1)
                pe.wait_ge(part_low[2], t + 1)
                if inner or t >= 1:
                    pe.wait_ge(y_ready, t)
                for i, (f, (hl, wl)) in enumerate((f, pair) for f in range(F1 // P) for pair in PAIRS):
                    last = mm(psum[:, 7, 0:D], (hT_lo if hl else hT_hi)[:, f, :], weights_at(place, wl, 2, f * D, D),
                              start=(i == 0), stop=(i == 3 * (F1 // P) - 1))
                last.then_inc(dn_done, 1)

            def place_of(t):
                return pe.value_load(tile_info[0:1, 1, bass.ds(t, 1)], min_val=0, max_val=(SLOTS - 1) * SLOT)

            def tile_step(t, p, loads_next, inner=False):
                place = place_of(t)
                pe.wait_ge(xT_low, t + 1)
                gate_up_half(t, p, 0, place, inner)
                if inner or t >= 1:
                    h_transposes(t - 1, 1 - p)
                if not inner and t == 0:
                    x_transposes(1, 1, loads_next)
                gate_up_half(t, p, 1, place, inner)
                if inner or 0 < t < NT - 1:
                    x_transposes(t + 1, 1 - p, loads_next, inner)
                if inner or t >= 1:
                    down_d(t - 1, place_of(t - 1), inner)

            pe.wait_ge(info_ready, 1)
            x_transposes(0, 0, 1)
            tile_step(0, 0, 1)
            with pe.Fori(0, (NT - 3) // 4) as i:
                for n in range(2):
                    tile_step(4 * i + (2 * n + 1), 1, 2 * i + (n + 2), inner=True)
                    tile_step(4 * i + (2 * n + 2), 0, 2 * i + (n + 2), inner=True)
            tile_step(NT - 2, 1, NT // 2 + 1)
            tile_step(NT - 1, 0, None)
            h_transposes(NT - 1, 0)
            down_d(NT - 1, place_of(NT - 1))

        @block.scalar
        def _(act):
            act_fn = nc.scalar.activation

            def front(b, p):
                act.wait_ge(t1_done, b + 1)
                act_fn(xcT[:, p, :, :], bank0[:, :, :], ACT.Copy).then_inc(t1_evac, 1)

            def exps(b, m):
                act.wait_ge(shifted_ready, 2 * b + m + 1)
                act_fn(probs[:, m, :, :], probs[:, m, :, :], ACT.Exp, scale=float(DH0) ** -0.5).then_inc(probs_ready, 1)

            def v_copy(b, p):
                act.wait_ge(v_done, b + 1)
                act_fn(v_ones[:, p, :, 0:DH0], bank2[:, 0:D].rearrange("p (h d) -> p h d", d=DH0), ACT.Copy).then_inc(v_evac, 1)

            def probsT_copy(b, m):
                act.wait_ge(pt_done, 2 * b + m + 1)
                act_fn(probsT[:, m, :, :], S_ps[m][:, :, :], ACT.Copy).then_inc(pt_evac, 1)

            def outT_copy(b):
                act.wait_ge(pv_done, 2 * b + 2)
                act_fn(outT[:, :, :], bank7[:, :, :], ACT.Copy).then_inc(outT_ready, 1)

            def step(b, p, inner=False):
                if inner or b >= 1:
                    outT_copy(b - 1)
                if inner or b + 1 < B:
                    front(b + 1, 1 - p)
                exps(b, 0)
                if inner or b + 1 < B:
                    v_copy(b + 1, 1 - p)
                if inner or b >= 1:
                    act.wait_ge(ot_done, b)
                    act_fn(oT[:, :, :], bank7[:, 0:KT, :], ACT.Copy).then_inc(oT_ready, 1)
                exps(b, 1)
                probsT_copy(b, 0)
                probsT_copy(b, 1)

            front(0, 0)
            act.wait_ge(v_preset, 2)
            v_copy(0, 0)
            steps(act, step)
            outT_copy(B - 1)
            act.wait_ge(ot_done, B)
            act_fn(oT[:, :, :], bank7[:, 0:KT, :], ACT.Copy).then_inc(oT_ready, 1)

            act.wait_ge(fw_loaded, 112)
            act_fn(clip[:], clip[:], ACT.Exp, scale=-1.0).then_inc(clip_exp, 1)
            act.wait_ge(wT_done, 1)
            for q in range(3):
                last = act_fn(wguT[:, :, 4 * q:4 * q + 4, :].rearrange("p k n c -> p n k c"), bank(q, 4, KT, P, dt=BF16), ACT.Copy)
            last.then_inc(wT_evac, 1)
            act.wait_ge(wT_done, 3)
            act.wait_ge(fw_preset, 6)
            act_fn(wdT[:, 0:4, :], bank(3, 4, D, dt=BF16), ACT.Copy)
            act_fn(wdT[:, 4:5, :], bank(4, 4, D, dt=BF16)[:, 0:1, :], ACT.Copy)
            act_fn(wdT[0:IR, 5:6, :], bank(4, 4, D, dt=BF16)[0:IR, 1:2, :], ACT.Copy).then_inc(wT_evac, 1)
            act_fn(down_scale[:], psum[:, 5, 0:D], ACT.Copy).then_inc(wT_evac, 1)

            def round_group(g):
                act.wait_ge(x1_clipped, 2 * g + 2)
                act_fn(x1_q[:, g * GB:(g + 1) * GB, :], x1n[:, g * GB:(g + 1) * GB, :], ACT.Copy, bias=-MAGIC).then_inc(x1_q_ready, 1)

            def group_copy(g):
                act.wait_ge(x1t_done, g + 1)
                act_fn(xq[:, :, g * TB:(g + 1) * TB], bank(6 + g % 2, KT, TB, dt=BF16), ACT.Copy).then_inc(xq_ready, 1)

            round_group(0)
            group_copy(0)
            act.wait_ge(gu_ready, 1)

            def silu(g, first=False):
                for t in range(IT):
                    act.wait_ge(gate_done, IT * g + t + 1)
                    if not first or t >= 2:
                        act.wait_ge(hT_ready, IT * g + t - 1)
                    act_fn(sil[:, t % 2, :], psum[:, 2 * (t % 2), :], ACT.Silu, scale=gu_scale[:, t:t + 1]).then_inc(sil_ready, 1)
                    if first and t % 2 == 0:
                        round_group(t // 2 + 1)
                    elif first:
                        group_copy(t // 2 + 1)

            silu(0, first=True)
            with act.Fori(1, G) as g:
                silu(g)
            with act.Fori(0, 2 * G) as g:
                act.wait_ge(h_clipped, 2 * g + 2)
                act_fn(hq[:, :, bass.ts(g, TB // 2)], hT[:, :, bass.ts(g, TB // 2)], ACT.Copy, bias=-MAGIC).then_inc(hq_ready, 1)

            HALF = P // 2

            def front_c(b, p):
                act.wait_ge(ct_done, b + 1)
                for half in range(2):
                    rows = slice(half * HALF, (half + 1) * HALF)
                    act_fn(q_only[rows, p, half:H1:2, :], bank(p, 4, P)[rows, 0:KT, :], ACT.Copy).then_inc(ct_evac, 1)
                act_fn(qT_c[:, p, :, :], bank(p, 4, P)[:, 0:KT, :], ACT.Copy)
                act_fn(ctxT_c[:, p, :, :], bank(p, 4, P)[:, KT:2 * KT, :], ACT.Copy).then_inc(ct_evac, 1)

            act.wait_ge(q_preset, 2)
            front_c(0, 0)
            front_c(1, 1)
            with act.Fori(0, B // 2 - 1) as i:
                for p in range(2):
                    act.wait_ge(st_done, 2 * i + p + 1)
                    front_c(2 * i + (p + 2), p)

            act.wait_ge(soft_abs, 1)
            act_fn(lf[0:B * H1, :], lf[0:B * H1, :], ACT.Exp, scale=-1.0).then_inc(soft_log, 1)
            act.wait_ge(soft_log, 1)
            act_fn(lf[0:B * H1, :], lf[0:B * H1, :], ACT.Ln, bias=one_col[0:B * H1, :]).then_inc(soft_log, 1)
            act.wait_ge(floor_ready, 1)
            act_fn(gtmp[0:B * H1, 1, :], gsum[0:B * H1, :], ACT.Exp, scale=-1.0).then_inc(a_ready, 1)
            act.wait_ge(aT_done, 1)
            act_fn(aT, psum[:, 6, 0:B * H1], ACT.Copy)
            act_fn(floorT, psum[:, 6, B * H1:2 * B * H1], ACT.Copy, bias=1e-6).then_inc(aT_ready, 1)

            def decays(b, p, inner=False):
                act.wait_ge(masked_ready, b + 1)
                if inner or b >= 2:
                    act.wait_ge(decayed_ready, b - 1)
                for h in range(H1):
                    n = H1 * b + h
                    last = act_fn(decay[:, p, h, :], neg_max[:, bass.ds(n, 1), :].rearrange("p o c -> p (o c)"), ACT.Exp,
                                  bias=aT[:, bass.ds(n, 1)])
                last.then_inc(decay_ready, 1)

            def squares(b, p):
                act.wait_ge(h_c_ready, b + 1)
                if not isinstance(b, int) or b >= 1:
                    act.wait_ge(ms_ready, b)
                act_fn(h_sq, h_c[:, p, :, :], ACT.Square, scale=float(DH1) ** -0.5).then_inc(h_sq_ready, 1)

            def router_copies(b, p, inner=False):
                act.wait_ge(dt_done, b + 1)
                if inner or b >= 2:
                    act.wait_ge(logits_done, b - 1)
                act_fn(xT_r[:, p, :, :], bank(2 + p, 4, P)[:, 0:KT, :], ACT.Copy)
                act_fn(xrow[:, bass.ds(b, 1), 0:D].rearrange("p o d -> p (o d)"), xn_r[:, p, :], ACT.Copy).then_inc(dt_evac, 1)

            def logits_copy(b, p):
                act.wait_ge(logits_done, b + 1)
                act_fn(logits[:, bass.ds(b, 1), :].rearrange("p o e -> p (o e)"), psum[:, 4 + p, 0:E], ACT.Copy).then_inc(logits_copied, 1)

            def step_c(b, p, inner=False):
                if inner or b + 2 < B:
                    decays(b + 2, p, inner)
                if inner or b + 1 < B:
                    squares(b + 1, 1 - p)
                if inner or 0 <= b - 2 < B:
                    router_copies(b - 2, p, inner)
                if inner or 0 <= b - 3 < B:
                    logits_copy(b - 3, 1 - p)

            act.wait_ge(aT_ready, 1)
            decays(0, 0)
            decays(1, 1)
            squares(0, 0)
            for b in range(PEEL):
                step_c(b, b % 2)
            with act.Fori(PEEL // 2, B // 2 - 1) as i:
                for p in range(2):
                    step_c(2 * i + p, p, inner=True)
            for b in range(B - 2, B + 3):
                step_c(b, b % 2)

            act.wait_ge(gap_ready, 1)
            act_fn(e2, v2, ACT.Exp).then_inc(e2_ready, 1)

            def silu_d(t, f):
                act.wait_ge(gu_done, 2 * t + f + 1)
                act_fn(sil_d[:, f, :], psum[:, 2 * f, :], ACT.Silu).then_inc(sil_d_ready, 1)

            def x_high(t, p):
                act.wait_ge(tx_done, t + 1)
                act_fn(xT_hi[:, p, :, :], bank(6, 4, P)[:, 0:KT, :], ACT.Copy).then_inc(xT_high, 1)

            def h_high(t):
                act.wait_ge(th_done, t + 1)
                act_fn(hT_hi, bank(4, F1 // P, P, count=2), ACT.Copy).then_inc(hT_high, 1)

            def weights_high(n, t, p, loads, inner=False):
                place = act.value_load(tile_info[0:1, 1, bass.ds(t, 1)], min_val=0, max_val=(SLOTS - 1) * SLOT)
                new = act.value_load(tile_info[0:1, 2, bass.ds(t, 1)], min_val=0, max_val=1)
                if inner or t >= 1:
                    act.wait_ge(part_high[n], t)
                act.wait_ge(part_loaded[n][p], 16 * loads)
                act_fn(pause_a[:, 3 + n:4 + n], one_col[:], ACT.Copy)
                with act.If(new > 0):
                    act_fn(expert_w[:, bass.ds(place + n * PART, PART)], stage[:, p, n, :], ACT.Copy)
                act_fn(pause_a[:, n:n + 1], one_col[:], ACT.Copy).then_inc(part_high[n], 1)

            def tile_step(t, p, pair, inner=False):
                silu_d(t, 0)
                if inner or t >= 1:
                    h_high(t - 1)
                if inner or t + 2 < NT:
                    weights_high(0, t + 2, p, pair + 2, inner)
                if not inner and t == 0:
                    x_high(1, 1)
                silu_d(t, 1)
                if inner or 0 < t < NT - 1:
                    x_high(t + 1, 1 - p)
                if inner or t + 2 < NT:
                    weights_high(1, t + 2, p, pair + 2, inner)
                if inner or t + 1 < NT:
                    weights_high(2, t + 1, 1 - p, pair + 1 + p, inner)

            act.wait_ge(info_ready, 1)
            weights_high(0, 0, 0, 1)
            weights_high(1, 0, 0, 1)
            x_high(0, 0)
            weights_high(2, 0, 0, 1)
            weights_high(0, 1, 1, 1)
            weights_high(1, 1, 1, 1)
            tile_step(0, 0, 0)
            with act.Fori(0, (NT - 3) // 2) as i:
                tile_step(2 * i + 1, 1, i, inner=True)
                tile_step(2 * i + 2, 0, i + 1, inner=True)
            tile_step(NT - 2, 1, (NT - 2) // 2)
            tile_step(NT - 1, 0, (NT - 1) // 2)
            h_high(NT - 1)

        @block.vector
        def _(dve):
            def row_stats(b, chain):
                nc.vector.bn_stats(stats[:, 0, :], x_sb[:, b, :]).then_inc(ln_chain, 1)
                dve.wait_ge(ln_chain, chain + 1)
                nc.vector.bn_aggr(mv[:, b, :], stats[:, 0, :]).then_inc(ln_chain, 1)
                dve.wait_ge(ln_chain, chain + 2)
                nc.vector.tensor_scalar_add(rstd[:, b:b + 1], mv[:, b, 1:2], LN_EPS).then_inc(ln_chain, 1)

            def norm(b, p, inner=False):
                if inner or b >= 2:
                    dve.wait_ge(t1_done, b - 1)
                nc.vector.tensor_scalar(xn[:, p, :], x_sb[:, b, :], mv[:, b, 0:1], rstd[:, bass.ds(b, 1)] if inner else rstd[:, b:b + 1],
                                        ALU.subtract, ALU.mult).then_inc(xn_ready, 1)

            nc.vector.memset(wgu[IR:P, IT - 1, :], 1.0).then_inc(fw_preset, 1)
            nc.vector.memset(wgu[IR:P, 2 * IT - 1, :], 1.0).then_inc(fw_preset, 1)
            nc.vector.memset(wdT[IR:P, IT - 1, :], 0.0).then_inc(fw_preset, 1)

            for i in range(4):
                dve.wait_ge(x_loaded[i], 16)
                for b in range(4 * i, 4 * i + 4):
                    row_stats(b, 3 * b)
                if i == 0:
                    dve.wait_ge(rstd1_ready, 1)
                    norm(0, 0)
                    norm(1, 1)
            dve.wait_ge(rstd1_ready, 4)

            def qk_copy(b, p):
                dve.wait_ge(qk_done, b + 1)
                nc.vector.tensor_copy(qkT[:, p, :, :], bank1[:, :, :]).then_inc(qk_evac, 1)

            def softmax_shift(b, m):
                dve.wait_ge(s_done, 2 * b + m + 1)
                nc.vector.tensor_reduce(row_max[:, m, :], S_ps[m][:, :, :], AX.X, ALU.max).then_inc(max_ready, 1)
                dve.wait_ge(max_ready, 2 * b + m + 1)
                nc.vector.tensor_tensor(probs[:, m, :, :], S_ps[m][:, :, :],
                                        row_max[:, m, :].unsqueeze(2).to_broadcast([P, HT, P]),
                                        ALU.subtract).then_inc(shifted_ready, 1)

            def tail_norm(b):
                dve.wait_ge(to_done, b + 1)
                o_v = bank7[:, :, :].rearrange("p n (q c) -> p (n q) c", c=VW)
                nc.vector.reciprocal(rec0[:, :, :], o_v[:, :, DH0:DH0 + 1]).then_inc(rec0_ready, 1)
                dve.wait_ge(rec0_ready, b + 1)
                nc.vector.tensor_tensor(o_sb[:].rearrange("p (h d) -> p h d", d=DH0), o_v[:, :, 0:DH0],
                                        rec0[:, :, :].to_broadcast([P, H0, DH0]), ALU.mult).then_inc(o_ready, 1)

            def tail_add(b):
                dve.wait_ge(wo_done, b + 1)
                nc.vector.tensor_tensor(x_sb[:, b, :], x_sb[:, b, :], bank7[:, 0:KT, :].rearrange("p k n -> p (k n)"),
                                        ALU.add).then_inc(x1_ready, 1)
                dve.wait_ge(x1_ready, b + 1)
                token_stats(b, ln2_chain, 3 * b)
                for n, op in enumerate((ALU.max, ALU.min)):
                    nc.vector.tensor_reduce(x1_range[:, n, bass.ds(b, 1)], x_sb[:, b, :], AX.X, op).then_inc(x1_range_step, 1)

            def token_stats(b, chain, n):
                nc.vector.memset(pause[:], 0.0)
                nc.vector.bn_stats(stats[:, 0, :], x_sb[:, b, :]).then_inc(chain, 1)
                dve.wait_ge(chain, n + 1)
                nc.vector.memset(pause[:], 0.0)
                nc.vector.bn_aggr(mv1[:], stats[:, 0, :]).then_inc(chain, 1)
                dve.wait_ge(chain, n + 2)
                nc.vector.tensor_copy(mv[:, b, :], mv1[:]).then_inc(chain, 1)

            def step(b, p, inner=False, late=None):
                softmax_shift(b, 0)
                if inner or b + 2 < B:
                    norm(b + 2, p, inner)
                if inner or b >= 1:
                    tail_norm(b - 1)
                softmax_shift(b, 1)
                if inner or b + 1 < B:
                    qk_copy(b + 1, 1 - p)
                if inner or b >= 1:
                    tail_add(b - 1)
                if late:
                    late()

            counted = [0]

            def link(instruction):
                counted[0] += 1
                instruction.then_inc(b_chain, 1)
                dve.wait_ge(b_chain, counted[0])

            def gate_up_maxima():
                dve.wait_ge(fw_loaded, 112)
                dve.wait_ge(fw_preset, 6)
                nc.vector.tensor_reduce(w_amax[:, 0:2 * IT], wgu, AX.X, ALU.max, apply_absolute_value=True)

            def weight_scales():
                link(nc.vector.tensor_reduce(w_amax[:, 2 * IT:2 * IT + KT], wd, AX.X, ALU.max, apply_absolute_value=True))
                link(nc.vector.tensor_scalar_mul(w_scale[:], w_amax[:], 1.0 / QMAX))
                link(nc.vector.reciprocal(w_inv[:], w_scale[:]))

            def gate_up_scaled():
                for n in range(2 * IT):
                    last = nc.vector.tensor_scalar(wgu[:, n, :], wgu[:, n, :], w_inv[:, n:n + 1], QMAX, ALU.mult, ALU.min)
                link(last)

            def gate_up_shifted():
                link(nc.vector.tensor_scalar(wgu, wgu, -QMAX - 1.0, MAGIC, ALU.max, ALU.add))

            def gate_up_rounded():
                link(nc.vector.tensor_scalar_add(wgu_q, wgu, -MAGIC))
                nc.vector.memset(wgu_q[IR:P, IT - 1, :], 0.0)
                nc.vector.memset(wgu_q[IR:P, 2 * IT - 1, :], 0.0).then_inc(wq_ready, 1)
                dve.wait_ge(ln2_chain, 3 * (B - 2))
                nc.vector.tensor_scalar_add(rstd[:, 0:EARLY], mv[:, 0:EARLY, 1], LN_EPS).then_inc(ln2_eps, 1)

            def down_rounded():
                for k in range(KT):
                    last = nc.vector.tensor_scalar(wd[:, k, :], wd[:, k, :], w_inv[:, 2 * IT + k:2 * IT + k + 1], QMAX, ALU.mult, ALU.min)
                    nc.vector.tensor_scalar(wd_diag[:, k, :], ident[:], w_scale[:, 2 * IT + k:2 * IT + k + 1], None, ALU.mult)
                link(last)
                link(nc.vector.tensor_scalar(wd, wd, -QMAX - 1.0, MAGIC, ALU.max, ALU.add))
                nc.vector.tensor_scalar_add(wd_q, wd, -MAGIC).then_inc(wq_ready, 1)

            def norm_x1(batches):
                for b in batches:
                    nc.vector.tensor_scalar(x1n[:, b, :], x_sb[:, b, :], mv[:, b, 0:1], rstd[:, b:b + 1],
                                            ALU.subtract, ALU.mult).then_inc(x1n_step, 1)

            def early_norms():
                dve.wait_ge(rstd2_ready, 1)
                norm_x1(range(EARLY))

            qk_copy(0, 0)
            step(0, 0)
            rest = (gate_up_maxima, weight_scales, down_rounded, gate_up_scaled, gate_up_shifted, gate_up_rounded, early_norms)
            with dve.Fori(0, (B - 1 - len(rest)) // 2) as i:
                step(2 * i + 1, 1, inner=True)
                step(2 * i + 2, 0, inner=True)
            for b in range(B - len(rest), B):
                step(b, b % 2, late=rest[b - (B - len(rest))])
            tail_norm(B - 1)
            tail_add(B - 1)

            dve.wait_ge(ln2_chain, 3 * B)
            nc.vector.tensor_scalar_add(rstd[:, EARLY:B], mv[:, EARLY:B, 1], LN_EPS).then_inc(ln2_eps, 1)
            dve.wait_ge(clip_exp, 1)
            link(nc.vector.tensor_scalar(clip[:], clip[:], 1.0, QMAX, ALU.add, ALU.mult))
            link(nc.vector.reciprocal(clip[:], clip[:]))

            dve.wait_ge(x1_range_step, 2 * B)
            link(nc.vector.tensor_tensor(x1_range[:], x1_range[:], mv[:, :, 0].unsqueeze(1).to_broadcast([P, 2, B]), ALU.subtract))
            dve.wait_ge(rstd2_ready, 2)
            link(nc.vector.tensor_tensor(x1_range[:], x1_range[:], rstd[:].unsqueeze(1).to_broadcast([P, 2, B]), ALU.mult))

            def activation_scale(n, values, meanwhile=None):
                nc.vector.tensor_reduce(amax_col[:, n:n + 1], values, AX.X, ALU.max, apply_absolute_value=True).then_inc(amax_ready, 1)
                if meanwhile:
                    meanwhile()
                dve.wait_ge(amax_all_ready, n + 1)
                link(nc.vector.tensor_tensor(act_scale[:, n:n + 1], amax_all[:, n:n + 1], clip[:, n:n + 1], ALU.mult))
                link(nc.vector.reciprocal(act_inv[:, n:n + 1], act_scale[:, n:n + 1]))

            activation_scale(0, x1_range[:].rearrange("p n b -> p (n b)"), meanwhile=lambda: norm_x1(range(EARLY, B)))
            nc.vector.tensor_scalar(gu_scale[:], w_scale[:, 0:2 * IT], act_scale[:, 0:1], None, ALU.mult).then_inc(gu_ready, 1)

            def clip_group(g):
                part = x1n[:, g * GB:(g + 1) * GB, :]
                dve.wait_ge(x1n_step, B)
                nc.vector.tensor_scalar(part, part, act_inv[:, 0:1], QMAX, ALU.mult, ALU.min).then_inc(x1_clipped, 1)
                dve.wait_ge(x1_clipped, 2 * g + 1)
                nc.vector.tensor_scalar(part, part, -QMAX - 1.0, MAGIC, ALU.max, ALU.add).then_inc(x1_clipped, 1)

            clip_group(0)
            clip_group(1)

            def hidden(g, first=False):
                for t in range(IT):
                    n = IT * g + t
                    dve.wait_ge(up_done, n + 1)
                    dve.wait_ge(sil_ready, n + 1)
                    part = hT[:, t, bass.ts(g, TB)]
                    nc.vector.scalar_tensor_tensor(out=part, in0=psum[:, 2 * (t % 2) + 1, :],
                                                   scalar=gu_scale[:, IT + t:IT + t + 1], in1=sil[:, t % 2, :],
                                                   op0=ALU.mult, op1=ALU.mult).then_inc(hT_ready, 1)
                    dve.wait_ge(hT_ready, n + 1)
                    nc.vector.tensor_reduce(amax_h[:, bass.ds(n, 1)], part, AX.X, ALU.max,
                                            apply_absolute_value=True).then_inc(amax_h_step, 1)
                    if first and t < G - 2:
                        clip_group(t + 2)

            hidden(0, first=True)
            with dve.Fori(1, G) as g:
                hidden(g)
            dve.wait_ge(amax_h_step, G * IT)
            activation_scale(1, amax_h[:])
            dve.wait_ge(wT_evac, 3)
            link(nc.vector.tensor_scalar(down_scale[:], down_scale[:], act_scale[:, 1:2], None, ALU.mult))

            def clip_above(n):
                part = hT[:, :, bass.ts(n, TB // 2)]
                nc.vector.tensor_scalar(part, part, act_inv[:, 1:2], QMAX, ALU.mult, ALU.min).then_inc(h_clipped, 1)

            def clip_below(n):
                part = hT[:, :, bass.ts(n, TB // 2)]
                dve.wait_ge(h_clipped, 2 * n + 1)
                nc.vector.tensor_scalar(part, part, -QMAX - 1.0, MAGIC, ALU.max, ALU.add).then_inc(h_clipped, 1)

            def add_down(g, rounding=True):
                for q in range(2):
                    n = 2 * g + q
                    if rounding:
                        clip_above(n + 2)
                    dve.wait_ge(down_done, n + 1)
                    nc.vector.tensor_tensor(down_out[:], bank(4 + q, 2, D), down_scale[:].unsqueeze(1).to_broadcast([P, 2, D]),
                                            ALU.mult).then_inc(down_read, 1)
                    if rounding:
                        clip_below(n + 2)
                    dve.wait_ge(down_read, n + 1)
                    x_two = x_sb[:, bass.ds(2 * n, 2), :]
                    nc.vector.tensor_tensor(x_two, x_two, down_out[:], ALU.add).then_inc(x2_ready, 1)
                    dve.wait_ge(x2_ready, n + 1)
                    nc.vector.memset(pause[:], 0.0)
                    for j in range(2):
                        last = nc.vector.bn_stats(stats[:, j, :], x_sb[:, 2 * n + j, :])
                    last.then_inc(ln3_chain, 1)
                    dve.wait_ge(ln3_chain, 3 * n + 1)
                    nc.vector.memset(pause[:], 0.0)
                    for j in range(2):
                        last = nc.vector.bn_aggr(mv2[:, j, :], stats[:, j, :])
                    last.then_inc(ln3_chain, 1)
                    dve.wait_ge(ln3_chain, 3 * n + 2)
                    nc.vector.tensor_copy(mv[:, bass.ds(2 * n, 2), :], mv2[:]).then_inc(ln3_chain, 1)

            for n in range(2):
                clip_above(n)
                clip_below(n)
            with dve.Fori(0, G - 1) as g:
                add_down(g)
            dve.wait_ge(ln3_chain, 6 * (G - 1))
            nc.vector.tensor_scalar_add(rstd[:, 0:EARLY], mv[:, 0:EARLY, 1], LN_EPS).then_inc(ln3_eps, 1)
            add_down(G - 1, rounding=False)

            dve.wait_ge(ln3_chain, 6 * G)
            nc.vector.tensor_scalar_add(rstd[:, EARLY:B], mv[:, EARLY:B, 1], LN_EPS).then_inc(ln3_eps, 1)
            dve.wait_ge(gk_loaded, 16 * (4 + 2 * B))
            nc.vector.tensor_tensor(gk_ctx[:], gk[:, KT:2 * KT, :], gk[:, 2 * KT:3 * KT, :], ALU.add).then_inc(gk_ready, 1)
            nc.vector.tensor_scalar_add(rms1[:], rms1[:], 1.0)
            dve.wait_ge(rstd3_ready, 2)

            def norm_c(b, p):
                nc.vector.tensor_scalar(xn_c[:, p, :], x_sb[:, b, :], mv[:, b, 0:1], rstd[:, bass.ds(b, 1)],
                                        ALU.subtract, ALU.mult).then_inc(xn_c_ready, 1)

            def read_gates_and_scores(b, p):
                dve.wait_ge(gates_done, b + 1)
                nc.vector.tensor_copy(gates_all[0:2 * H1, bass.ts(b, P)], psum[0:2 * H1, 2 + p, 0:P]).then_inc(gates_read, 1)
                dve.wait_ge(st_done, b + 1)
                nc.vector.tensor_scalar_mul(ST[:, bass.ds(H1 * b, H1), :], bank(4 + p, H1, P), float(DH1) ** -0.5).then_inc(st_read, 1)

            norm_c(0, 0)
            norm_c(1, 1)
            with dve.Fori(0, B // 2 - 1) as i:
                for p in range(2):
                    dve.wait_ge(ct_done, 2 * i + p + 1)
                    norm_c(2 * i + (p + 2), p)
                    read_gates_and_scores(2 * i + p, p)
            read_gates_and_scores(B - 2, 0)
            read_gates_and_scores(B - 1, 1)

            R = B * H1
            counted = [0]

            def link_c(instruction):
                counted[0] += 1
                instruction.then_inc(c_chain, 1)
                dve.wait_ge(c_chain, counted[0])

            dve.wait_ge(gates_loaded, 16)
            for n in range(2):
                last = nc.vector.tensor_scalar(gates8[0:R, n, :], gates8[0:R, n, :], gbias[0:R, n:n + 1], None, ALU.add)
            link_c(last)
            link_c(nc.vector.tensor_scalar_mul(lf[0:R, :], gates8[0:R, 1, :], -1.0))
            nc.vector.tensor_tensor(lf[0:R, :], lf[0:R, :], gates8[0:R, 1, :], ALU.max).then_inc(soft_abs, 1)
            dve.wait_ge(soft_log, 2)
            link_c(nc.vector.scalar_tensor_tensor(out=lf[0:R, :], in0=gates8[0:R, 1, :], scalar=0.0, in1=lf[0:R, :],
                                                  op0=ALU.min, op1=ALU.subtract))
            link_c(nc.vector.tensor_tensor_scan(gsum[0:R, :], ones_sb[0:R, :], lf[0:R, :], 0.0, ALU.mult, ALU.add))
            nc.vector.tensor_tensor(gtmp[0:R, 0, :], gates8[0:R, 0, :], gsum[0:R, :], ALU.subtract).then_inc(a_ready, 1)
            dve.wait_ge(a_ready, 1)
            link_c(nc.vector.tensor_tensor_scan(gmax[0:R, :], ones_sb[0:R, :], gtmp[0:R, 0, :], NEG, ALU.mult, ALU.max))
            nc.vector.tensor_scalar_mul(ga[0:R, :], gmax[0:R, :], -1.0).then_inc(neg_max_ready, 1)
            nc.vector.tensor_tensor(gsum[0:R, :], gsum[0:R, :], gmax[0:R, :], ALU.add).then_inc(floor_ready, 1)

            def decay_scores(b, p, inner=False):
                dve.wait_ge(decay_ready, b + 1)
                if inner or b >= 2:
                    dve.wait_ge(pvc_done, b - 1)
                nc.vector.tensor_tensor(decayed[:, p, :, :], ST[:, bass.ds(H1 * b, H1), :], decay[:, p, :, :],
                                        ALU.mult).then_inc(decayed_ready, 1)

            def normalise(b, p):
                o_v = psum[:, p, 0:H1 * (DH1 + 1)].rearrange("p (h d) -> p h d", d=DH1 + 1)
                dve.wait_ge(pvc_done, b + 1)
                nc.vector.scalar_tensor_tensor(out=o_rec, in0=o_v[:, :, DH1], scalar=1e-6, in1=floorT[:, bass.ds(H1 * b, H1)],
                                               op0=ALU.add, op1=ALU.max).then_inc(o_rec_ready, 1)
                dve.wait_ge(o_rec_ready, 2 * b + 1)
                nc.vector.reciprocal(o_rec, o_rec).then_inc(o_rec_ready, 1)
                dve.wait_ge(o_rec_ready, 2 * b + 2)
                nc.vector.tensor_tensor(h_c[:, p, :, :], o_v[:, :, 0:DH1], o_rec.unsqueeze(2).to_broadcast([P, H1, DH1]),
                                        ALU.mult).then_inc(h_c_ready, 1)
            def mean_square(b, p):
                dve.wait_ge(h_sq_ready, b + 1)
                nc.vector.tensor_reduce(ms[:, p, :], h_sq, AX.X, ALU.add).then_inc(ms_ready, 1)

            def add_attention(b, p):
                h_v = h_c[:, p, :, :]
                dve.wait_ge(rs_ready, b + 1)
                nc.vector.tensor_tensor(h_v, h_v, ms_rs[:, p, :].unsqueeze(2).to_broadcast([P, H1, DH1]), ALU.mult).then_inc(scaled_ready, 1)
                dve.wait_ge(scaled_ready, 2 * b + 1)
                nc.vector.tensor_tensor(h_v, h_v, rms1[:].unsqueeze(1).to_broadcast([P, H1, DH1]), ALU.mult).then_inc(scaled_ready, 1)
                dve.wait_ge(scaled_ready, 2 * b + 2)
                x_b = x_sb[:, bass.ds(b, 1), :].rearrange("p o d -> p (o d)")
                nc.vector.tensor_tensor(x_b, x_b, h_v.rearrange("p h d -> p (h d)"), ALU.add).then_inc(x3_ready, 1)
                dve.wait_ge(x3_ready, b + 1)
                token_stats(b, ln4_chain, 4 * b)
                nc.vector.tensor_scalar_add(rstd[:, bass.ds(b, 1)], mv1[:, 1:2], LN_EPS).then_inc(ln4_chain, 1)

            def router_norm(b, p, inner=False):
                dve.wait_ge(rstd4_ready, b + 1)
                if inner or b >= 2:
                    dve.wait_ge(dt_evac, b - 1)
                nc.vector.tensor_scalar(xn_r[:, p, :], x_sb[:, b, :], mv[:, b, 0:1], rstd[:, bass.ds(b, 1)],
                                        ALU.subtract, ALU.mult).then_inc(xn_r_ready, 1)

            def step_c(b, p, inner=False):
                if inner or b + 1 < B:
                    normalise(b + 1, 1 - p)
                if inner or b + 2 < B:
                    decay_scores(b + 2, p, inner)
                if inner or b < B:
                    add_attention(b, p)
                if inner or b + 1 < B:
                    mean_square(b + 1, 1 - p)
                if inner or 0 <= b - 1 < B:
                    router_norm(b - 1, 1 - p, inner)

            decay_scores(0, 0)
            decay_scores(1, 1)
            normalise(0, 0)
            mean_square(0, 0)
            for b in range(PEEL):
                step_c(b, b % 2)
            with dve.Fori(PEEL // 2, B // 2 - 1) as i:
                for p in range(2):
                    step_c(2 * i + p, p, inner=True)
            for b in range(B - 2, B + 1):
                step_c(b, b % 2)

            counted_d = [0]

            def link_d(instruction):
                counted_d[0] += 1
                instruction.then_inc(d_chain, 1)
                dve.wait_ge(d_chain, counted_d[0])

            tt = nc.vector.tensor_tensor
            over_e = lambda v: v.unsqueeze(2).to_broadcast([P, B, E])
            over_b = lambda v: v.unsqueeze(1).to_broadcast([P, B, E])
            dve.wait_ge(route_consts, 12)
            nc.vector.tensor_copy(iota_e, int_tmp[:, 0:E])
            at = E + NT
            nc.vector.tensor_copy(iota_row[:], int_tmp[:, at:at + P])
            nc.vector.tensor_copy(batch_no[:], int_tmp[:, at + P:at + P + B])
            nc.vector.tensor_copy(token_p[:], int_tmp[:, at + P + B:at + P + B + 1])
            nc.vector.tensor_copy(empty_p[:], int_tmp[:, at + P + B + 1:at + P + B + 2])
            link_d(nc.vector.tensor_copy(iota_t, int_tmp[:, E:E + NT]))
            dve.wait_ge(logits_copied, B)
            left = logits
            for n, (value, one_hot) in enumerate(((v1, oh1), (v2, oh2))):
                link_d(nc.vector.tensor_reduce(value, left, AX.X, ALU.max))
                link_d(tt(rt, left, over_e(value), ALU.is_ge))
                link_d(tt(rt, rt, over_b(iota_e), ALU.mult))
                link_d(nc.vector.tensor_reduce(m12[:, n, :], rt, AX.X, ALU.max))
                link_d(tt(one_hot, over_b(iota_e), over_e(m12[:, n, :]), ALU.is_equal))
                if n == 0:
                    link_d(nc.vector.scalar_tensor_tensor(out=top, in0=one_hot, scalar=NEG, in1=left, op0=ALU.mult, op1=ALU.add))
                    left = top
            nc.vector.tensor_tensor(chosen_b[:], oh1, oh2, ALU.add).then_inc(chosen_ready, 1)
            nc.vector.tensor_tensor(v2, v2, v1, ALU.subtract).then_inc(gap_ready, 1)
            dve.wait_ge(e2_ready, 1)
            link_d(nc.vector.tensor_scalar_add(w12[:, 0, :], e2, 1.0))
            link_d(nc.vector.reciprocal(w12[:, 0, :], w12[:, 0, :]))
            link_d(tt(w12[:, 1, :], e2, w12[:, 0, :], ALU.mult))
            col = lambda c: xrow[:, :, D + c]
            nc.vector.tensor_copy(col(1), m12[:, 0, :])
            tt(col(2), w12[:, 0, :], w12[:, 1, :], ALU.subtract)
            nc.vector.tensor_copy(col(3), w12[:, 1, :]).then_inc(xrow_routed, 1)
            dve.wait_ge(ranks_done, 1)
            counts = psum[:, 4, 0:B * E].rearrange("p (b e) -> p b e", e=E)
            by_expert = lambda v: v.rearrange("p b e -> p (b e)").rearrange("p (e b) -> p e b", b=B)
            by_batch = lambda v: by_expert(v).rearrange("p e b -> p b e")
            link_d(nc.vector.tensor_copy(by_batch(rt), counts))
            link_d(nc.vector.tensor_tensor_scan(incl.rearrange("p b e -> p (b e)"), scan_keep[:].rearrange("p e b -> p (e b)"),
                                                rt.rearrange("p b e -> p (b e)"), 0.0, ALU.mult, ALU.add))
            link_d(nc.vector.tensor_scalar(etiles, by_expert(incl)[:, :, B - 1], P - 1.0, 1.0 / P, ALU.add, ALU.mult))
            link_d(nc.vector.tensor_scalar(etiles, etiles, -(0.5 - 0.25 / P), MAGIC, ALU.add, ALU.add))
            link_d(nc.vector.tensor_scalar_add(etiles, etiles, -MAGIC))
            link_d(nc.vector.tensor_tensor_scan(eend, ones_sb[:, 0:E], etiles, 0.0, ALU.mult, ALU.add))
            link_d(tt(tcmp, eend.unsqueeze(1).to_broadcast([P, NT, E]), iota_t.unsqueeze(2).to_broadcast([P, NT, E]), ALU.is_le))
            link_d(nc.vector.tensor_reduce(te, tcmp, AX.X, ALU.add))
            link_d(nc.vector.tensor_scalar_min(te, te, E - 1.0))
            nc.vector.memset(tchg[:, 0:1], 1.0)
            link_d(tt(tchg[:, 1:NT], te[:, 1:NT], te[:, 0:NT - 1], ALU.not_equal))
            link_d(nc.vector.tensor_tensor_scan(tcum, ones_sb[:, 0:NT], tchg, -1.0, ALU.mult, ALU.add))
            link_d(nc.vector.tensor_scalar(tslot, tcum, 1.0 / SLOTS, -1.0 / SLOTS, ALU.mult, ALU.add))
            link_d(nc.vector.tensor_scalar_add(tslot, tslot, MAGIC))
            link_d(nc.vector.tensor_scalar(tslot, tslot, -MAGIC, -float(SLOTS), ALU.add, ALU.mult))
            link_d(tt(tslot, tslot, tcum, ALU.add))
            link_d(nc.vector.tensor_scalar_mul(tslot, tslot, float(SLOT)))
            nc.vector.tensor_copy(tile_info[:, 0, :], te)
            nc.vector.tensor_copy(tile_info[:, 1, :], tslot)
            link_d(nc.vector.tensor_copy(tile_info[:, 2, :], tchg))
            nc.vector.tensor_scalar(te, te, -1.0, float(E), ALU.mult, ALU.add).then_inc(info_ready, 1)
            link_d(tt(eoff, eend, etiles, ALU.subtract))
            link_d(nc.vector.tensor_scalar_mul(eoff, eoff, float(P)))
            link_d(tt(rbase, by_batch(incl), by_batch(rt), ALU.subtract))
            link_d(tt(rbase, rbase, psum[:, 3, 0:B * E].rearrange("p (b e) -> p b e", e=E), ALU.add))
            link_d(tt(rbase, rbase, over_b(eoff), ALU.add))
            for n, one_hot in enumerate((oh1, oh2)):
                link_d(tt(rt2, one_hot, rbase, ALU.mult))
                link_d(nc.vector.tensor_reduce(slots_f[:, n, :], rt2, AX.X, ALU.add))
            link_d(nc.vector.tensor_scalar(place_tile[:], slots_f, 0.5 - P / 2.0, 1.0 / P, ALU.add, ALU.mult))
            link_d(nc.vector.tensor_scalar_add(place_tile[:], place_tile[:], MAGIC))
            link_d(nc.vector.tensor_scalar_add(place_tile[:], place_tile[:], -MAGIC))
            link_d(nc.vector.scalar_tensor_tensor(out=place_row[:], in0=place_tile[:], scalar=-float(P), in1=slots_f,
                                                  op0=ALU.mult, op1=ALU.add))
            N2 = TOP * B
            flat = lambda v: v.rearrange("p n b -> p (n b)").unsqueeze(2)
            link_d(tt(tile_hot, iota_t.unsqueeze(1).to_broadcast([P, N2, NT]), flat(place_tile[:]).to_broadcast([P, N2, NT]), ALU.is_equal))
            nc.vector.tensor_scalar(tile_num[:, :, 0, :], tile_hot, token_p[:, 0:1], None, ALU.mult)
            for n in range(TOP):
                tt(tile_num[:, n * B:(n + 1) * B, 1, :], tile_hot[:, n * B:(n + 1) * B, :],
                   batch_no[:].unsqueeze(2).to_broadcast([P, B, NT]), ALU.mult)
            for n in range(HOT):
                part = slice(n * N2 // HOT, (n + 1) * N2 // HOT)
                tt(row_hot[:, part, :], iota_row[:].unsqueeze(1).to_broadcast([P, N2 // HOT, P]),
                   flat(place_row[:])[:, part, :].to_broadcast([P, N2 // HOT, P]), ALU.is_equal).then_inc(hot_ready, 1)
            def weights_low(n, t, p, inner=False):
                place = dve.value_load(tile_info[0:1, 1, bass.ds(t, 1)], min_val=0, max_val=(SLOTS - 1) * SLOT)
                new = dve.value_load(tile_info[0:1, 2, bass.ds(t, 1)], min_val=0, max_val=1)
                if inner or t >= 1:
                    dve.wait_ge(part_low[n], t)
                dve.wait_ge(part_high[n], t + 1)
                nc.vector.memset(pause_d[:, 3 + n:4 + n], 0.0)
                with dve.If(new > 0):
                    tt(expert_w[:, bass.ds(place + (3 + n) * PART, PART)], stage[:, p, n, :],
                       expert_w[:, bass.ds(place + n * PART, PART)], ALU.subtract)
                nc.vector.memset(pause_d[:, n:n + 1], 0.0).then_inc(part_low[n], 1)

            weights_low(0, 0, 0)
            dve.wait_ge(places_done, 1)
            part_p, part_b = psum[:, 5, 0:NT], psum[:, 5, NT:2 * NT]
            nc.vector.tensor_scalar(row_empty[:], part_b, 0.0, empty_p[:, 0:1], ALU.is_equal, ALU.mult)
            link_d(nc.vector.tensor_scalar(row_token_f[:], part_b, float(P), -float(P), ALU.mult, ALU.add))
            link_d(tt(row_token_f[:], row_token_f[:], part_p, ALU.add))
            link_d(tt(row_token_f[:], row_token_f[:], row_empty[:], ALU.add))
            link_d(nc.vector.tensor_copy(row_token[:], row_token_f[:]))
            nc.vector.tensor_copy(next_token[:], row_token[:, 0:2]).then_inc(tokens_placed, 1)

            def hidden_d(t, p, f):
                dve.wait_ge(gu_done, 2 * t + f + 1)
                dve.wait_ge(sil_d_ready, 2 * t + f + 1)
                tt(h_d[:, p, f * FH:(f + 1) * FH], psum[:, 2 * f + 1, :], sil_d[:, f, :], ALU.mult).then_inc(h_d_ready, 1)

            def route_of(t, p, loads, inner=False):
                dve.wait_ge(xg_loaded[p], 16 * loads)
                if inner or t >= 2:
                    dve.wait_ge(sum_added, 16 * (t - 1))
                nc.vector.tensor_scalar(w_col[:, p:p + 1], xg[:, p, D + 1:D + 2], te[:, bass.ds(t, 1)],
                                        xg[:, p, D + 2:D + 3], ALU.is_equal, ALU.mult).then_inc(w_part, 1)
                dve.wait_ge(w_part, t + 1)
                tt(w_col[:, p:p + 1], w_col[:, p:p + 1], xg[:, p, D + 3:D + 4], ALU.add)
                dve.wait_ge(tx_done, t + 1)
                last = nc.vector.tensor_copy(tok_idx[:, p:p + 1], xg[:, p, D:D + 1].bitcast(U32))
                if inner or t + 2 < NT:
                    last = nc.vector.tensor_copy(next_token[:, p:p + 1], row_token[:, bass.ds(t + 2, 1)])
                last.then_inc(meta_ready, 1)

            def weighted(t, p):
                dve.wait_ge(dn_done, t + 1)
                dve.wait_ge(meta_ready, t + 1)
                nc.vector.tensor_scalar(y_d[:, p, :], psum[:, 7, 0:D], w_col[:, p:p + 1], None, ALU.mult).then_inc(y_ready, 1)

            def x_low(t, p):
                dve.wait_ge(xT_high, t + 1)
                tt(xT_lo[:, p, :, :], bank(6, 4, P)[:, 0:KT, :], xT_hi[:, p, :, :], ALU.subtract).then_inc(xT_low, 1)

            def h_low(t):
                dve.wait_ge(hT_high, t + 1)
                tt(hT_lo, bank(4, F1 // P, P, count=2), hT_hi, ALU.subtract).then_inc(hT_low, 1)

            def tile_step(t, p, loads, inner=False):
                hidden_d(t, p, 0)
                if inner or t >= 1:
                    h_low(t - 1)
                if not inner and t == 0:
                    x_low(1, 1)
                hidden_d(t, p, 1)
                if inner or 0 < t < NT - 1:
                    x_low(t + 1, 1 - p)
                if inner or t + 2 < NT:
                    weights_low(1, t + 2, p, inner)
                route_of(t, p, loads, inner)
                if inner or t >= 1:
                    weighted(t - 1, 1 - p)
                if inner or t + 1 < NT:
                    weights_low(2, t + 1, 1 - p, inner)

            weights_low(1, 0, 0)
            x_low(0, 0)
            weights_low(2, 0, 0)
            weights_low(0, 1, 1)
            weights_low(1, 1, 1)
            tile_step(0, 0, 1)
            tile_step(1, 1, 1)
            tile_step(2, 0, 2)
            with dve.Fori(1, (NT - 3) // 2) as i:
                tile_step(2 * i + 1, 1, i + 1, inner=True)
                tile_step(2 * i + 2, 0, i + 2, inner=True)
            tile_step(NT - 2, 1, NT // 2)
            tile_step(NT - 1, 0, NT // 2 + 1)
            h_low(NT - 1)
            weighted(NT - 1, 0)


def kernel(**inputs):
    import numpy as np
    import concourse.bacc as bacc
    from concourse.bass_utils import run_bass_kernel_spmd

    nc = bacc.Bacc("TRN2", target_bir_lowering=False, num_devices=1)
    arrays, args = {}, []
    for name in INPUTS:
        a = np.ascontiguousarray(inputs[name])
        arrays[f"in_{name}"] = a
        args.append(nc.dram_tensor(f"in_{name}", a.shape, mybir.dt.from_np(a.dtype), kind="ExternalInput").ap())
    out = nc.dram_tensor("out_x", inputs["x"].shape, mybir.dt.float32, kind="ExternalOutput").ap()
    build(nc, *args, out)
    return run_bass_kernel_spmd(nc, [arrays], core_ids=[0]).results[0]["out_x"]
```
